# Optimizing a Trainium2 kernel written in Bass

```python
import numpy as np
import jax
import jax.numpy as jnp

def _softmax(x, axis=-1):
    return jax.nn.softmax(x, axis=axis)

def _gelu(x):
    return jax.nn.gelu(x, approximate=True)

def _silu(x):
    return jax.nn.silu(x)

def _sigmoid(x):
    return jax.nn.sigmoid(x)

def _layernorm(x, axis=-1, eps=1e-05):
    m = jnp.mean(x, axis=axis, keepdims=True)
    v = jnp.var(x, axis=axis, keepdims=True)
    return (x - m) / jnp.sqrt(v + eps)

def _scatter_add(tgt, idx, src, axis=0):
    return tgt.at[idx].add(src)

def _segment_sum(src, seg, n):
    return jax.ops.segment_sum(src, seg, n)
kernel_name = 'mk_prb_d1_jaxref_r4_37ef63'

def setup_inputs(seed: int=0):
    np.random.seed(seed)
    _w = jnp.asarray

    def _L0_attn_setup():
        import jax, jax.numpy as jnp
        import numpy as np
        B, S, E, H = (4, 1024, 256, 16)
        D = E // H

        def _xavier(key, out_f, in_f):
            lim = float(np.sqrt(6.0 / (in_f + out_f)))
            return jax.random.uniform(key, (out_f, in_f), jnp.float32, -lim, lim)

        def _feature_map(t):
            return jax.nn.elu(t) + 1.0
        key = jax.random.key(seed)
        ks = jax.random.split(key, 9)
        x = jax.random.normal(ks[0], (B, S, E), jnp.float32)
        Wq = _xavier(ks[1], E, E)
        Wk = _xavier(ks[2], E, E)
        Wv = _xavier(ks[3], E, E)
        Wo = _xavier(ks[4], E, E)
        bq = jnp.zeros((E,), jnp.float32)
        bk = jnp.zeros((E,), jnp.float32)
        bv = jnp.zeros((E,), jnp.float32)
        bo = jnp.zeros((E,), jnp.float32)
        return {'x': x, 'Wq': Wq, 'bq': bq, 'Wk': Wk, 'bk': bk, 'Wv': Wv, 'bv': bv, 'Wo': Wo, 'bo': bo}
    _L0_attn_in = _L0_attn_setup()

    def _L0_ffn_setup():
        import jax, jax.numpy as jnp
        import numpy as np
        N, T, D = (4, 1024, 256)
        NUM_EXPERTS = 8
        EXPERT_CAP = 2.0
        MLP_RATIO = 4
        HIDDEN = MLP_RATIO * D
        key = jax.random.key(seed)
        k1, k2, k3, k4 = jax.random.split(key, 4)
        x = jax.random.normal(k1, (N, T, D), dtype=jnp.float32)
        gate_w = jax.random.truncated_normal(k2, -2.0, 2.0, (D, NUM_EXPERTS), dtype=jnp.float32) * 0.02
        w1 = jax.random.normal(k3, (NUM_EXPERTS, D, HIDDEN), dtype=jnp.float32) * 0.02
        w2 = jax.random.normal(k4, (NUM_EXPERTS, HIDDEN, D), dtype=jnp.float32) * 0.02
        return {'x': x, 'gate_w': gate_w, 'w1': w1, 'w2': w2}
    _L0_ffn_in = _L0_ffn_setup()
    _d = {'L0_attn_x': _L0_attn_in['x'], 'L0_attn_Wq': _L0_attn_in['Wq'], 'L0_attn_bq': _L0_attn_in['bq'], 'L0_attn_Wk': _L0_attn_in['Wk'], 'L0_attn_bk': _L0_attn_in['bk'], 'L0_attn_Wv': _L0_attn_in['Wv'], 'L0_attn_bv': _L0_attn_in['bv'], 'L0_attn_Wo': _L0_attn_in['Wo'], 'L0_attn_bo': _L0_attn_in['bo'], 'L0_ffn_gate_w': _L0_ffn_in['gate_w'], 'L0_ffn_w1': _L0_ffn_in['w1'], 'L0_ffn_w2': _L0_ffn_in['w2']}
    _x0 = _d['L0_attn_x']
    _d['L0_attn_x'] = jax.random.normal(jax.random.fold_in(jax.random.key(seed), 1), (16, 1024, 256), dtype=_x0.dtype)
    del _x0
    return _d

def reference(L0_attn_x, L0_attn_Wq, L0_attn_bq, L0_attn_Wk, L0_attn_bk, L0_attn_Wv, L0_attn_bv, L0_attn_Wo, L0_attn_bo, L0_ffn_gate_w, L0_ffn_w1, L0_ffn_w2):

    def _L0_attn_ref(x, Wq, bq, Wk, bk, Wv, bv, Wo, bo):
        import jax, jax.numpy as jnp
        import numpy as np
        B, S, E, H = (4, 1024, 256, 16)
        D = E // H

        def _xavier(key, out_f, in_f):
            lim = float(np.sqrt(6.0 / (in_f + out_f)))
            return jax.random.uniform(key, (out_f, in_f), jnp.float32, -lim, lim)

        def _feature_map(t):
            return jax.nn.elu(t) + 1.0
        b, s, _ = x.shape
        Q = (x @ Wq.T + bq).reshape(b, s, H, D)
        K = (x @ Wk.T + bk).reshape(b, s, H, D)
        V = (x @ Wv.T + bv).reshape(b, s, H, D)
        Q = _feature_map(Q)
        K = _feature_map(K)
        KV = jnp.einsum('bshd,bshe->bhde', K, V)
        K_sum = K.sum(axis=1)
        Z = 1.0 / (jnp.einsum('bshd,bhd->bsh', Q, K_sum) + 1e-06)
        out = jnp.einsum('bshd,bhde,bsh->bshe', Q, KV, Z)
        out = out.reshape(b, s, E)
        out = out @ Wo.T + bo
        return out

    def _L0_ffn_ref(x, gate_w, w1, w2):
        import jax, jax.numpy as jnp
        import numpy as np
        N, T, D = (4, 1024, 256)
        NUM_EXPERTS = 8
        EXPERT_CAP = 2.0
        MLP_RATIO = 4
        HIDDEN = MLP_RATIO * D
        x = x.astype(jnp.float32)
        n, t, d = x.shape
        k = int(EXPERT_CAP * t / NUM_EXPERTS)
        scores = jnp.einsum('ntd,de->nte', x, gate_w)
        probs = jax.nn.softmax(scores, axis=-1)
        probs = jnp.transpose(probs, (0, 2, 1))
        g, m = jax.lax.top_k(probs, k)
        xin = jax.vmap(lambda xb, mb: xb[mb])(x, m)
        h = jax.nn.gelu(jnp.einsum('nekd,edf->nekf', xin, w1))
        h = jnp.einsum('nekf,efd->nekd', h, w2)
        weighted = g[..., None] * h
        flat_idx = (m + jnp.arange(n, dtype=m.dtype)[:, None, None] * t).reshape(-1)
        out = jnp.zeros((n * t, d), dtype=jnp.float32).at[flat_idx].add(weighted.reshape(-1, d))
        out = out.reshape(n, t, d)
        return out.astype(jnp.bfloat16)
    x = L0_attn_x
    xn = _layernorm(x, axis=-1)
    x = x + _L0_attn_ref(xn, L0_attn_Wq, L0_attn_bq, L0_attn_Wk, L0_attn_bk, L0_attn_Wv, L0_attn_bv, L0_attn_Wo, L0_attn_bo) + _L0_ffn_ref(xn, L0_ffn_gate_w, L0_ffn_w1, L0_ffn_w2)
    return x

_drawn_inputs = setup_inputs


def setup_inputs(seed=0):
    import zlib

    import numpy as np

    out = dict(_drawn_inputs(seed))
    spreads = {'L0_attn_bq': (0.0, 0.8),
     'L0_attn_bk': (0.0, 0.8),
     'L0_attn_bv': (0.0, 0.1),
     'L0_attn_bo': (0.0, 0.1)}
    factors = {'L0_attn_Wq': 7.54, 'L0_attn_Wk': 4.179}
    for name, (base, spread) in spreads.items():
        noise = np.random.default_rng([zlib.crc32(name.encode()), seed]).standard_normal(out[name].shape)
        drawn = base * np.exp(spread * noise) if base else spread * noise
        out[name] = jnp.asarray(drawn.astype(out[name].dtype))
    for name, factor in factors.items():
        out[name] = (out[name] * factor).astype(out[name].dtype)
    return out
```

```python
from contextlib import ExitStack

import concourse.bass as bass
from concourse import mybir

ALU = mybir.AluOpType
ACT = mybir.ActivationFunctionType
F32 = mybir.dt.float32
F16 = mybir.dt.float16
BF16 = mybir.dt.bfloat16
U32 = mybir.dt.uint32
I32 = mybir.dt.int32
AX = mybir.AxisListType
ds = bass.ds

P = 128
S = 1024
D = 256
E = 8
HID = 1024
CAP = 2 * S // E
HD = 16
NT = S // P
DC = D // P
HC = HID // P
HALF = NT // 2
XSCALE = 2.0 ** 11
EXP_MASK = 0x7F800000
TOP = 8


class Counts:

    def __init__(self):
        self.of = {}

    def add(self, sem, per, step, credit):
        self.of[sem.name] = (per, step, credit)
        return sem

    def at(self, sem, n, k=0):
        per, step, credit = self.of[sem.name]
        return n * (per * step) + (k + 1 + credit) * step

    def credit(self, sem):
        per, step, credit = self.of[sem.name]
        return credit * step


def held(eng, value):
    return value if isinstance(value, int) else eng.to_reg(value)


def block_program(nc, x, Wq, bq, Wk, bk, Wv, bv, Wo, bo, gate_w, w1, w2, out, table, mix, acc):
    NB = x.shape[0]
    NE = NB * E
    LAG = min(3, NB - 3)
    XR = LAG + 3
    QR = LAG + 1
    GB = 4
    NG = NB // GB
    NBODY = 4 * NG
    PIECES = 32 // NB
    ROUNDS = CAP // TOP
    RPL = ROUNDS // LAG

    x_rows = x.rearrange("n (j p) d -> n p j d", p=P)
    mix_rows = mix.rearrange("(n j p) d -> n p j d", p=P, j=NT)
    acc_rows = acc.rearrange("(n j p) d -> n p j d", p=P, j=NT)
    table_rows = table.rearrange("(n j p) d -> n p j d", p=P, j=NT)
    w1_rows = w1.rearrange("e d f -> (e d) f")
    w2_rows = w2.rearrange("e f d -> (e f) d")

    with ExitStack() as whole:
        def sem(name):
            return whole.enter_context(nc.semaphore(name))

        counts = Counts()
        at, credit = counts.at, counts.credit

        def event(name, per=1, step=1, credit=0):
            return counts.add(sem(name), per, step, credit)

        def sb_in(ctx):
            return lambda name, shape, dt: ctx.enter_context(nc.sbuf_tensor(name, shape, dt))

        def ps_in(ctx):
            return lambda name, shape, dt=F32: ctx.enter_context(nc.psum_tensor(name, shape, dt))

        sb = sb_in(whole)
        ident16 = sb("ident16", [P, P], F16)
        ident = sb("ident", [P, P], F32)
        picks = sb("picks", [P, NG * E * 2 * 4], U32)
        gains = sb("gains", [P, NG * E * 2 * 4], F32)
        scales = sb("scales", [P, E, 5], F32)

        with ExitStack() as ctx:
            sb, ps = sb_in(ctx), ps_in(ctx)
            xring = sb("xring", [P, XR, NT, D], F32)
            qring = sb("qring", [P, QR, DC, S], F32)
            kvring = sb("kvring", [P, QR, DC, P + 1], F32)
            xhl = [sb(f"xhl{h}", [P, HALF, 2, DC, P], F16) for h in range(2)]
            xT = [sb(f"xT{h}", [P, 2, DC, HALF * P], F16) for h in range(2)]
            stats = sb("stats", [P, NT, 6], F32)
            moments = sb("moments", [P, NT, 2], F32)
            veps = sb("veps", [P, NT], F32)
            rpow = sb("rpow", [P, NT], F32)
            rstd = sb("rstd", [P, NT], F32)
            minus_half = sb("minus_half", [P, NT], F32)
            xm = sb("xm", [P, 2, D], F32)
            wraw = sb("wraw", [P, 4, DC, D], F32)
            graw = sb("graw", [P, DC, E], F32)
            bias_raw = sb("bias_raw", [P, 2 * D], F32)
            bias_tmp = sb("bias_tmp", [P, 2 * D], F32)
            bias_rows = sb("bias_rows", [P, 2 * D], F16)
            bias_hi = sb("bias_hi", [P, 2 * D], F16)
            bias_lhs = sb("bias_lhs", [P, P], F16)
            row01 = sb("row01", [P, 1], F32)
            wq = sb("wq", [P, 2, DC, D], F16)
            wkv = sb("wkv", [P, 2, DC, 2 * D], F16)
            wg = sb("wg", [P, 2, DC, E], F16)
            woT = sb("woT", [P, DC, D], F32)
            bqT = sb("bqT", [P, DC], F32)
            bo_row = sb("bo_row", [1, D], F32)
            bo_all = sb("bo_all", [P, D], F32)
            wmax = sb("wmax", [P, 5], F32)
            wmax_all = sb("wmax_all", [P, 5], F32)
            wpow = sb("wpow", [P, 3], F32)
            wsc = sb("wsc", [P, 3], F32)
            wrec = sb("wrec", [P, 3], F32)
            winv = sb("winv", [P, 3], F32)
            head_mask = sb("head_mask", [P, P], F32)
            ek = sb("ek", [P, 2, D], F32)
            kraw = sb("kraw", [P, 2, D], F32)
            phik = sb("phik", [P, 2, D], F32)
            vone = sb("vone", [P, 2, DC, P + 1], F32)
            eq = sb("eq", [P, HALF * P], F32)
            qraw = sb("qraw", [P, HALF * P], F32)
            gsub = sb("gsub", [P, 2, HALF, E], F32)
            gexp = sb("gexp", [P, 2, HALF, E], F32)
            gmax = sb("gmax", [P, 2, HALF], F32)
            gsum = sb("gsum", [P, 2, HALF], F32)
            grec = sb("grec", [P, 2, HALF], F32)
            probs = sb("probs", [P, NT, NE], F32)
            kvs = sb("kvs", [P, DC, P + 1], F32)
            kvm = sb("kvm", [P, DC, P], F32)
            ksm = sb("ksm", [P, DC, P], F32)
            kvT = sb("kvT", [P, DC, P], F32)
            mo = sb("mo", [P, DC, D], F32)
            qz = [sb(f"qz{h}", [P, DC, HALF * P], F32) for h in range(2)]
            dd = sb("dd", [P, HALF * P], F32)
            zz = sb("zz", [P, HALF * P], F32)
            eps6 = sb("eps6", [P, 1], F32)
            zeros = sb("zeros", [P, D], F32)
            wpiece = sb("wpiece", [P, 2, 1024], F32)
            piece_max = sb("piece_max", [P, 2, 16], F32)
            ewmax = sb("ewmax", [P, 2, E], F32)
            ewall = sb("ewall", [P, 2, E], F32)
            ewpow = sb("ewpow", [P, 2, E], F32)
            ewrec = sb("ewrec", [P, 2, E], F32)
            rows = sb("rows", [NE, S], F32)
            top8 = sb("top8", [NE, TOP], F32)
            at8 = sb("at8", [NE, TOP], U32)
            topv = sb("topv", [NE, CAP], F32)
            topi = sb("topi", [NE, CAP], F32)
            rowno = sb("rowno", [NE, 1], I32)
            rowbase = sb("rowbase", [NE, 1], I32)
            rowoff = sb("rowoff", [NE, 1], F32)

            pT = ps("pT", [P, 2, DC, P], F16)
            pP = [ps(f"pP{i}", [P, 512]) for i in range(2)]
            pG = ps("pG", [P, 2, HALF, 64])
            pKV = ps("pKV", [P, 512])
            pQ = ps("pQ", [P, 512])
            pD = ps("pD", [P, 512])
            pO = ps("pO", [P, 2, D])

            consts = event("consts")
            w_in = event("w_in", step=16)
            wprep = event("wprep")
            wfold = event("wfold")
            wturn = event("wturn")
            whi = event("whi")
            x_in = event("x_in", step=16)
            zero_out = event("zero_out", step=16)
            stat_done = event("stat_done")
            aggr_done = event("aggr_done")
            veps_done = event("veps_done", credit=1)
            rpow_done = event("rpow_done")
            rstd_done = event("rstd_done", credit=1)
            xm_done = event("xm_done", per=NT)
            hi_done = event("hi_done", per=NT)
            lo_done = event("lo_done", per=NT)
            row_out = [event(f"row_out{h}", step=16, credit=1) for h in range(2)]
            turned = event("turned", per=NT, credit=HALF + 1)
            xT_done = event("xT_done", per=NT, credit=1)
            proj = event("proj", per=NT)
            gated = event("gated", per=2)
            v_done = event("v_done", per=NT, credit=2)
            kraw_done = event("kraw_done", per=NT)
            kmin_done = event("kmin_done", per=NT)
            ek_done = event("ek_done", per=NT)
            k_done = event("k_done", per=NT, credit=2)
            kv_used = event("kv_used", per=NT, credit=2)
            kv_out = event("kv_out", credit=1)
            gmax_done = event("gmax_done", per=2)
            gsub_done = event("gsub_done", per=2, credit=1)
            gexp_done = event("gexp_done", per=2)
            gsum_done = event("gsum_done", per=2)
            grec_done = event("grec_done", per=2)
            prob_done = event("prob_done", per=2)
            q_proj = event("q_proj", per=4, credit=3)
            qraw_done = event("qraw_done", per=4, credit=1)
            qmin_done = event("qmin_done", per=4)
            eq_done = event("eq_done", per=4)
            q_done = event("q_done", per=4, credit=1)
            bo_done = event("bo_done")
            kvs_done = event("kvs_done")
            kvm_done = event("kvm_done", per=4)
            kv_turned = event("kv_turned")
            kvT_done = event("kvT_done")
            mo_mm = event("mo_mm")
            mo_done = event("mo_done")
            den = event("den", per=4)
            shifted = event("shifted", per=4, credit=1)
            inverted = event("inverted", per=4)
            qz_done = event("qz_done", per=4, credit=1)
            out_mm = event("out_mm", per=4, credit=1)
            mix_done = event("mix_done", per=4, credit=1)
            mix_out = [event(f"mix_out{h}", step=16, credit=XR - 2) for h in range(2)]
            piece_in = [event(f"piece_in{i}", per=PIECES // 2, step=16) for i in range(2)]
            piece_done = [event(f"piece_done{i}", per=PIECES // 2, credit=1) for i in range(2)]
            p_turned = event("p_turned")
            rows_done = event("rows_done")
            found = event("found", per=1)
            taken = event("taken", per=1)
            kept = event("kept", per=1)
            sc_step = event("sc_step")
            sc_fold = event("sc_fold")
            pick_turned = event("pick_turned")
            picks_done = event("picks_done")

            segments = [(0, LAG, True, False, True), (LAG, NB - 1, True, True, True),
                        (NB - 1, NB, True, True, False), (NB, NB + LAG, False, True, False)]

            def run(eng, body):
                for lo, hi, s1, s2, nxt in segments:
                    if hi - lo == 1:
                        body(lo, s1, s2, nxt)
                    else:
                        with eng.Fori(lo, hi) as n:
                            body(n, s1, s2, nxt)

            block = ctx.enter_context(nc.Block())

            @block.sync
            def _(sp):
                for i, w in enumerate((Wq, Wk, Wv, Wo)):
                    sp.dma_start(wraw[:, i, :, :], w.rearrange("(c p) d -> p c d", p=P)).then_inc(w_in, 16)
                sp.dma_start(graw[:, :, :], gate_w.rearrange("(c p) e -> p c e", p=P)).then_inc(w_in, 16)
                value = held(sp, at(consts, 0, 0))
                sp.wait_ge(consts, 1)
                sp.wait_ge(consts, value)
                for r in range(2):
                    sp.dma_start(bias_raw[r:r + 1, 0:D], bk.rearrange("(a n) -> a n", a=1)).then_inc(w_in, 16)
                    sp.dma_start(bias_raw[r:r + 1, D:2 * D], bv.rearrange("(a n) -> a n", a=1)).then_inc(w_in, 16)
                sp.dma_start(bo_row[:, :], bo.rearrange("(a n) -> a n", a=1)).then_inc(w_in, 16)
                for c in range(DC):
                    sp.dma_start(bqT[:, c:c + 1], bq[c * P:(c + 1) * P].rearrange("(p a) -> p a", a=1)).then_inc(w_in, 16)
                sp.dma_start(xring[:, 0, :, :], x_rows[0]).then_inc(x_in, 16)
                value = held(sp, at(x_in, 0))
                sp.wait_ge(consts, 1)
                sp.wait_ge(x_in, value)
                sp.dma_start(xring[:, 1, :, :], x_rows[1]).then_inc(x_in, 16)
                value = held(sp, at(consts, 0, 1))
                sp.wait_ge(consts, 1)
                sp.wait_ge(consts, value)

                def body(n, s1, s2, load):
                    if load:
                        value = held(sp, at(x_in, n, 1))
                        sp.wait_ge(consts, 1)
                        sp.wait_ge(x_in, value)
                        for h in range(2):
                            value = held(sp, at(mix_out[h], n, 2 - XR))
                            sp.wait_ge(consts, 1)
                            sp.wait_ge(mix_out[h], value)
                        sp.dma_start(xring[:, (n + 2) % XR, :, :], x_rows[ds(n + 2, 1)].rearrange("o p j d -> p (o j) d")).then_inc(x_in, 16)
                    if s1:
                        for h in range(2):
                            value = held(sp, at(lo_done, n, (h + 1) * HALF - 1))
                            sp.wait_ge(consts, 1)
                            sp.wait_ge(lo_done, value)
                            value = held(sp, at(row_out[h], n, -1))
                            sp.wait_ge(consts, 1)
                            sp.wait_ge(row_out[h], value)
                            sp.dma_start(
                                table_rows[ds(n, 1), :, h * HALF:(h + 1) * HALF, :].rearrange("o p j d -> p (o j) d"),
                                xhl[h][:, :, :, :, :].rearrange("p j a c t -> p j (a c t)")).then_inc(row_out[h], 16)
                        for q in range(PIECES):
                            i = q % 2
                            piece = n * (PIECES // 2) + q // 2
                            value = held(sp, at(piece_done[i], n, q // 2 - 1))
                            sp.wait_ge(consts, 1)
                            sp.wait_ge(piece_done[i], value)
                            if i == 0:
                                dst, src = wpiece[:, 0, :], w1_rows[ds(piece * P, P), :]
                            else:
                                dst = wpiece[:, 1, :].rearrange("p (r d) -> p r d", r=4)
                                src = w2_rows[ds(piece * (4 * P), 4 * P), :].rearrange("(r p) d -> p r d", p=P)
                            sp.dma_start(dst, src).then_inc(piece_in[i], 16)
                        sp.dma_start(
                            acc_rows[ds(n, 1)].rearrange("o p j d -> p (o j) d"),
                            zeros[:, :].unsqueeze(1).to_broadcast([P, NT, D])).then_inc(zero_out, 16)
                    if s2:
                        for h in range(2):
                            value = held(sp, at(mix_done, n - LAG, 2 * h + 1))
                            sp.wait_ge(consts, 1)
                            sp.wait_ge(mix_done, value)
                            value = held(sp, at(mix_out[h], n - LAG, -1))
                            sp.wait_ge(consts, 1)
                            sp.wait_ge(mix_out[h], value)
                            sp.dma_start(
                                mix_rows[ds(n - LAG, 1), :, h * HALF:(h + 1) * HALF, :].rearrange("o p j d -> p (o j) d"),
                                xring[:, ds((n - LAG) % XR, 1), h * HALF:(h + 1) * HALF, :].rearrange("p o j d -> p (o j) d")).then_inc(mix_out[h], 16)

                for lo, hi, s1, s2, load in [(0, LAG, True, False, True), (LAG, NB - 2, True, True, True),
                                             (NB - 2, NB, True, True, False), (NB, NB + LAG, False, True, False)]:
                    if hi - lo == 1:
                        body(lo, s1, s2, load)
                    else:
                        with sp.Fori(lo, hi) as n:
                            body(n, s1, s2, load)
                value = held(sp, at(zero_out, NB - 1))
                sp.wait_ge(consts, 1)
                sp.wait_ge(zero_out, value)
                for h in range(2):
                    value = held(sp, at(row_out[h], NB - 1))
                    sp.wait_ge(consts, 1)
                    sp.wait_ge(row_out[h], value)
                    value = held(sp, at(mix_out[h], NB - 1))
                    sp.wait_ge(consts, 1)
                    sp.wait_ge(mix_out[h], value)

            @block.gpsimd
            def _(pool):
                g = nc.gpsimd
                for ev in (*row_out, *mix_out, *piece_done, veps_done, rstd_done, turned, xT_done, v_done, k_done, kv_used,
                           kv_out, gsub_done, q_proj, qraw_done, q_done, shifted, qz_done, out_mm, mix_done):
                    pool.sem_inc(ev, credit(ev))
                g.memset(bias_raw[:, :], 0.0).then_inc(consts, 1)
                g.memset(zeros[:, :], 0.0).then_inc(consts, 1)
                g.memset(ident[:, :], 0.0).then_inc(consts, 1)
                g.memset(ident16[:, :], 0.0).then_inc(consts, 1)
                g.memset(head_mask[:, :], 1.0).then_inc(consts, 1)
                g.memset(minus_half[:, :], -0.5).then_inc(consts, 1)
                g.iota(rowno[:, :], pattern=[[0, 1]], base=0, channel_multiplier=1).then_inc(consts, 1)
                g.memset(vone[:, :, :, :], 1.0).then_inc(consts, 1)
                g.memset(eps6[:, :], 1e-6)
                g.memset(wmax[:, :], 0.0).then_inc(consts, 1)
                pool.wait_ge(consts, at(consts, 0, 8))
                for m in (ident, ident16):
                    g.affine_select(out=m[:, :], in_=m[:, :], compare_op=ALU.not_equal, fill=1.0,
                                              base=0, pattern=[[-1, P]], channel_multiplier=1).then_inc(consts, 1)
                blocks = head_mask[:, :].rearrange("p (b i) -> p b i", i=HD)
                g.affine_select(out=blocks, in_=blocks, compare_op=ALU.is_ge, fill=0.0,
                                          base=0, pattern=[[-HD, P // HD], [0, HD]], channel_multiplier=1).then_inc(consts, 1)
                pool.wait_ge(consts, at(consts, 0, 11))
                g.affine_select(out=blocks, in_=blocks, compare_op=ALU.is_ge, fill=0.0,
                                          base=HD - 1, pattern=[[HD, P // HD], [0, HD]], channel_multiplier=-1).then_inc(consts, 1)
                pool.wait_ge(consts, at(consts, 0, 12))
                pool.wait_ge(w_in, at(w_in, 0, 11))
                g.partition_broadcast(bo_all[:, :], bo_row[:, :], P).then_inc(consts, 1)
                pool.wait_ge(wprep, at(wprep, 0, 2))
                g.partition_all_reduce(wmax_all[:, :], wmax[:, :], P, bass.bass_isa.ReduceOp.max).then_inc(wfold, 1)

                def norm(n):
                    value = held(pool, at(aggr_done, n))
                    pool.wait_ge(consts, 1)
                    pool.wait_ge(aggr_done, value)
                    g.tensor_scalar(veps[:, :], moments[:, :, 1], 1e-5, None, ALU.add).then_inc(veps_done, 1)
                    pool.wait_ge(veps_done, at(veps_done, n))
                    pool.wait_ge(rstd_done, at(rstd_done, n, -1))
                    g.tensor_tensor(rpow[:, :], veps[:, :], minus_half[:, :], ALU.pow).then_inc(rpow_done, 1)

                norm(0)

                def body(n, s1, s2, nxt):
                    if s2:
                        m = n - LAG
                        pool.wait_ge(kv_out, at(kv_out, m))
                        pool.wait_ge(out_mm, at(out_mm, m, -1))
                        g.tensor_copy(kvs[:, :, :], kvring[:, ds(m % QR, 1), :, :].rearrange("p o c t -> p (o c) t")).then_inc(kvs_done, 1)
                        value = held(pool, at(kvs_done, m))
                        pool.wait_ge(consts, 1)
                        pool.wait_ge(kvs_done, value)
                        for c in range(DC):
                            g.tensor_tensor(kvm[:, c, :], kvs[:, c, 0:P], head_mask[:, :], ALU.mult).then_inc(kvm_done, 1)
                            g.tensor_scalar(ksm[:, c, :], head_mask[:, :], kvs[:, c, P:P + 1], None, ALU.mult).then_inc(kvm_done, 1)
                    if nxt:
                        norm(n + 1)
                    if s1:
                        pool.wait_ge(xm_done, at(xm_done, n, NT - 1))
                        slot = xring[:, ds(n % XR, 1), :, :].rearrange("p o j d -> p (o j) d")
                        g.tensor_tensor(slot, slot, bo_all[:, :].unsqueeze(1).to_broadcast([P, NT, D]), ALU.add).then_inc(bo_done, 1)

                run(pool, body)
                pool.wait_ge(sc_step, at(sc_step, 0, 0))
                g.partition_all_reduce(ewall[:, :, :].rearrange("p a e -> p (a e)"),
                                                  ewmax[:, :, :].rearrange("p a e -> p (a e)"), P,
                                                  bass.bass_isa.ReduceOp.max).then_inc(sc_fold, 1)

            @block.scalar
            def _(act):
                a = nc.scalar
                act.wait_ge(wprep, at(wprep, 0, 8))
                for i, (src, dst) in enumerate(((pP[0], wq[:, 0, :, :]), (pP[1], wkv[:, 0, :, 0:D]), (pQ, wkv[:, 0, :, D:2 * D]))):
                    act.wait_ge(wturn, at(wturn, 0, i))
                    a.activation(dst, src[:, :].rearrange("p (c e) -> p c e", c=DC), ACT.Copy,
                                        scale=wsc[:, (0, 2, 2)[i]:(0, 2, 2)[i] + 1]).then_inc(whi, 1)
                a.activation(wg[:, 0, :, :], graw[:, :, :], ACT.Copy, scale=wsc[:, 1:2]).then_inc(whi, 1)
                act.wait_ge(wturn, at(wturn, 0, 3))
                a.activation(woT[:, :, :], pD[:, :].rearrange("p (c e) -> p c e", c=DC), ACT.Copy).then_inc(whi, 1)

                def high(n, j):
                    h, jj = divmod(j, HALF)
                    act.wait_ge(xm_done, at(xm_done, n, j))
                    if jj == 0:
                        act.wait_ge(row_out[h], at(row_out[h], n, -1))
                        act.wait_ge(turned, at(turned, n, j + HALF - 1 - NT))
                    a.activation(xhl[h][:, jj, 0, :, :].rearrange("p c t -> p (c t)"), xm[:, j % 2, :], ACT.Copy,
                                            scale=rstd[:, j:j + 1]).then_inc(hi_done, 1)

                def turn_out(n, j):
                    h, jj = divmod(j, HALF)
                    act.wait_ge(turned, at(turned, n, j))
                    if jj == 0:
                        act.wait_ge(q_proj, at(q_proj, n, 2 * h + 1 - 4))
                    a.activation(xT[h][:, :, :, jj * P:(jj + 1) * P], pT[:, :, :, :], ACT.Copy).then_inc(xT_done, 1)

                def q_copy(n, u):
                    c = u % DC
                    act.wait_ge(q_proj, at(q_proj, n, u))
                    act.wait_ge(q_done, at(q_done, n, u - 1))
                    a.activation(qraw[:, :], pQ[:, :], ACT.Identity, scale=winv[:, 0:1], bias=bqT[:, c:c + 1]).then_inc(qraw_done, 1)

                def q_exp(n, u):
                    act.wait_ge(qmin_done, at(qmin_done, n, u))
                    a.activation(eq[:, :], eq[:, :], ACT.Exp).then_inc(eq_done, 1)

                def gate_exp(n, h):
                    act.wait_ge(gsub_done, at(gsub_done, n, h))
                    a.activation(gexp[:, h, :, :], gsub[:, h, :, :], ACT.Exp, scale=winv[:, 1:2]).then_inc(gexp_done, 1)

                act.wait_ge(consts, at(consts, 0, 9))
                act.wait_ge(rstd_done, at(rstd_done, 0))
                for j in range(NT):
                    high(0, j)
                turn_out(0, 0)

                def body(n, s1, s2, nxt):
                    m = n - LAG
                    for j in range(NT):
                        if s1:
                            act.wait_ge(proj, at(proj, n, j))
                            act.wait_ge(k_done, at(k_done, n, j - 2))
                            a.activation(kraw[:, j % 2, :], pP[j % 2][:, 0:D], ACT.Copy, scale=winv[:, 2:3]).then_inc(kraw_done, 1)
                            act.wait_ge(kv_used, at(kv_used, n, j - 2))
                            a.activation(vone[:, j % 2, :, 0:P], pP[j % 2][:, D:2 * D].rearrange("p (c t) -> p c t", c=DC),
                                                   ACT.Copy, scale=winv[:, 2:3]).then_inc(v_done, 1)
                            if j < NT - 1:
                                turn_out(n, j + 1)
                            elif nxt:
                                turn_out(n + 1, 0)
                            act.wait_ge(kmin_done, at(kmin_done, n, j))
                            a.activation(ek[:, j % 2, :], ek[:, j % 2, :], ACT.Exp).then_inc(ek_done, 1)
                        if s2 and j == 2:
                            act.wait_ge(mo_mm, at(mo_mm, m))
                            a.activation(mo[:, :, :].rearrange("p c d -> p (c d)"), pD[:, :], ACT.Copy).then_inc(mo_done, 1)
                        if s2 and j in (3, 4, 5, 6):
                            act.wait_ge(den, at(den, m, j - 3))
                            act.wait_ge(qz_done, at(qz_done, m, j - 4))
                            a.activation(dd[:, :], pD[:, :], ACT.Identity, bias=eps6[:, 0:1]).then_inc(shifted, 1)
                        if s1:
                            if j == 4:
                                gate_exp(n, 0)
                            if j in (4, 5):
                                q_copy(n, j - 4)
                            if nxt and j >= 4:
                                if j == 4:
                                    act.wait_ge(rstd_done, at(rstd_done, n, 1))
                                high(n + 1, 2 * (j - 4))
                                high(n + 1, 2 * (j - 4) + 1)
                            if j in (4, 5):
                                q_exp(n, j - 4)
                    if s1:
                        q_copy(n, 2)
                        gate_exp(n, 1)
                        q_exp(n, 2)
                        q_copy(n, 3)
                        q_exp(n, 3)

                run(act, body)

            @block.vector
            def _(dve):
                v = nc.vector
                dve.wait_ge(w_in, at(w_in, 0, 11))
                dve.wait_ge(consts, at(consts, 0, 12))
                for col, src in ((0, wraw[:, 0, :, :]), (2, wraw[:, 1, :, :]), (3, wraw[:, 2, :, :])):
                    v.tensor_reduce(wmax[:, col:col + 1], src, AX.XY, ALU.max, apply_absolute_value=True)
                v.tensor_reduce(wmax[:, 1:2], graw[:, :, :], AX.XY, ALU.max, apply_absolute_value=True).then_inc(wprep, 1)
                v.tensor_reduce(wmax[:, 4:5], bias_raw[:, :], AX.X, ALU.max, apply_absolute_value=True).then_inc(wprep, 1)
                v.tensor_tensor(row01[:, :], ident[:, 0:1], ident[:, 1:2], ALU.add).then_inc(wprep, 1)
                v.memset(bias_lhs[:, :], XSCALE).then_inc(wprep, 1)
                dve.wait_ge(wfold, at(wfold, 0))
                v.tensor_copy(wpow[:, 0:2], wmax_all[:, 0:2])
                v.tensor_reduce(wpow[:, 2:3], wmax_all[:, 2:5], AX.X, ALU.max).then_inc(wprep, 1)
                dve.wait_ge(wprep, at(wprep, 0, 4))
                v.tensor_scalar(wpow[:, :], wpow[:, :], 2.0 ** -60, None, ALU.max).then_inc(wprep, 1)
                dve.wait_ge(wprep, at(wprep, 0, 5))
                bits = wpow[:, :].bitcast(U32)
                v.tensor_scalar(bits, bits, EXP_MASK, None, ALU.bitwise_and).then_inc(wprep, 1)
                dve.wait_ge(wprep, at(wprep, 0, 6))
                v.reciprocal(wrec[:, :], wpow[:, :]).then_inc(wprep, 1)
                dve.wait_ge(wprep, at(wprep, 0, 7))
                v.tensor_scalar(wsc[:, :], wrec[:, :], 2.0 ** 14, None, ALU.mult).then_inc(wprep, 1)
                v.tensor_scalar(winv[:, :], wpow[:, :], 2.0 ** -14 / XSCALE, None, ALU.mult).then_inc(wprep, 1)
                dve.wait_ge(wprep, at(wprep, 0, 9))
                for i, (src, s, hi, lo) in enumerate((
                        (pP[0], 0, wq[:, 0, :, :], wq[:, 1, :, :]),
                        (pP[1], 2, wkv[:, 0, :, 0:D], wkv[:, 1, :, 0:D]),
                        (pQ, 2, wkv[:, 0, :, D:2 * D], wkv[:, 1, :, D:2 * D]),
                        (None, 1, wg[:, 0, :, :], wg[:, 1, :, :]))):
                    full = graw[:, :, :] if src is None else src[:, :].rearrange("p (c e) -> p c e", c=DC)
                    dve.wait_ge(whi, at(whi, 0, i))
                    v.scalar_tensor_tensor(out=lo, in0=full, scalar=wsc[:, s:s + 1], in1=hi,
                                                    op0=ALU.mult, op1=ALU.subtract).then_inc(wprep, 1)
                v.tensor_scalar(bias_hi[:, :], bias_raw[:, :], wsc[:, 2:3], None, ALU.mult).then_inc(wprep, 1)
                dve.wait_ge(wprep, at(wprep, 0, 14))
                v.scalar_tensor_tensor(out=bias_tmp[:, :], in0=bias_raw[:, :], scalar=wsc[:, 2:3],
                                                in1=bias_hi[:, :], op0=ALU.mult, op1=ALU.subtract).then_inc(wprep, 1)
                dve.wait_ge(wprep, at(wprep, 0, 15))
                v.tensor_scalar(bias_tmp[:, :], bias_tmp[:, :], ident[:, 1:2], None, ALU.mult).then_inc(wprep, 1)
                dve.wait_ge(wprep, at(wprep, 0, 16))
                v.scalar_tensor_tensor(out=bias_rows[:, :], in0=bias_hi[:, :], scalar=ident[:, 0:1],
                                                in1=bias_tmp[:, :], op0=ALU.mult, op1=ALU.add).then_inc(wprep, 1)
                v.tensor_scalar(bias_lhs[:, :], bias_lhs[:, :], row01[:, 0:1], None, ALU.mult).then_inc(wprep, 1)

                def tile_of(n, j):
                    return xring[:, ds(n % XR, 1), j, :].rearrange("p o d -> p (o d)")

                def stats_of(n, j):
                    if j == 0:
                        dve.wait_ge(x_in, at(x_in, n))
                    last = v.bn_stats(stats[:, j, :], tile_of(n, j))
                    if j == NT - 1:
                        last.then_inc(stat_done, 1)

                def moments_of(n):
                    value = held(dve, at(veps_done, n, -1))
                    dve.wait_ge(consts, 1)
                    dve.wait_ge(veps_done, value)
                    value = held(dve, at(stat_done, n))
                    dve.wait_ge(consts, 1)
                    dve.wait_ge(stat_done, value)
                    for j in range(NT):
                        last = v.bn_aggr(moments[:, j, :], stats[:, j, :])
                    last.then_inc(aggr_done, 1)

                def root_of(n):
                    dve.wait_ge(rpow_done, at(rpow_done, n))
                    v.tensor_scalar(rstd[:, :], rpow[:, :], XSCALE, None, ALU.mult).then_inc(rstd_done, 1)

                def centre(n, j):
                    v.tensor_scalar(xm[:, j % 2, :], tile_of(n, j), moments[:, j, 0:1], None, ALU.subtract).then_inc(xm_done, 1)

                def low(n, j):
                    h, jj = divmod(j, HALF)
                    if j == 0:
                        dve.wait_ge(rstd_done, at(rstd_done, n))
                    dve.wait_ge(hi_done, at(hi_done, n, j))
                    v.scalar_tensor_tensor(
                        out=xhl[h][:, jj, 1, :, :].rearrange("p c t -> p (c t)"), in0=xm[:, j % 2, :],
                        scalar=rstd[:, j:j + 1], in1=xhl[h][:, jj, 0, :, :].rearrange("p c t -> p (c t)"),
                        op0=ALU.mult, op1=ALU.subtract).then_inc(lo_done, 1)

                def gate_max(n, h):
                    dve.wait_ge(gated, at(gated, n, h))
                    v.tensor_reduce(gmax[:, h, :], pG[:, h, :, 0:E], AX.X, ALU.max).then_inc(gmax_done, 1)
                    dve.wait_ge(gmax_done, at(gmax_done, n, h))
                    v.tensor_tensor(gsub[:, h, :, :], pG[:, h, :, 0:E],
                                                 gmax[:, h, :].unsqueeze(2).to_broadcast([P, HALF, E]), ALU.subtract).then_inc(gsub_done, 1)

                def gate_probs(n, h):
                    dve.wait_ge(gexp_done, at(gexp_done, n, h))
                    v.tensor_reduce(gsum[:, h, :], gexp[:, h, :, :], AX.X, ALU.add).then_inc(gsum_done, 1)
                    dve.wait_ge(gsum_done, at(gsum_done, n, h))
                    v.reciprocal(grec[:, h, :], gsum[:, h, :]).then_inc(grec_done, 1)
                    dve.wait_ge(grec_done, at(grec_done, n, h))
                    v.tensor_tensor(probs[:, h * HALF:(h + 1) * HALF, ds(n * E, E)], gexp[:, h, :, :],
                                                 grec[:, h, :].unsqueeze(2).to_broadcast([P, HALF, E]), ALU.mult).then_inc(prob_done, 1)

                def q_min(n, u):
                    dve.wait_ge(qraw_done, at(qraw_done, n, u))
                    v.tensor_scalar(eq[:, :], qraw[:, :], 0.0, None, ALU.min).then_inc(qmin_done, 1)

                def q_feature(n, u):
                    h, c = divmod(u, DC)
                    dve.wait_ge(eq_done, at(eq_done, n, u))
                    v.scalar_tensor_tensor(
                        out=qring[:, ds(n % QR, 1), c, h * HALF * P:(h + 1) * HALF * P].rearrange("p o t -> p (o t)"),
                        in0=qraw[:, :], scalar=0.0, in1=eq[:, :], op0=ALU.max, op1=ALU.add).then_inc(q_done, 1)

                def divide(m, u):
                    h, c = divmod(u, DC)
                    dve.wait_ge(shifted, at(shifted, m, u))
                    q = qring[:, ds(m % QR, 1), c, h * HALF * P:(h + 1) * HALF * P].rearrange("p o t -> p (o t)")
                    v.reciprocal(zz[:, :], dd[:, :]).then_inc(inverted, 1)
                    dve.wait_ge(inverted, at(inverted, m, u))
                    v.tensor_tensor(qz[h][:, c, :], q, zz[:, :], ALU.mult).then_inc(qz_done, 1)

                def add_x(m, u):
                    if u == 0:
                        dve.wait_ge(bo_done, at(bo_done, m))
                    dve.wait_ge(out_mm, at(out_mm, m, u))
                    tiles = xring[:, ds(m % XR, 1), 2 * u:2 * u + 2, :].rearrange("p o j d -> p (o j) d")
                    v.tensor_tensor(tiles, tiles, pO[:, :, :], ALU.add).then_inc(mix_done, 1)

                def piece(n, q):
                    i = q % 2
                    dve.wait_ge(piece_in[i], at(piece_in[i], n, q // 2))
                    v.tensor_reduce(piece_max[:, i, ds(n * (PIECES // 2) + q // 2, 1)], wpiece[:, i, :],
                                                     AX.X, ALU.max, apply_absolute_value=True).then_inc(piece_done[i], 1)

                def top_round(r):
                    v.max(top8[:, :], rows[:, :]).then_inc(found, 1)
                    dve.wait_ge(found, at(found, r))
                    v.tensor_copy(topv[:, ds(r * TOP, TOP)], top8[:, :])
                    v.max_index(at8[:, :], top8[:, :], rows[:, :])
                    v.match_replace(rows[:, :], top8[:, :], rows[:, :], -1.0).then_inc(taken, 1)
                    dve.wait_ge(taken, at(taken, r))
                    v.tensor_scalar(topi[:, ds(r * TOP, TOP)], at8[:, :], rowoff[:, 0:1], None, ALU.add).then_inc(kept, 1)

                for j in range(NT):
                    stats_of(0, j)
                moments_of(0)
                root_of(0)
                for j in range(NT):
                    centre(0, j)
                    low(0, j)

                def body(n, s1, s2, nxt):
                    m = n - LAG
                    for j in range(NT):
                        if s1:
                            if nxt and j < 4:
                                stats_of(n + 1, 2 * j)
                                stats_of(n + 1, 2 * j + 1)
                                if j == 3:
                                    moments_of(n + 1)
                            dve.wait_ge(kraw_done, at(kraw_done, n, j))
                            v.tensor_scalar(ek[:, j % 2, :], kraw[:, j % 2, :], 0.0, None, ALU.min).then_inc(kmin_done, 1)
                            if j in (5, 6):
                                q_feature(n, j - 5)
                            dve.wait_ge(kv_used, at(kv_used, n, j - 2))
                            dve.wait_ge(ek_done, at(ek_done, n, j))
                            v.scalar_tensor_tensor(out=phik[:, j % 2, :], in0=kraw[:, j % 2, :], scalar=0.0,
                                                             in1=ek[:, j % 2, :], op0=ALU.max, op1=ALU.add).then_inc(k_done, 1)
                            if j == HALF - 1:
                                gate_max(n, 0)
                            if j in (4, 5):
                                q_min(n, j - 4)
                            if j == 6:
                                gate_probs(n, 0)
                        if s2:
                            if j == 1:
                                dve.wait_ge(kv_turned, at(kv_turned, m))
                                v.tensor_copy(kvT[:, :, :].rearrange("p c t -> p (c t)"), pD[:, 0:DC * P]).then_inc(kvT_done, 1)
                            if j in (3, 4, 5, 6):
                                divide(m, j - 3)
                            if j >= 5:
                                add_x(m, j - 5)
                        if s1:
                            if nxt and j >= 4:
                                if j == 4:
                                    root_of(n + 1)
                                centre(n + 1, 2 * (j - 4))
                                centre(n + 1, 2 * (j - 4) + 1)
                                low(n + 1, 2 * (j - 4))
                                low(n + 1, 2 * (j - 4) + 1)
                            for q in range(PIECES):
                                if q % NT == j:
                                    piece(n, q)
                    if s1:
                        gate_max(n, 1)
                    if s2:
                        add_x(m, 3)
                    if s1:
                        q_min(n, 2)
                        q_feature(n, 2)
                        gate_probs(n, 1)
                        q_min(n, 3)
                        q_feature(n, 3)
                        dve.wait_ge(kv_used, at(kv_used, n, NT - 1))
                        v.tensor_copy(kvring[:, ds(n % QR, 1), :, :].rearrange("p o c t -> p (o c t)"),
                                                pKV[:, 0:DC * (P + 1)]).then_inc(kv_out, 1)
                    if not s1:
                        for r in range(RPL):
                            top_round((n - NB) * RPL + r)

                for lo, hi, s1, s2, nxt in segments:
                    if not s1:
                        v.tensor_reduce(ewmax[:, :, :], piece_max[:, :, :].rearrange("p a (e h) -> p a e h", h=2),
                                                   AX.X, ALU.max).then_inc(sc_step, 1)
                        v.tensor_scalar(rowbase[:, :], rowno[:, :], ~(E - 1) & 0xFFFF, None, ALU.bitwise_and).then_inc(sc_step, 1)
                        dve.wait_ge(sc_step, at(sc_step, 0, 1))
                        v.tensor_scalar(rowoff[:, :], rowbase[:, :], float(S // E), None, ALU.mult).then_inc(sc_step, 1)
                        dve.wait_ge(sc_step, at(sc_step, 0, 2))
                        for half in range(2):
                            dve.wait_ge(p_turned, at(p_turned, 0, half))
                            last = v.tensor_copy(rows[:, half * 512:(half + 1) * 512], pP[half][0:NE, :])
                        last.then_inc(rows_done, 1)
                        dve.wait_ge(rows_done, at(rows_done, 0))
                    if hi - lo == 1:
                        body(lo, s1, s2, nxt)
                    else:
                        with dve.Fori(lo, hi) as n:
                            body(n, s1, s2, nxt)
                for r in range(RPL * LAG, ROUNDS):
                    top_round(r)
                dve.wait_ge(sc_fold, at(sc_fold, 0))
                v.tensor_copy(ewpow[:, :, :], ewall[:, :, :]).then_inc(sc_step, 1)
                dve.wait_ge(sc_step, at(sc_step, 0, 3))
                v.tensor_scalar(ewpow[:, :, :], ewpow[:, :, :], 2.0 ** -60, None, ALU.max).then_inc(sc_step, 1)
                dve.wait_ge(sc_step, at(sc_step, 0, 4))
                bits = ewpow[:, :, :].bitcast(U32)
                v.tensor_scalar(bits, bits, EXP_MASK, None, ALU.bitwise_and).then_inc(sc_step, 1)
                dve.wait_ge(sc_step, at(sc_step, 0, 5))
                v.reciprocal(ewrec[:, :, :].rearrange("p a e -> p (a e)"), ewpow[:, :, :].rearrange("p a e -> p (a e)")).then_inc(sc_step, 1)
                dve.wait_ge(sc_step, at(sc_step, 0, 6))
                v.tensor_scalar(scales[:, :, 0], ewpow[:, 0, :], 2.0 ** -14 / XSCALE, None, ALU.mult)
                v.tensor_scalar(scales[:, :, 1], ewrec[:, 0, :], 2.0 ** 6, None, ALU.mult)
                v.tensor_scalar(scales[:, :, 2], ewrec[:, 0, :], 2.0 ** 14, None, ALU.mult)
                v.tensor_scalar(scales[:, :, 3], ewrec[:, 1, :], 2.0 ** 14, None, ALU.mult)
                v.scalar_tensor_tensor(out=scales[:, :, 4], in0=ewpow[:, 0, :], scalar=2.0 ** -20,
                                                  in1=ewpow[:, 1, :], op0=ALU.mult, op1=ALU.mult).then_inc(sc_step, 1)
                for i, dst in enumerate((gains, picks)):
                    for s in range(CAP // P):
                        dve.wait_ge(pick_turned, at(pick_turned, 0, 2 * i + s))
                        src = (pP[i] if s == 0 else (pQ, pD)[i])[:, 0:NE].rearrange("p (g b e) -> p g e b", g=NG, e=E)
                        v.tensor_copy(
                            dst[:, :].rearrange("p (g e b s) -> p g e b s", g=NG, e=E, s=2)[:, :, :, :, s], src).then_inc(picks_done, 1)

            @block.tensor
            def _(pe):
                t = nc.tensor
                pe.wait_ge(consts, at(consts, 0, 12))
                pe.wait_ge(w_in, at(w_in, 0, 11))
                for i, dst in enumerate((pP[0], pP[1], pQ, pD)):
                    for c in range(DC):
                        for r in range(DC):
                            last = t.transpose(dst[:, c * D + r * P:c * D + (r + 1) * P], wraw[:, i, r, c * P:(c + 1) * P], ident[:, :])
                    last.then_inc(wturn, 1)

                def turn(n, j):
                    h, jj = divmod(j, HALF)
                    pe.wait_ge(lo_done, at(lo_done, n, j))
                    pe.wait_ge(xT_done, at(xT_done, n, j - 1))
                    for a in range(2):
                        for c in range(DC):
                            last = t.transpose(pT[:, a, c, :], xhl[h][:, jj, a, c, :], ident16[:, :])
                    last.then_inc(turned, 1)

                def project(n, j):
                    h, jj = divmod(j, HALF)
                    pe.wait_ge(xT_done, at(xT_done, n, j))
                    pe.wait_ge(v_done, at(v_done, n, j - 2))
                    cols = slice(jj * P, (jj + 1) * P)
                    t.matmul(pP[j % 2][:, :], bias_lhs[:, :], bias_rows[:, :], start=True, stop=False)
                    terms = [(0, 0), (0, 1), (1, 0)]
                    for k, (a, b) in enumerate(terms):
                        for c in range(DC):
                            last = t.matmul(pP[j % 2][:, :], xT[h][:, a, c, cols], wkv[:, b, c, :], start=False,
                                            stop=k == 2 and c == DC - 1)
                    last.then_inc(proj, 1)
                    if jj == 0:
                        pe.wait_ge(gsub_done, at(gsub_done, n, h - 1))
                    for k, (a, b) in enumerate(terms):
                        for c in range(DC):
                            last = t.matmul(pG[:, h, jj, 0:E], xT[h][:, a, c, cols], wg[:, b, c, :],
                                            start=k == 0 and c == 0, stop=k == 2 and c == DC - 1)
                    if jj == HALF - 1:
                        last.then_inc(gated, 1)

                def sum_kv(n, j):
                    pe.wait_ge(k_done, at(k_done, n, j))
                    pe.wait_ge(v_done, at(v_done, n, j))
                    if j == 0:
                        pe.wait_ge(kv_out, at(kv_out, n, -1))
                    for c in range(DC):
                        last = t.matmul(pKV[:, c * (P + 1):(c + 1) * (P + 1)], phik[:, j % 2, c * P:(c + 1) * P],
                                        vone[:, j % 2, c, :], start=j == 0 and c == 0, stop=j == NT - 1,
                                        skip_group_check=True)
                    last.then_inc(kv_used, 1)

                def q_part(n, u):
                    h, c = divmod(u, DC)
                    pe.wait_ge(qraw_done, at(qraw_done, n, u - 1))
                    terms = [(0, 0), (0, 1), (1, 0)]
                    for k, (a, b) in enumerate(terms):
                        for cc in range(DC):
                            last = t.matmul(pQ[:, :], wq[:, b, cc, c * P:(c + 1) * P], xT[h][:, a, cc, :],
                                            start=k == 0 and cc == 0, stop=k == 2 and cc == DC - 1)
                    last.then_inc(q_proj, 1)

                def denominator(m, u):
                    h, c = divmod(u, DC)
                    if u == 0:
                        pe.wait_ge(mo_done, at(mo_done, m))
                    else:
                        pe.wait_ge(shifted, at(shifted, m, u - 1))
                    t.matmul(pD[:, :], ksm[:, c, :],
                                    qring[:, ds(m % QR, 1), c, h * HALF * P:(h + 1) * HALF * P].rearrange("p o t -> p (o t)"),
                                    start=True, stop=True).then_inc(den, 1)

                def output(m, u):
                    h = u // 2
                    if u % 2 == 0:
                        pe.wait_ge(qz_done, at(qz_done, m, 2 * h + 1))
                    pe.wait_ge(mix_done, at(mix_done, m, u - 1))
                    for i in range(2):
                        tokens = slice(((u % 2) * 2 + i) * P, ((u % 2) * 2 + i + 1) * P)
                        for c in range(DC):
                            last = t.matmul(pO[:, i, :], qz[h][:, c, tokens], mo[:, c, :], start=c == 0, stop=c == DC - 1)
                    last.then_inc(out_mm, 1)

                pe.wait_ge(wprep, at(wprep, 0, 18))
                pe.wait_ge(whi, at(whi, 0, 4))
                turn(0, 0)

                def body(n, s1, s2, nxt):
                    m = n - LAG
                    for j in range(NT):
                        if s1:
                            if j < NT - 1:
                                turn(n, j + 1)
                            elif nxt:
                                turn(n + 1, 0)
                        if s2 and j == 1:
                            pe.wait_ge(kvm_done, at(kvm_done, m, 3))
                            pe.wait_ge(shifted, at(shifted, m, -1))
                            for c in range(DC):
                                last = t.transpose(pD[:, c * P:(c + 1) * P], kvm[:, c, :], ident[:, :])
                            last.then_inc(kv_turned, 1)
                        if s1:
                            project(n, j)
                        if s2:
                            if j == 2:
                                pe.wait_ge(kvT_done, at(kvT_done, m))
                                for c in range(DC):
                                    last = t.matmul(pD[:, c * D:(c + 1) * D], kvT[:, c, :], woT[:, c, :], start=True, stop=True)
                                last.then_inc(mo_mm, 1)
                            if j in (3, 4, 5, 6):
                                denominator(m, j - 3)
                            if j >= 5:
                                output(m, j - 5)
                        if s1:
                            if j > 0:
                                sum_kv(n, j - 1)
                            if j in (4, 5):
                                q_part(n, j - 4)
                    if s1:
                        q_part(n, 2)
                    if s2:
                        output(m, 3)
                    if s1:
                        sum_kv(n, NT - 1)
                        q_part(n, 3)

                for lo, hi, s1, s2, nxt in segments:
                    if not s1:
                        pe.wait_ge(prob_done, at(prob_done, NB - 1, 1))
                        pe.wait_ge(v_done, at(v_done, NB - 1, NT - 1))
                        for half in range(2):
                            for jj in range(HALF):
                                last = t.transpose(pP[half][0:NE, jj * P:(jj + 1) * P], probs[:, half * HALF + jj, :], ident[:, :])
                            last.then_inc(p_turned, 1)
                    if hi - lo == 1:
                        body(lo, s1, s2, nxt)
                    else:
                        with pe.Fori(lo, hi) as n:
                            body(n, s1, s2, nxt)
                pe.wait_ge(kept, at(kept, ROUNDS - 1))
                pe.wait_ge(rows_done, at(rows_done, 0))
                pe.wait_ge(qz_done, at(qz_done, NB - 1, 3))
                for i, src in enumerate((topv, topi)):
                    for s in range(CAP // P):
                        dst = pP[i] if s == 0 else (pQ, pD)[i]
                        t.transpose(dst[:, 0:NE], src[:, s * P:(s + 1) * P], ident[0:NE, 0:NE]).then_inc(pick_turned, 1)

        with ExitStack() as ctx:
            sb, ps = sb_in(ctx), ps_in(ctx)
            w1s = [sb(f"w1s{i}", [P, 2, DC, HID], F16) for i in range(2)]
            w2s = [sb(f"w2s{i}", [P, 2, HC, D], F16) for i in range(2)]
            stage = sb("stage", [P, 4, 1024], F32)
            cur = [sb(f"cur{i}", [P, 5], F32) for i in range(2)]
            idx = [sb(f"idx{i}", [P, 4], U32) for i in range(4)]
            xg = [sb(f"xg{i}", [P, 4, 2, DC, P], F16) for i in range(2)]
            xgT = [sb(f"xgT{i}", [P, 2, DC, 512], F16) for i in range(2)]
            gel = sb("gel", [P, 2, 512], F32)
            hid = sb("hid", [P, 4, 2, 512], F16)
            yo = [sb(f"yo{i}", [P, 4, D], F32) for i in range(2)]
            fmix = sb("fmix", [P, 2, 2, D], F32)
            facc = sb("facc", [P, 2, 2, D], F32)
            fffn = sb("fffn", [P, 2, 2, D], BF16)

            pX = [ps(f"pX{i}", [P, 2, DC, P], F16) for i in range(2)]
            pH = [ps(f"pH{i}", [P, 512]) for i in range(4)]
            pY = [ps(f"pY{i}", [P, 2, D]) for i in range(2)]

            idx_done = event("idx_done", per=4)
            rows_in = [event(f"rows_in{i}", step=64) for i in range(2)]
            x_turned = event("x_turned", per=4)
            xgT_done = event("xgT_done", per=4, credit=2)
            h_mm = event("h_mm", per=HC)
            gel_done = event("gel_done", per=HC, credit=4)
            hhi_done = event("hhi_done", per=HC)
            hlo_done = event("hlo_done", per=HC, credit=2)
            y_mm = event("y_mm", per=HC, credit=4)
            y_done = event("y_done", credit=1)
            added = [event(f"added{i}", step=64) for i in range(2)]
            part_in = [event(f"part_in{r}", step=16) for r in range(4)]
            cur_done = event("cur_done")
            whi_done = event("whi_done", per=4)
            wlo_done = event("wlo_done", per=4, credit=4)
            fin_in = [event(f"fin_in{i}", step=32) for i in range(2)]
            fin_cast = event("fin_cast")
            fin_done = event("fin_done")
            fin_out = [event(f"fin_out{i}", step=16, credit=1) for i in range(2)]

            LAST = 4 * NBODY - 1
            FIN0 = 16
            bodies = [(0, 1, False, False), (1, 4 if NG > 1 else 3, False, False)]
            if NG > 1:
                bodies.append((4, NBODY - 1, True, False))
            bodies.append((NBODY - 1, NBODY, NG > 1, True))

            def run_b(eng, body, tail=None):
                for lo, hi, fin, last in bodies:
                    if hi - lo == 1:
                        body(lo, fin, last)
                    else:
                        with eng.Fori(lo, hi) as b:
                            body(b, fin, last)
                if tail is not None:
                    with eng.Fori(NBODY, NBODY + 4) as b:
                        tail(b)

            def fin_rows(dram, b, q):
                f = b * 4 + (q - FIN0)
                return dram[ds(f * (2 * P), 2 * P), :].rearrange("(s p) d -> p s d", p=P)

            out_rows = out.rearrange("n t d -> (n t) d")

            def part_src(e, r):
                if r < 2:
                    return w1_rows[ds(e * D + r * P, P), :]
                return w2_rows[ds(e * HID + (r - 2) * 4 * P, 4 * P), :].rearrange("(q p) d -> p q d", p=P)

            def part_dst(i, b, r):
                if r < 2:
                    return w1s[i][:, b, r, :]
                return w2s[i][:, b, (r - 2) * 4:(r - 1) * 4, :]

            def staged(r):
                return stage[:, r, :] if r < 2 else stage[:, r, :].rearrange("p (q d) -> p q d", q=4)

            def first(b, q):
                return isinstance(b, int) and b == 0 and q < 2

            def parts_of(q, last):
                if last and q >= 2:
                    return None, ()
                return 1 + q // 2, ((0, 1), (2, 3))[q % 2]

            block = ctx.enter_context(nc.Block())

            @block.sync
            def _(sp):
                def load_part(load, r):
                    value = held(sp, at(wlo_done, load, r - 4))
                    sp.wait_ge(consts, 1)
                    sp.wait_ge(wlo_done, value)
                    sp.dma_start(staged(r), part_src(load % E, r)).then_inc(part_in[r], 16)

                def load_sums(b, q, tail):
                    i = q % 2
                    if tail:
                        for par in range(2):
                            value = held(sp, at(added[par], LAST // 2))
                            sp.wait_ge(consts, 1)
                            sp.wait_ge(added[par], value)
                    else:
                        value = held(sp, at(added[1 - i], 2 * b, (q - 1) // 2))
                        sp.wait_ge(consts, 1)
                        sp.wait_ge(added[1 - i], value)
                        value = held(sp, at(added[i], 2 * b, q // 2 - 1))
                        sp.wait_ge(consts, 1)
                        sp.wait_ge(added[i], value)
                    value = held(sp, at(fin_out[i], 2 * b, q // 2 - FIN0 // 2 - 1))
                    sp.wait_ge(consts, 1)
                    sp.wait_ge(fin_out[i], value)
                    sp.dma_start(fmix[:, i, :, :], fin_rows(mix, b, q)).then_inc(fin_in[i], 16)
                    sp.dma_start(facc[:, i, :, :], fin_rows(acc, b, q)).then_inc(fin_in[i], 16)

                for r in range(4):
                    load_part(0, r)

                def body(b, fin, last):
                    for q in range(4):
                        ahead, parts = parts_of(q, last)
                        for r in parts:
                            load_part(2 * b + ahead, r)
                        if fin:
                            load_sums(b, q, False)

                def tail(b):
                    for q in range(4):
                        load_sums(b, q, True)

                run_b(sp, body, tail)
                for i in range(2):
                    value = held(sp, at(fin_out[i], 8 * NG - 1))
                    sp.wait_ge(consts, 1)
                    sp.wait_ge(fin_out[i], value)

            @block.gpsimd
            def _(pool):
                g = nc.gpsimd
                for ev in (xgT_done, gel_done, hlo_done, y_mm, y_done, wlo_done, *fin_out):
                    pool.sem_inc(ev, credit(ev))

                def gather(b, q):
                    i = q % 2
                    k = b * 4 + q
                    g.tensor_copy(idx[q % 4][:, :], picks[:, ds(k * 4, 4)]).then_inc(idx_done, 1)
                    value = held(pool, at(idx_done, b, q))
                    pool.wait_ge(consts, 1)
                    pool.wait_ge(idx_done, value)
                    for s in range(4):
                        g.indirect_dma_start(
                            xg[i][:, s, :, :, :].rearrange("p a c t -> p (a c t)"), None, table,
                            bass.IndirectOffsetOnAxis(ap=idx[q % 4][:, s:s + 1], axis=0)).then_inc(rows_in[i], 16)

                gather(0, 0)
                gather(0, 1)

                def body(b, fin, last):
                    for q in range(4):
                        i = q % 2
                        if not first(b, q):
                            pool.wait_ge(added[i], at(added[i], 2 * b, q // 2 - 1))
                        if not (last and q >= 2):
                            pool.wait_ge(x_turned, at(x_turned, 4 * b, 4 * q + 3))
                            gather(b, q + 2)
                        value = held(pool, at(y_done, 4 * b, q))
                        pool.wait_ge(consts, 1)
                        pool.wait_ge(y_done, value)
                        for s in range(4):
                            g.indirect_dma_start(
                                acc, bass.IndirectOffsetOnAxis(ap=idx[q][:, s:s + 1], axis=0), yo[i][:, s, :], None,
                                compute_op=ALU.add).then_inc(added[i], 16)

                run_b(pool, body)
                for par in range(2):
                    pool.wait_ge(added[par], at(added[par], LAST // 2))

            @block.scalar
            def _(act):
                a = nc.scalar

                def weight_high(b, ahead, r, i):
                    load = 2 * b + ahead
                    act.wait_ge(part_in[r], at(part_in[r], load))
                    act.wait_ge(cur_done, at(cur_done, load))
                    a.activation(part_dst(i, 0, r), staged(r), ACT.Copy,
                                             scale=cur[i][:, 2 + r // 2:3 + r // 2]).then_inc(whi_done, 1)

                def rows_T(b, q, s):
                    act.wait_ge(x_turned, at(x_turned, 4 * b, 4 * q + s))
                    a.activation(xgT[q % 2][:, :, :, s * P:(s + 1) * P], pX[s % 2][:, :, :, :], ACT.Copy).then_inc(xgT_done, 1)

                def hidden(b, q, hc):
                    c = cur[(q // 2) % 2]
                    k = HC * q + hc
                    act.wait_ge(h_mm, at(h_mm, 4 * b, k))
                    act.wait_ge(hlo_done, at(hlo_done, 4 * b, k - 2))
                    a.activation(gel[:, hc % 2, :], pH[hc % 4][:, :], ACT.Gelu_apprx_tanh, scale=c[:, 0:1]).then_inc(gel_done, 1)
                    act.wait_ge(gel_done, at(gel_done, 4 * b, k))
                    act.wait_ge(y_mm, at(y_mm, 4 * b, k - 4))
                    a.activation(hid[:, hc % 4, 0, :], gel[:, hc % 2, :], ACT.Copy, scale=c[:, 1:2]).then_inc(hhi_done, 1)

                def store(b, q):
                    i = q % 2
                    act.wait_ge(fin_done, at(fin_done, 4 * b, q - FIN0))
                    act.dma_start(fin_rows(out_rows, b, q), fmix[:, i, :, :]).then_inc(fin_out[i], 16)

                for r in range(4):
                    weight_high(0, 0, r, 0)
                for s in range(4):
                    rows_T(0, 0, s)
                hidden(0, 0, 0)
                hidden(0, 0, 1)

                def body(b, fin, last):
                    for q in range(4):
                        more = not (last and q == 3)
                        ahead, parts = parts_of(q, last)
                        for hc in range(2, HC):
                            hidden(b, q, hc)
                            if more and hc < 6:
                                rows_T(b, q + 1, hc - 2)
                            if parts and hc in (3, 6):
                                r = parts[hc // 6]
                                if hc == 3 and r == 0:
                                    act.wait_ge(y_mm, at(y_mm, 4 * b, HC * q - 1))
                                weight_high(b, ahead, r, ahead % 2)
                        if fin:
                            store(b, q)
                        if more:
                            hidden(b, q + 1, 0)
                            hidden(b, q + 1, 1)

                def tail(b):
                    for q in range(4):
                        store(b, q)

                run_b(act, body, tail)

            @block.vector
            def _(dve):
                v = nc.vector

                def fetch_scales(b, ahead, i):
                    load = 2 * b + ahead
                    v.tensor_copy(cur[i][:, :], scales[:, ds(load % E, 1), :].rearrange("p o s -> p (o s)")).then_inc(cur_done, 1)

                def weight_low(b, ahead, r, i):
                    load = 2 * b + ahead
                    dve.wait_ge(whi_done, at(whi_done, load, r))
                    v.scalar_tensor_tensor(out=part_dst(i, 1, r), in0=staged(r), scalar=cur[i][:, 2 + r // 2:3 + r // 2],
                                                       in1=part_dst(i, 0, r), op0=ALU.mult, op1=ALU.subtract).then_inc(wlo_done, 1)

                def hidden_low(b, q, hc):
                    k = HC * q + hc
                    dve.wait_ge(hhi_done, at(hhi_done, 4 * b, k))
                    v.scalar_tensor_tensor(out=hid[:, hc % 4, 1, :], in0=gel[:, hc % 2, :],
                                                       scalar=cur[(q // 2) % 2][:, 1:2], in1=hid[:, hc % 4, 0, :],
                                                       op0=ALU.mult, op1=ALU.subtract).then_inc(hlo_done, 1)

                def weigh(b, q):
                    i = q % 2
                    dve.wait_ge(y_mm, at(y_mm, 4 * b, HC * q + HC - 1))
                    if not first(b, q):
                        dve.wait_ge(added[i], at(added[i], 2 * b, q // 2 - 1))
                    for s in range(4):
                        last = v.tensor_scalar(yo[i][:, s, :], pY[s // 2][:, s % 2, :], gains[:, ds((b * 4 + q) * 4 + s, 1)],
                                               cur[(q // 2) % 2][:, 4:5], ALU.mult, ALU.mult)
                    last.then_inc(y_done, 1)

                def finish(b, q):
                    i = q % 2
                    dve.wait_ge(fin_in[i], at(fin_in[i], 2 * b, q // 2 - FIN0 // 2))
                    v.tensor_copy(fffn[:, i, :, :], facc[:, i, :, :]).then_inc(fin_cast, 1)
                    dve.wait_ge(fin_cast, at(fin_cast, 4 * b, q - FIN0))
                    v.tensor_tensor(fmix[:, i, :, :], fmix[:, i, :, :], fffn[:, i, :, :], ALU.add).then_inc(fin_done, 1)

                fetch_scales(0, 0, 0)
                for r in range(4):
                    weight_low(0, 0, r, 0)
                hidden_low(0, 0, 0)
                hidden_low(0, 0, 1)

                def body(b, fin, last):
                    for q in range(4):
                        ahead, parts = parts_of(q, last)
                        if parts and parts[0] == 0:
                            dve.wait_ge(y_done, at(y_done, 4 * b, q - 1))
                            fetch_scales(b, ahead, ahead % 2)
                        for hc in range(2, HC):
                            hidden_low(b, q, hc)
                            if parts and hc in (3, 6):
                                weight_low(b, ahead, parts[hc // 6], ahead % 2)
                            if fin and hc == 5:
                                finish(b, q)
                        if not (last and q == 3):
                            hidden_low(b, q + 1, 0)
                            hidden_low(b, q + 1, 1)
                        weigh(b, q)

                def tail(b):
                    for q in range(4):
                        finish(b, q)

                run_b(dve, body, tail)

            @block.tensor
            def _(pe):
                t = nc.tensor
                terms = [(0, 0), (0, 1), (1, 0)]

                def turn_rows(b, q, s):
                    i = q % 2
                    if s == 0:
                        pe.wait_ge(rows_in[i], at(rows_in[i], 2 * b, q // 2))
                    pe.wait_ge(xgT_done, at(xgT_done, 4 * b, 4 * q + s - 2))
                    for a in range(2):
                        for c in range(DC):
                            last = t.transpose(pX[s % 2][:, a, c, :], xg[i][:, s, a, c, :], ident16[:, :])
                    last.then_inc(x_turned, 1)

                def product1(b, q, hc):
                    i, w = q % 2, w1s[(q // 2) % 2]
                    if hc == 0:
                        pe.wait_ge(xgT_done, at(xgT_done, 4 * b, 4 * q + 3))
                        if q % 2 == 0:
                            pe.wait_ge(wlo_done, at(wlo_done, 2 * b, 4 * (q // 2) + 3))
                    pe.wait_ge(gel_done, at(gel_done, 4 * b, HC * q + hc - 4))
                    for k, (ad, aw) in enumerate(terms):
                        for c in range(DC):
                            last = t.matmul(pH[hc % 4][:, :], w[:, aw, c, hc * P:(hc + 1) * P], xgT[i][:, ad, c, :],
                                            start=k == 0 and c == 0, stop=k == 2 and c == DC - 1)
                    last.then_inc(h_mm, 1)

                def product2(b, q, hc):
                    w = w2s[(q // 2) % 2]
                    if hc == 0:
                        pe.wait_ge(y_done, at(y_done, 4 * b, q - 1))
                    pe.wait_ge(hlo_done, at(hlo_done, 4 * b, HC * q + hc))
                    for s in range(4):
                        for k, (ad, aw) in enumerate(terms):
                            last = t.matmul(pY[s // 2][:, s % 2, :], hid[:, hc % 4, ad, s * P:(s + 1) * P], w[:, aw, hc, :],
                                            start=hc == 0 and k == 0 and s % 2 == 0, stop=hc == HC - 1 and k == 2,
                                            skip_group_check=True)
                    last.then_inc(y_mm, 1)

                for s in range(4):
                    turn_rows(0, 0, s)
                product1(0, 0, 0)
                product1(0, 0, 1)

                def body(b, fin, last):
                    for q in range(4):
                        more = not (last and q == 3)
                        for hc in range(2, HC):
                            product1(b, q, hc)
                            product2(b, q, hc - 2)
                            if more and hc < 6:
                                turn_rows(b, q + 1, hc - 2)
                        if more:
                            product1(b, q + 1, 0)
                        product2(b, q, 6)
                        if more:
                            product1(b, q + 1, 1)
                        product2(b, q, 7)

                run_b(pe, body)


def kernel(L0_attn_x, L0_attn_Wq, L0_attn_bq, L0_attn_Wk, L0_attn_bk, L0_attn_Wv, L0_attn_bv, L0_attn_Wo, L0_attn_bo,
           L0_ffn_gate_w, L0_ffn_w1, L0_ffn_w2):
    import numpy as _np
    import concourse.bacc as _bacc
    from concourse.bass_utils import run_bass_kernel_spmd as _run

    nc = _bacc.Bacc("TRN2", target_bir_lowering=False, num_devices=1)
    arrays, args = {}, []
    for name, a in [("x", L0_attn_x), ("Wq", L0_attn_Wq), ("bq", L0_attn_bq), ("Wk", L0_attn_Wk), ("bk", L0_attn_bk),
                    ("Wv", L0_attn_Wv), ("bv", L0_attn_bv), ("Wo", L0_attn_Wo), ("bo", L0_attn_bo),
                    ("gate_w", L0_ffn_gate_w), ("w1", L0_ffn_w1), ("w2", L0_ffn_w2)]:
        a = _np.ascontiguousarray(a)
        arrays[f"in_{name}"] = a
        args.append(nc.dram_tensor(f"in_{name}", a.shape, F32, kind="ExternalInput").ap())
    shape = tuple(arrays["in_x"].shape)
    tokens = shape[0] * shape[1]
    out = nc.dram_tensor("out_0", shape, F32, kind="ExternalOutput").ap()
    table = nc.dram_tensor("table", (tokens, 2 * D), F16).ap()
    mix = nc.dram_tensor("mix", (tokens, D), F32).ap()
    acc = nc.dram_tensor("acc", (tokens, D), F32).ap()
    block_program(nc, *args, out, table, mix, acc)
    r = _run(nc, [arrays], core_ids=[0])
    return r.results[0]["out_0"]
```

```python
from contextlib import ExitStack

import concourse.bass as bass
from concourse import mybir

ALU = mybir.AluOpType
ACT = mybir.ActivationFunctionType
F32 = mybir.dt.float32
F16 = mybir.dt.float16
BF16 = mybir.dt.bfloat16
U32 = mybir.dt.uint32
I32 = mybir.dt.int32
AX = mybir.AxisListType
ds = bass.ds

P = 128
S = 1024
D = 256
E = 8
HID = 1024
CAP = 2 * S // E
HD = 16
NT = S // P
DC = D // P
HC = HID // P
HALF = NT // 2
XSCALE = 2.0 ** 11
EXP_MASK = 0x7F800000
TOP = 8


class Counts:

    def __init__(self):
        self.of = {}

    def add(self, sem, per, step, credit):
        self.of[sem.name] = (per, step, credit)
        return sem

    def at(self, sem, n, k=0):
        per, step, credit = self.of[sem.name]
        return n * (per * step) + (k + 1 + credit) * step

    def credit(self, sem):
        per, step, credit = self.of[sem.name]
        return credit * step


def held(eng, value):
    return value if isinstance(value, int) else eng.to_reg(value)


def block_program(nc, x, Wq, bq, Wk, bk, Wv, bv, Wo, bo, gate_w, w1, w2, out, table, mix, acc):
    NB = x.shape[0]
    NE = NB * E
    LAG = min(8, NB - 3)
    XR = 3
    QR = LAG + 1
    GB = 4
    NG = NB // GB
    NBODY = 4 * NG
    PIECES = 32 // NB
    ROUNDS = CAP // TOP
    RPL = ROUNDS // LAG
    HEADS = D // HD
    CENTRE = HEADS * (NT - 1)

    x_rows = x.rearrange("n (j p) d -> n p j d", p=P)
    mix_rows = mix.rearrange("(n j p) d -> n p j d", p=P, j=NT)
    acc_rows = acc.rearrange("(n j p) d -> n p j d", p=P, j=NT)
    table_rows = table.rearrange("(n j p) d -> n p j d", p=P, j=NT)
    w1_rows = w1.rearrange("e d f -> (e d) f")
    w2_rows = w2.rearrange("e f d -> (e f) d")

    with ExitStack() as whole:
        def sem(name):
            return whole.enter_context(nc.semaphore(name))

        counts = Counts()
        at, credit = counts.at, counts.credit

        def event(name, per=1, step=1, credit=0):
            return counts.add(sem(name), per, step, credit)

        def sb_in(ctx):
            return lambda name, shape, dt: ctx.enter_context(nc.sbuf_tensor(name, shape, dt))

        def ps_in(ctx):
            return lambda name, shape, dt=F32: ctx.enter_context(nc.psum_tensor(name, shape, dt))

        sb = sb_in(whole)
        ident16 = sb("ident16", [P, P], F16)
        ident = sb("ident", [P, P], F32)
        picks = sb("picks", [P, NG * E * 2 * 4], U32)
        gains = sb("gains", [P, NG * E * 2 * 4], F32)
        scales = sb("scales", [P, E, 5], F32)

        with ExitStack() as ctx:
            sb, ps = sb_in(ctx), ps_in(ctx)
            xring = sb("xring", [P, XR, NT, D], F32)
            x2ring = sb("x2ring", [P, 2, NT, D], F32)
            qring = sb("qring", [P, QR, DC, S], F32)
            kvring = sb("kvring", [P, QR, DC, P + 1], F32)
            xhl = [sb(f"xhl{h}", [P, HALF, 2, DC, P], F16) for h in range(2)]
            xT = [sb(f"xT{h}", [P, 2, DC, HALF * P], F16) for h in range(2)]
            stats = sb("stats", [P, NT, 6], F32)
            moments = sb("moments", [P, NT, 2], F32)
            veps = sb("veps", [P, NT], F32)
            rpow = sb("rpow", [P, NT], F32)
            rstd = sb("rstd", [P, NT], F32)
            minus_half = sb("minus_half", [P, NT], F32)
            xm = sb("xm", [P, 2, D], F32)
            wraw = xring[:, XR - 1, :, :].rearrange("p (w c) d -> p w c d", c=DC)
            graw = sb("graw", [P, DC, E], F32)
            bias_raw = x2ring[:, 1, 0:2, :].rearrange("p j d -> p (j d)")
            bias_tmp = x2ring[:, 1, 2:4, :].rearrange("p j d -> p (j d)")
            bias_rows = sb("bias_rows", [P, 2 * D], F16)
            bias_hi = sb("bias_hi", [P, 2 * D], F16)
            bias_lhs = sb("bias_lhs", [P, P], F16)
            row01 = sb("row01", [P, 1], F32)
            wq = sb("wq", [P, 2, DC, D], F16)
            wkv = sb("wkv", [P, 2, DC, 2 * D], F16)
            wg = sb("wg", [P, 2, DC, E], F16)
            woT = sb("woT", [P, DC, D], F32)
            bqT = sb("bqT", [P, DC], F32)
            bqT_neg = sb("bqT_neg", [P, DC], F32)
            bo_row = sb("bo_row", [1, D], F32)
            bo_all = sb("bo_all", [P, D], F32)
            wmax = sb("wmax", [P, 5], F32)
            wmax_all = sb("wmax_all", [P, 5], F32)
            wpow = sb("wpow", [P, 3], F32)
            wsc = sb("wsc", [P, 3], F32)
            wrec = sb("wrec", [P, 3], F32)
            winv = sb("winv", [P, 3], F32)
            winv_neg = sb("winv_neg", [P, 3], F32)
            head_mask = sb("head_mask", [P, P], F32)
            ek = sb("ek", [P, 2, D], F32)
            kraw = sb("kraw", [P, 2, D], F32)
            phik = sb("phik", [P, 2, D], F32)
            vone = sb("vone", [P, 2, DC, P + 1], F32)
            eq = sb("eq", [P, 2, HALF * P], F32)
            qraw = sb("qraw", [P, 2, HALF * P], F32)
            gsub = sb("gsub", [P, 2, HALF, E], F32)
            gexp = sb("gexp", [P, 2, HALF, E], F32)
            gmax = sb("gmax", [P, 2, HALF], F32)
            gsum = sb("gsum", [P, 2, HALF], F32)
            grec = sb("grec", [P, 2, HALF], F32)
            probs = sb("probs", [P, NT, NE], F32)
            kvs = sb("kvs", [P, DC, P + 1], F32)
            kvm = sb("kvm", [P, DC, P], F32)
            ksz = sb("ksz", [P, DC, CENTRE + P], F32)
            spread = sb("spread", [P, NT, DC, P], BF16)
            kvT = sb("kvT", [P, DC, P], F32)
            mo = sb("mo", [P, DC, D], F32)
            qz = [sb(f"qz{h}", [P, DC, HALF * P], F32) for h in range(2)]
            dd = sb("dd", [P, P], F32)
            zz = sb("zz", [P, P], F32)
            zrest = sb("zrest", [P, P], F32)
            zpart = sb("zpart", [P, 3, P], BF16)
            zeros = sb("zeros", [P, D], F32)
            wpiece = sb("wpiece", [P, 2, 1024], F32)
            piece_max = sb("piece_max", [P, 2, 16], F32)
            ewmax = sb("ewmax", [P, 2, E], F32)
            ewall = sb("ewall", [P, 2, E], F32)
            ewpow = sb("ewpow", [P, 2, E], F32)
            ewrec = sb("ewrec", [P, 2, E], F32)
            rows = wpiece[0:NE, 0, :]
            topv = wpiece[0:NE, 1, 0:CAP]
            topi = wpiece[0:NE, 1, CAP:2 * CAP]
            top8 = sb("top8", [NE, TOP], F32)
            at8 = sb("at8", [NE, TOP], U32)
            rowno = sb("rowno", [NE, 1], I32)
            rowbase = sb("rowbase", [NE, 1], I32)
            rowoff = sb("rowoff", [NE, 1], F32)

            pT = ps("pT", [P, 2, DC, P], F16)
            pP = [ps(f"pP{i}", [P, 512]) for i in range(2)]
            pG = ps("pG", [P, 2, HALF, 64])
            pKV = ps("pKV", [P, 512])
            pQ = ps("pQ", [P, 512])
            pD = ps("pD", [P, 512])
            pO = ps("pO", [P, 2, D])
            banks_z, banks_o, banks_mo = {True: [pD], False: [pD, pKV]}, {True: [pO], False: [pO, pG]}, {True: pD, False: pP[0]}

            banks_q = [pQ, pQ, pQ, pD]

            def pair(bank):
                return (bank[:, :, :, :].rearrange("p a b c -> p (a b c)") if bank is pG else
                        bank[:, :, :].rearrange("p a d -> p (a d)")).rearrange("p (i d) -> p i d", i=2)

            def free_of(banks, u):
                return u - 1 if len(banks) == 1 or u == 0 else u - 2 if u > 1 else None

            consts = event("consts")
            w_in = event("w_in", step=16)
            wprep = event("wprep")
            wfold = event("wfold")
            wturn = event("wturn")
            whi = event("whi")
            x_in = event("x_in", step=16)
            x2_in = event("x2_in", step=16)
            zero_out = event("zero_out", step=16)
            stat_done = event("stat_done")
            aggr_done = event("aggr_done")
            veps_done = event("veps_done", credit=1)
            rpow_done = event("rpow_done")
            rstd_done = event("rstd_done", credit=1)
            xm_done = event("xm_done", per=NT, credit=1)
            hi_done = event("hi_done", per=NT)
            lo_done = event("lo_done", per=NT)
            row_out = [event(f"row_out{h}", step=16, credit=1) for h in range(2)]
            turned = event("turned", per=NT, credit=HALF + 1)
            xT_done = event("xT_done", per=NT, credit=1)
            proj = event("proj", per=NT)
            gated = event("gated", per=2)
            v_done = event("v_done", per=NT, credit=2)
            kraw_done = event("kraw_done", per=NT)
            kneg_done = event("kneg_done", per=NT)
            ek_done = event("ek_done", per=NT)
            k_done = event("k_done", per=NT, credit=2)
            kv_used = event("kv_used", per=NT, credit=2)
            kv_out = event("kv_out", credit=1)
            gmax_done = event("gmax_done", per=2)
            gsub_done = event("gsub_done", per=2, credit=1)
            gexp_done = event("gexp_done", per=2)
            gsum_done = event("gsum_done", per=2)
            grec_done = event("grec_done", per=2)
            prob_done = event("prob_done", per=2)
            q_proj = event("q_proj", per=4, credit=3)
            qneg_done = event("qneg_done", per=4)
            qraw_done = event("qraw_done", per=4, credit=1)
            eq_done = event("eq_done", per=4)
            q_done = event("q_done", per=4, credit=2)
            bo_done = event("bo_done")
            kvs_done = event("kvs_done")
            kvm_done = event("kvm_done", per=4)
            kv_turned = event("kv_turned", credit=1)
            kvT_done = event("kvT_done")
            mo_mm = event("mo_mm")
            mo_done = event("mo_done")
            den = event("den", credit=1)
            shifted = event("shifted", credit=1)
            inverted = event("inverted")
            zsplit = event("zsplit", per=4)
            bcast = event("bcast", per=4)
            qz_done = event("qz_done", per=4, credit=1)
            out_mm = event("out_mm", per=4)
            mix_done = event("mix_done", per=4, credit=1)
            mix_out = [event(f"mix_out{h}", step=16, credit=1) for h in range(2)]
            piece_in = [event(f"piece_in{i}", per=PIECES // 2, step=16) for i in range(2)]
            piece_done = [event(f"piece_done{i}", per=PIECES // 2, credit=1) for i in range(2)]
            p_turned = event("p_turned")
            rows_done = event("rows_done")
            found = event("found", per=1)
            taken = event("taken", per=1)
            kept = event("kept", per=1)
            sc_step = event("sc_step")
            sc_fold = event("sc_fold")
            pick_turned = event("pick_turned")
            picks_done = event("picks_done")

            segments = [(0, LAG, True, False, True), (LAG, NB - 1, True, True, True),
                        (NB - 1, NB, True, True, False), (NB, NB + LAG, False, True, False)]

            def run(eng, body):
                for lo, hi, s1, s2, nxt in segments:
                    if hi - lo == 1:
                        body(lo, s1, s2, nxt)
                    else:
                        with eng.Fori(lo, hi) as n:
                            body(n, s1, s2, nxt)

            block = ctx.enter_context(nc.Block())

            @block.sync
            def _(sp):
                for i, w in enumerate((Wq, Wk, Wv, Wo)):
                    sp.dma_start(wraw[:, i, :, :], w.rearrange("(c p) d -> p c d", p=P)).then_inc(w_in, 16)
                sp.dma_start(graw[:, :, :], gate_w.rearrange("(c p) e -> p c e", p=P)).then_inc(w_in, 16)
                value = held(sp, at(consts, 0, 0))
                sp.wait_ge(consts, 1)
                sp.wait_ge(consts, value)
                for r in range(2):
                    sp.dma_start(bias_raw[r:r + 1, 0:D], bk.rearrange("(a n) -> a n", a=1)).then_inc(w_in, 16)
                    sp.dma_start(bias_raw[r:r + 1, D:2 * D], bv.rearrange("(a n) -> a n", a=1)).then_inc(w_in, 16)
                sp.dma_start(bo_row[:, :], bo.rearrange("(a n) -> a n", a=1)).then_inc(w_in, 16)
                for c in range(DC):
                    sp.dma_start(bqT[:, c:c + 1], bq[c * P:(c + 1) * P].rearrange("(p a) -> p a", a=1)).then_inc(w_in, 16)
                sp.dma_start(xring[:, 0, :, :], x_rows[0]).then_inc(x_in, 16)
                value = held(sp, at(x_in, 0))
                sp.wait_ge(consts, 1)
                sp.wait_ge(x_in, value)
                sp.dma_start(xring[:, 1, :, :], x_rows[1]).then_inc(x_in, 16)
                sp.dma_start(x2ring[:, 0, :, :], x_rows[0]).then_inc(x2_in, 16)
                value = held(sp, at(consts, 0, 1))
                sp.wait_ge(consts, 1)
                sp.wait_ge(consts, value)
                sp.wait_ge(wprep, at(wprep, 0, 18))
                sp.wait_ge(wturn, at(wturn, 0, 3))

                def pieces(n, which):
                    for q in which:
                        i = q % 2
                        piece = n * (PIECES // 2) + q // 2
                        value = held(sp, at(piece_done[i], n, q // 2 - 1))
                        sp.wait_ge(consts, 1)
                        sp.wait_ge(piece_done[i], value)
                        if i == 0:
                            dst, src = wpiece[:, 0, :], w1_rows[ds(piece * P, P), :]
                        else:
                            dst = wpiece[:, 1, :].rearrange("p (r d) -> p r d", r=4)
                            src = w2_rows[ds(piece * (4 * P), 4 * P), :].rearrange("(r p) d -> p r d", p=P)
                        sp.dma_start(dst, src).then_inc(piece_in[i], 16)

                def body(n, s1, s2, load, load2):
                    if s1:
                        pieces(n, range(min(2, PIECES)))
                    if load:
                        value = held(sp, at(x_in, n, 1))
                        sp.wait_ge(consts, 1)
                        sp.wait_ge(x_in, value)
                        value = held(sp, at(xm_done, n, -1))
                        sp.wait_ge(consts, 1)
                        sp.wait_ge(xm_done, value)
                        sp.dma_start(xring[:, (n + 2) % XR, :, :], x_rows[ds(n + 2, 1)].rearrange("o p j d -> p (o j) d")).then_inc(x_in, 16)
                    if s1:
                        for h in range(2):
                            value = held(sp, at(lo_done, n, (h + 1) * HALF - 1))
                            sp.wait_ge(consts, 1)
                            sp.wait_ge(lo_done, value)
                            value = held(sp, at(row_out[h], n, -1))
                            sp.wait_ge(consts, 1)
                            sp.wait_ge(row_out[h], value)
                            sp.dma_start(
                                table_rows[ds(n, 1), :, h * HALF:(h + 1) * HALF, :].rearrange("o p j d -> p (o j) d"),
                                xhl[h][:, :, :, :, :].rearrange("p j a c t -> p j (a c t)")).then_inc(row_out[h], 16)
                        pieces(n, range(2, PIECES))
                        sp.dma_start(
                            acc_rows[ds(n, 1)].rearrange("o p j d -> p (o j) d"),
                            zeros[:, :].unsqueeze(1).to_broadcast([P, NT, D])).then_inc(zero_out, 16)
                    if load2:
                        value = held(sp, at(x2_in, n - LAG))
                        sp.wait_ge(consts, 1)
                        sp.wait_ge(x2_in, value)
                        for h in range(2):
                            value = held(sp, at(mix_out[h], n - LAG, -1))
                            sp.wait_ge(consts, 1)
                            sp.wait_ge(mix_out[h], value)
                        sp.dma_start(x2ring[:, ds((n - LAG + 1) % 2, 1), :, :].rearrange("p o j d -> p (o j) d"),
                                     x_rows[ds(n - LAG + 1, 1)].rearrange("o p j d -> p (o j) d")).then_inc(x2_in, 16)
                    if s2:
                        for h in range(2):
                            value = held(sp, at(mix_done, n - LAG, 2 * h + 1))
                            sp.wait_ge(consts, 1)
                            sp.wait_ge(mix_done, value)
                            value = held(sp, at(mix_out[h], n - LAG, -1))
                            sp.wait_ge(consts, 1)
                            sp.wait_ge(mix_out[h], value)
                            sp.dma_start(
                                mix_rows[ds(n - LAG, 1), :, h * HALF:(h + 1) * HALF, :].rearrange("o p j d -> p (o j) d"),
                                x2ring[:, ds((n - LAG) % 2, 1), h * HALF:(h + 1) * HALF, :].rearrange("p o j d -> p (o j) d")).then_inc(mix_out[h], 16)

                for lo, hi, s1, s2, load, load2 in [
                        (0, LAG, True, False, True, False), (LAG, NB - 2, True, True, True, True),
                        (NB - 2, NB, True, True, False, True), (NB, NB + LAG - 1, False, True, False, True),
                        (NB + LAG - 1, NB + LAG, False, True, False, False)]:
                    if hi - lo == 1:
                        body(lo, s1, s2, load, load2)
                    elif hi > lo:
                        with sp.Fori(lo, hi) as n:
                            body(n, s1, s2, load, load2)
                value = held(sp, at(zero_out, NB - 1))
                sp.wait_ge(consts, 1)
                sp.wait_ge(zero_out, value)
                for h in range(2):
                    value = held(sp, at(row_out[h], NB - 1))
                    sp.wait_ge(consts, 1)
                    sp.wait_ge(row_out[h], value)
                    value = held(sp, at(mix_out[h], NB - 1))
                    sp.wait_ge(consts, 1)
                    sp.wait_ge(mix_out[h], value)

            @block.gpsimd
            def _(pool):
                g = nc.gpsimd
                for ev in (*row_out, *mix_out, *piece_done, xm_done, veps_done, rstd_done, turned, xT_done, v_done, k_done, kv_used,
                           kv_out, gsub_done, q_proj, qraw_done, q_done, shifted, den, kv_turned, qz_done, mix_done):
                    pool.sem_inc(ev, credit(ev))
                g.memset(bias_raw[:, :], 0.0).then_inc(consts, 1)
                g.memset(zeros[:, :], 0.0).then_inc(consts, 1)
                g.memset(ident[:, :], 0.0).then_inc(consts, 1)
                g.memset(ident16[:, :], 0.0).then_inc(consts, 1)
                g.memset(head_mask[:, :], 1.0).then_inc(consts, 1)
                g.memset(minus_half[:, :], -0.5).then_inc(consts, 1)
                g.iota(rowno[:, :], pattern=[[0, 1]], base=0, channel_multiplier=1).then_inc(consts, 1)
                g.memset(vone[:, :, :, :], 1.0).then_inc(consts, 1)
                g.memset(ksz[:, :, :], 0.0)
                g.memset(wmax[:, :], 0.0).then_inc(consts, 1)
                pool.wait_ge(consts, at(consts, 0, 8))
                for m in (ident, ident16):
                    g.affine_select(out=m[:, :], in_=m[:, :], compare_op=ALU.not_equal, fill=1.0,
                                              base=0, pattern=[[-1, P]], channel_multiplier=1).then_inc(consts, 1)
                blocks = head_mask[:, :].rearrange("p (b i) -> p b i", i=HD)
                g.affine_select(out=blocks, in_=blocks, compare_op=ALU.is_ge, fill=0.0,
                                          base=0, pattern=[[-HD, P // HD], [0, HD]], channel_multiplier=1).then_inc(consts, 1)
                pool.wait_ge(consts, at(consts, 0, 11))
                g.affine_select(out=blocks, in_=blocks, compare_op=ALU.is_ge, fill=0.0,
                                          base=HD - 1, pattern=[[HD, P // HD], [0, HD]], channel_multiplier=-1).then_inc(consts, 1)
                pool.wait_ge(consts, at(consts, 0, 12))
                g.tensor_copy(spread[:, :, :, :].rearrange("p j c (b i) -> p (j c b) i", i=HD),
                              ident[:, :].unsqueeze(2).to_broadcast([P, P, HD]))
                pool.wait_ge(w_in, at(w_in, 0, 11))
                g.partition_broadcast(bo_all[:, :], bo_row[:, :], P).then_inc(consts, 1)
                pool.wait_ge(wprep, at(wprep, 0, 2))
                g.partition_all_reduce(wmax_all[:, :], wmax[:, :], P, bass.bass_isa.ReduceOp.max).then_inc(wfold, 1)

                def norm(n):
                    value = held(pool, at(aggr_done, n))
                    pool.wait_ge(consts, 1)
                    pool.wait_ge(aggr_done, value)
                    g.tensor_scalar(veps[:, :], moments[:, :, 1], 1e-5, None, ALU.add).then_inc(veps_done, 1)
                    pool.wait_ge(veps_done, at(veps_done, n))
                    pool.wait_ge(rstd_done, at(rstd_done, n, -1))
                    g.tensor_tensor(rpow[:, :], veps[:, :], minus_half[:, :], ALU.pow).then_inc(rpow_done, 1)

                norm(0)

                def body(n, s1, s2, nxt):
                    if s2:
                        m = n - LAG
                        pool.wait_ge(kv_out, at(kv_out, m))
                        pool.wait_ge(den, at(den, m, -1))
                        pool.wait_ge(kv_turned, at(kv_turned, m, -1))
                        g.tensor_copy(kvs[:, :, :], kvring[:, ds(m % QR, 1), :, :].rearrange("p o c t -> p (o c) t")).then_inc(kvs_done, 1)
                        value = held(pool, at(kvs_done, m))
                        pool.wait_ge(consts, 1)
                        pool.wait_ge(kvs_done, value)
                        for c in range(DC):
                            g.tensor_tensor(kvm[:, c, :], kvs[:, c, 0:P], head_mask[:, :], ALU.mult).then_inc(kvm_done, 1)
                            first = CENTRE + c * (P // HD)
                            g.tensor_scalar(ksz[:, c, first:first + P // HD], head_mask[:, :].rearrange("p (b i) -> p b i", i=HD)[:, :, 0],
                                            kvs[:, c, P:P + 1], None, ALU.mult).then_inc(kvm_done, 1)
                        pool.wait_ge(x2_in, at(x2_in, m))
                        slot = x2ring[:, ds(m % 2, 1), :, :].rearrange("p o j d -> p (o j) d")
                        g.tensor_tensor(slot, slot, bo_all[:, :].unsqueeze(1).to_broadcast([P, NT, D]), ALU.add).then_inc(bo_done, 1)
                    if nxt:
                        norm(n + 1)

                run(pool, body)
                pool.wait_ge(sc_step, at(sc_step, 0, 0))
                g.partition_all_reduce(ewall[:, :, :].rearrange("p a e -> p (a e)"),
                                                  ewmax[:, :, :].rearrange("p a e -> p (a e)"), P,
                                                  bass.bass_isa.ReduceOp.max).then_inc(sc_fold, 1)

            @block.scalar
            def _(act):
                a = nc.scalar
                act.wait_ge(wprep, at(wprep, 0, 8))
                for i, (src, dst) in enumerate(((pP[0], wq[:, 0, :, :]), (pP[1], wkv[:, 0, :, 0:D]), (pQ, wkv[:, 0, :, D:2 * D]))):
                    act.wait_ge(wturn, at(wturn, 0, i))
                    a.activation(dst, src[:, :].rearrange("p (c e) -> p c e", c=DC), ACT.Copy,
                                        scale=wsc[:, (0, 2, 2)[i]:(0, 2, 2)[i] + 1]).then_inc(whi, 1)
                a.activation(wg[:, 0, :, :], graw[:, :, :], ACT.Copy, scale=wsc[:, 1:2]).then_inc(whi, 1)
                act.wait_ge(wturn, at(wturn, 0, 3))
                a.activation(woT[:, :, :], pD[:, :].rearrange("p (c e) -> p c e", c=DC), ACT.Copy).then_inc(whi, 1)

                def high(n, j):
                    h, jj = divmod(j, HALF)
                    act.wait_ge(xm_done, at(xm_done, n, j))
                    if jj == 0:
                        act.wait_ge(row_out[h], at(row_out[h], n, -1))
                        act.wait_ge(turned, at(turned, n, j + HALF - 1 - NT))
                    a.activation(xhl[h][:, jj, 0, :, :].rearrange("p c t -> p (c t)"), xm[:, j % 2, :], ACT.Copy,
                                            scale=rstd[:, j:j + 1]).then_inc(hi_done, 1)

                def turn_out(n, j):
                    h, jj = divmod(j, HALF)
                    act.wait_ge(turned, at(turned, n, j))
                    if jj == 0:
                        act.wait_ge(q_proj, at(q_proj, n, 2 * h + 1 - 4))
                    a.activation(xT[h][:, :, :, jj * P:(jj + 1) * P], pT[:, :, :, :], ACT.Copy).then_inc(xT_done, 1)

                def q_out(n, u):
                    c = u % DC
                    act.wait_ge(q_proj, at(q_proj, n, u))
                    act.wait_ge(q_done, at(q_done, n, u - 2))
                    a.activation(eq[:, u % 2, :], banks_q[u][:, :], ACT.Relu, scale=winv_neg[:, 0:1], bias=bqT_neg[:, c:c + 1]).then_inc(qneg_done, 1)
                    a.activation(qraw[:, u % 2, :], banks_q[u][:, :], ACT.Identity, scale=winv[:, 0:1], bias=bqT[:, c:c + 1]).then_inc(qraw_done, 1)

                def q_exp(n, u):
                    act.wait_ge(qneg_done, at(qneg_done, n, u))
                    a.activation(eq[:, u % 2, :], eq[:, u % 2, :], ACT.Exp, scale=-1.0).then_inc(eq_done, 1)

                def gate_exp(n, h):
                    act.wait_ge(gsub_done, at(gsub_done, n, h))
                    a.activation(gexp[:, h, :, :], gsub[:, h, :, :], ACT.Exp, scale=winv[:, 1:2]).then_inc(gexp_done, 1)

                act.wait_ge(consts, at(consts, 0, 9))
                act.wait_ge(rstd_done, at(rstd_done, 0))
                for j in range(HALF):
                    high(0, j)
                turn_out(0, 0)

                def body(n, s1, s2, nxt):
                    m = n - LAG
                    for j in range(NT):
                        if s1:
                            if j < NT - 1:
                                turn_out(n, j + 1)
                            elif nxt:
                                turn_out(n + 1, 0)
                            if j < HALF:
                                high(n, j + HALF)
                            elif nxt:
                                if j == HALF:
                                    act.wait_ge(rstd_done, at(rstd_done, n, 1))
                                high(n + 1, j - HALF)
                            if j in (5, 6):
                                q_out(n, j - 5)
                                if j == 5:
                                    gate_exp(n, 0)
                                q_exp(n, j - 5)
                            act.wait_ge(proj, at(proj, n, j))
                            act.wait_ge(k_done, at(k_done, n, j - 2))
                            a.activation(ek[:, j % 2, :], pP[j % 2][:, 0:D], ACT.Relu, scale=winv_neg[:, 2:3]).then_inc(kneg_done, 1)
                            a.activation(kraw[:, j % 2, :], pP[j % 2][:, 0:D], ACT.Copy, scale=winv[:, 2:3]).then_inc(kraw_done, 1)
                            act.wait_ge(kv_used, at(kv_used, n, j - 2))
                            a.activation(vone[:, j % 2, :, 0:P], pP[j % 2][:, D:2 * D].rearrange("p (c t) -> p c t", c=DC),
                                                   ACT.Copy, scale=winv[:, 2:3]).then_inc(v_done, 1)
                            act.wait_ge(kneg_done, at(kneg_done, n, j))
                            a.activation(ek[:, j % 2, :], ek[:, j % 2, :], ACT.Exp, scale=-1.0).then_inc(ek_done, 1)
                        if s2 and j == 2:
                            act.wait_ge(mo_mm, at(mo_mm, m))
                            a.activation(mo[:, :, :].rearrange("p c d -> p (c d)"), banks_mo[s1][:, :], ACT.Copy).then_inc(mo_done, 1)
                    if s1:
                        q_out(n, 2)
                        q_out(n, 3)
                        gate_exp(n, 1)
                        q_exp(n, 2)
                        q_exp(n, 3)

                run(act, body)

            @block.vector
            def _(dve):
                v = nc.vector
                dve.wait_ge(w_in, at(w_in, 0, 11))
                dve.wait_ge(consts, at(consts, 0, 12))
                for col, src in ((0, wraw[:, 0, :, :]), (2, wraw[:, 1, :, :]), (3, wraw[:, 2, :, :])):
                    v.tensor_reduce(wmax[:, col:col + 1], src, AX.XY, ALU.max, apply_absolute_value=True)
                v.tensor_reduce(wmax[:, 1:2], graw[:, :, :], AX.XY, ALU.max, apply_absolute_value=True).then_inc(wprep, 1)
                v.tensor_reduce(wmax[:, 4:5], bias_raw[:, :], AX.X, ALU.max, apply_absolute_value=True).then_inc(wprep, 1)
                v.tensor_tensor(row01[:, :], ident[:, 0:1], ident[:, 1:2], ALU.add).then_inc(wprep, 1)
                v.memset(bias_lhs[:, :], XSCALE).then_inc(wprep, 1)
                dve.wait_ge(wfold, at(wfold, 0))
                v.tensor_copy(wpow[:, 0:2], wmax_all[:, 0:2])
                v.tensor_reduce(wpow[:, 2:3], wmax_all[:, 2:5], AX.X, ALU.max).then_inc(wprep, 1)
                dve.wait_ge(wprep, at(wprep, 0, 4))
                v.tensor_scalar(wpow[:, :], wpow[:, :], 2.0 ** -60, None, ALU.max).then_inc(wprep, 1)
                dve.wait_ge(wprep, at(wprep, 0, 5))
                bits = wpow[:, :].bitcast(U32)
                v.tensor_scalar(bits, bits, EXP_MASK, None, ALU.bitwise_and).then_inc(wprep, 1)
                dve.wait_ge(wprep, at(wprep, 0, 6))
                v.reciprocal(wrec[:, :], wpow[:, :]).then_inc(wprep, 1)
                dve.wait_ge(wprep, at(wprep, 0, 7))
                v.tensor_scalar(wsc[:, :], wrec[:, :], 2.0 ** 14, None, ALU.mult).then_inc(wprep, 1)
                v.tensor_scalar(winv_neg[:, :], wpow[:, :], -2.0 ** -14 / XSCALE, None, ALU.mult)
                v.tensor_scalar(bqT_neg[:, :], bqT[:, :], -1.0, None, ALU.mult)
                v.tensor_scalar(winv[:, :], wpow[:, :], 2.0 ** -14 / XSCALE, None, ALU.mult).then_inc(wprep, 1)
                dve.wait_ge(wprep, at(wprep, 0, 9))
                for i, (src, s, hi, lo) in enumerate((
                        (pP[0], 0, wq[:, 0, :, :], wq[:, 1, :, :]),
                        (pP[1], 2, wkv[:, 0, :, 0:D], wkv[:, 1, :, 0:D]),
                        (pQ, 2, wkv[:, 0, :, D:2 * D], wkv[:, 1, :, D:2 * D]),
                        (None, 1, wg[:, 0, :, :], wg[:, 1, :, :]))):
                    full = graw[:, :, :] if src is None else src[:, :].rearrange("p (c e) -> p c e", c=DC)
                    dve.wait_ge(whi, at(whi, 0, i))
                    v.scalar_tensor_tensor(out=lo, in0=full, scalar=wsc[:, s:s + 1], in1=hi,
                                                    op0=ALU.mult, op1=ALU.subtract).then_inc(wprep, 1)
                v.tensor_scalar(bias_hi[:, :], bias_raw[:, :], wsc[:, 2:3], None, ALU.mult).then_inc(wprep, 1)
                dve.wait_ge(wprep, at(wprep, 0, 14))
                v.scalar_tensor_tensor(out=bias_tmp[:, :], in0=bias_raw[:, :], scalar=wsc[:, 2:3],
                                                in1=bias_hi[:, :], op0=ALU.mult, op1=ALU.subtract).then_inc(wprep, 1)
                dve.wait_ge(wprep, at(wprep, 0, 15))
                v.tensor_scalar(bias_tmp[:, :], bias_tmp[:, :], ident[:, 1:2], None, ALU.mult).then_inc(wprep, 1)
                dve.wait_ge(wprep, at(wprep, 0, 16))
                v.scalar_tensor_tensor(out=bias_rows[:, :], in0=bias_hi[:, :], scalar=ident[:, 0:1],
                                                in1=bias_tmp[:, :], op0=ALU.mult, op1=ALU.add).then_inc(wprep, 1)
                v.tensor_scalar(bias_lhs[:, :], bias_lhs[:, :], row01[:, 0:1], None, ALU.mult).then_inc(wprep, 1)

                def tile_of(n, j):
                    return xring[:, ds(n % XR, 1), j, :].rearrange("p o d -> p (o d)")

                def stats_of(n, j):
                    if j == 0:
                        dve.wait_ge(x_in, at(x_in, n))
                    last = v.bn_stats(stats[:, j, :], tile_of(n, j))
                    if j == NT - 1:
                        last.then_inc(stat_done, 1)

                def moments_of(n):
                    value = held(dve, at(veps_done, n, -1))
                    dve.wait_ge(consts, 1)
                    dve.wait_ge(veps_done, value)
                    if not (isinstance(n, int) and n == 0):
                        value = held(dve, at(xm_done, n, -1))
                        dve.wait_ge(consts, 1)
                        dve.wait_ge(xm_done, value)
                    value = held(dve, at(stat_done, n))
                    dve.wait_ge(consts, 1)
                    dve.wait_ge(stat_done, value)
                    for j in range(NT):
                        last = v.bn_aggr(moments[:, j, :], stats[:, j, :])
                    last.then_inc(aggr_done, 1)

                def root_of(n):
                    if not (isinstance(n, int) and n == 0):
                        dve.wait_ge(lo_done, at(lo_done, n, -1))
                    dve.wait_ge(rpow_done, at(rpow_done, n))
                    v.tensor_scalar(rstd[:, :], rpow[:, :], XSCALE, None, ALU.mult).then_inc(rstd_done, 1)

                def centre(n, j):
                    if j == 0:
                        dve.wait_ge(aggr_done, at(aggr_done, n))
                    v.tensor_scalar(xm[:, j % 2, :], tile_of(n, j), moments[:, j, 0:1], None, ALU.subtract).then_inc(xm_done, 1)

                def low(n, j):
                    h, jj = divmod(j, HALF)
                    if j == 0:
                        dve.wait_ge(rstd_done, at(rstd_done, n))
                    dve.wait_ge(hi_done, at(hi_done, n, j))
                    v.scalar_tensor_tensor(
                        out=xhl[h][:, jj, 1, :, :].rearrange("p c t -> p (c t)"), in0=xm[:, j % 2, :],
                        scalar=rstd[:, j:j + 1], in1=xhl[h][:, jj, 0, :, :].rearrange("p c t -> p (c t)"),
                        op0=ALU.mult, op1=ALU.subtract).then_inc(lo_done, 1)

                def gate_max(n, h):
                    dve.wait_ge(gated, at(gated, n, h))
                    v.tensor_reduce(gmax[:, h, :], pG[:, h, :, 0:E], AX.X, ALU.max).then_inc(gmax_done, 1)
                    dve.wait_ge(gmax_done, at(gmax_done, n, h))
                    v.tensor_tensor(gsub[:, h, :, :], pG[:, h, :, 0:E],
                                                 gmax[:, h, :].unsqueeze(2).to_broadcast([P, HALF, E]), ALU.subtract).then_inc(gsub_done, 1)

                def gate_probs(n, h):
                    dve.wait_ge(gexp_done, at(gexp_done, n, h))
                    v.tensor_reduce(gsum[:, h, :], gexp[:, h, :, :], AX.X, ALU.add).then_inc(gsum_done, 1)
                    dve.wait_ge(gsum_done, at(gsum_done, n, h))
                    v.reciprocal(grec[:, h, :], gsum[:, h, :]).then_inc(grec_done, 1)
                    dve.wait_ge(grec_done, at(grec_done, n, h))
                    v.tensor_tensor(probs[:, h * HALF:(h + 1) * HALF, ds(n * E, E)], gexp[:, h, :, :],
                                                 grec[:, h, :].unsqueeze(2).to_broadcast([P, HALF, E]), ALU.mult).then_inc(prob_done, 1)

                def q_feature(n, u):
                    h, c = divmod(u, DC)
                    dve.wait_ge(qraw_done, at(qraw_done, n, u))
                    dve.wait_ge(eq_done, at(eq_done, n, u))
                    v.scalar_tensor_tensor(
                        out=qring[:, ds(n % QR, 1), c, h * HALF * P:(h + 1) * HALF * P].rearrange("p o t -> p (o t)"),
                        in0=qraw[:, u % 2, :], scalar=0.0, in1=eq[:, u % 2, :], op0=ALU.max, op1=ALU.add).then_inc(q_done, 1)

                def shift(m):
                    dve.wait_ge(den, at(den, m))
                    v.tensor_scalar(dd[:, :], pQ[:, 0:P], 1e-6, None, ALU.add).then_inc(shifted, 1)

                def invert(m):
                    dve.wait_ge(shifted, at(shifted, m))
                    v.reciprocal(zz[:, :], dd[:, :]).then_inc(inverted, 1)
                    dve.wait_ge(inverted, at(inverted, m))
                    v.tensor_copy(zpart[:, 0, :], zz[:, :]).then_inc(zsplit, 1)

                def split_rest(m):
                    dve.wait_ge(zsplit, at(zsplit, m, 0))
                    v.tensor_tensor(zrest[:, :], zz[:, :], zpart[:, 0, :], ALU.subtract).then_inc(zsplit, 1)
                    dve.wait_ge(zsplit, at(zsplit, m, 1))
                    v.tensor_copy(zpart[:, 1, :], zrest[:, :]).then_inc(zsplit, 1)
                    dve.wait_ge(zsplit, at(zsplit, m, 2))
                    v.tensor_tensor(zpart[:, 2, :], zrest[:, :], zpart[:, 1, :], ALU.subtract).then_inc(zsplit, 1)

                def divide(m, u, s1=True):
                    h, c = divmod(u, DC)
                    q = qring[:, ds(m % QR, 1), c, h * HALF * P:(h + 1) * HALF * P].rearrange("p o t -> p (o t)")
                    dve.wait_ge(bcast, at(bcast, m, u))
                    v.tensor_tensor(qz[h][:, c, :], q, banks_z[s1][u % len(banks_z[s1])][:, :], ALU.mult).then_inc(qz_done, 1)

                def add_x(m, u, s1=True):
                    if u == 0:
                        dve.wait_ge(bo_done, at(bo_done, m))
                    dve.wait_ge(out_mm, at(out_mm, m, u))
                    tiles = x2ring[:, ds(m % 2, 1), 2 * u:2 * u + 2, :].rearrange("p o j d -> p (o j) d")
                    v.tensor_tensor(tiles, tiles, pair(banks_o[s1][u % len(banks_o[s1])]), ALU.add).then_inc(mix_done, 1)

                def piece(n, q):
                    i = q % 2
                    dve.wait_ge(piece_in[i], at(piece_in[i], n, q // 2))
                    v.tensor_reduce(piece_max[:, i, ds(n * (PIECES // 2) + q // 2, 1)], wpiece[:, i, :],
                                                     AX.X, ALU.max, apply_absolute_value=True).then_inc(piece_done[i], 1)

                def top_round(r):
                    v.max(top8[:, :], rows[:, :]).then_inc(found, 1)
                    dve.wait_ge(found, at(found, r))
                    v.tensor_copy(topv[:, ds(r * TOP, TOP)], top8[:, :])
                    v.max_index(at8[:, :], top8[:, :], rows[:, :])
                    v.match_replace(rows[:, :], top8[:, :], rows[:, :], -1.0).then_inc(taken, 1)
                    dve.wait_ge(taken, at(taken, r))
                    v.tensor_scalar(topi[:, ds(r * TOP, TOP)], at8[:, :], rowoff[:, 0:1], None, ALU.add).then_inc(kept, 1)

                for j in range(NT):
                    stats_of(0, j)
                moments_of(0)
                root_of(0)
                for j in range(HALF):
                    centre(0, j)
                    low(0, j)
                centre(0, HALF)

                def body2(n):
                    m = n - LAG

                    def rounds(place):
                        for r in range(place * RPL // 4, (place + 1) * RPL // 4):
                            top_round((n - NB) * RPL + r)

                    dve.wait_ge(kv_turned, at(kv_turned, m))
                    v.tensor_copy(kvT[:, :, :].rearrange("p c t -> p (c t)"), pD[:, 0:DC * P]).then_inc(kvT_done, 1)
                    shift(m)
                    invert(m)
                    split_rest(m)
                    rounds(0)
                    divide(m, 0, False)
                    divide(m, 1, False)
                    rounds(1)
                    divide(m, 2, False)
                    divide(m, 3, False)
                    add_x(m, 0, False)
                    add_x(m, 1, False)
                    rounds(2)
                    add_x(m, 2, False)
                    add_x(m, 3, False)
                    rounds(3)

                def body(n, s1, s2, nxt):
                    m = n - LAG
                    for j in range(NT):
                        if s1:
                            if nxt:
                                for i in ((0, 1, 2), (3, 4, 5), (6, 7))[j] if j < 3 else ():
                                    stats_of(n + 1, i)
                                if j == HALF:
                                    root_of(n + 1)
                            if j == HALF:
                                gate_max(n, 0)
                            if j < HALF:
                                low(n, j + HALF)
                            elif nxt:
                                low(n + 1, j - HALF)
                        if s2 and j == 2:
                            shift(m)
                        if s1:
                            if j < HALF - 1:
                                centre(n, j + 1 + HALF)
                            elif nxt and j < NT - 1:
                                centre(n + 1, j + 1 - HALF)
                            elif nxt:
                                centre(n + 1, HALF)
                            if nxt and j == 2:
                                moments_of(n + 1)
                        if s2:
                            if j == 2:
                                invert(m)
                            if j >= 4:
                                add_x(m, j - 4)
                            if j in (3, 4, 5):
                                divide(m, (0, 2, 3)[j - 3])
                        if s1:
                            dve.wait_ge(kraw_done, at(kraw_done, n, j))
                            dve.wait_ge(kv_used, at(kv_used, n, j - 2))
                            dve.wait_ge(ek_done, at(ek_done, n, j))
                            v.scalar_tensor_tensor(out=phik[:, j % 2, :], in0=kraw[:, j % 2, :], scalar=0.0,
                                                             in1=ek[:, j % 2, :], op0=ALU.max, op1=ALU.add).then_inc(k_done, 1)
                        if s2:
                            if j == 1:
                                dve.wait_ge(kv_turned, at(kv_turned, m))
                                v.tensor_copy(kvT[:, :, :].rearrange("p c t -> p (c t)"), pD[:, 0:DC * P]).then_inc(kvT_done, 1)
                            if j == 2:
                                split_rest(m)
                            if j == 3:
                                divide(m, 1)
                        if s1:
                            if j in (6, 7):
                                q_feature(n, j - 6)
                            if j == 6:
                                gate_probs(n, 0)
                            for q in range(PIECES):
                                if min(2 * q + 5, NT - 1) == j:
                                    piece(n, q)
                    if s1:
                        gate_max(n, 1)
                        q_feature(n, 2)
                        gate_probs(n, 1)
                        q_feature(n, 3)
                        dve.wait_ge(kv_used, at(kv_used, n, NT - 1))
                        v.tensor_copy(kvring[:, ds(n % QR, 1), :, :].rearrange("p o c t -> p (o c t)"),
                                                pKV[:, 0:DC * (P + 1)]).then_inc(kv_out, 1)

                for lo, hi, s1, s2, nxt in segments:
                    if not s1:
                        v.tensor_reduce(ewmax[:, :, :], piece_max[:, :, :].rearrange("p a (e h) -> p a e h", h=2),
                                                   AX.X, ALU.max).then_inc(sc_step, 1)
                        v.tensor_scalar(rowbase[:, :], rowno[:, :], ~(E - 1) & 0xFFFF, None, ALU.bitwise_and).then_inc(sc_step, 1)
                        dve.wait_ge(sc_step, at(sc_step, 0, 1))
                        v.tensor_scalar(rowoff[:, :], rowbase[:, :], float(S // E), None, ALU.mult).then_inc(sc_step, 1)
                        dve.wait_ge(sc_step, at(sc_step, 0, 2))
                        for i in range(2):
                            dve.wait_ge(piece_done[i], at(piece_done[i], NB - 1, PIECES // 2 - 1))
                        for half in range(2):
                            dve.wait_ge(p_turned, at(p_turned, 0, half))
                            last = v.tensor_copy(rows[:, half * 512:(half + 1) * 512], pP[half][0:NE, :])
                        last.then_inc(rows_done, 1)
                        dve.wait_ge(rows_done, at(rows_done, 0))
                    if not s1:
                        with dve.Fori(lo, hi) as n:
                            body2(n)
                    elif hi - lo == 1:
                        body(lo, s1, s2, nxt)
                    else:
                        with dve.Fori(lo, hi) as n:
                            body(n, s1, s2, nxt)
                for r in range(RPL * LAG, ROUNDS):
                    top_round(r)
                dve.wait_ge(sc_fold, at(sc_fold, 0))
                v.tensor_copy(ewpow[:, :, :], ewall[:, :, :]).then_inc(sc_step, 1)
                dve.wait_ge(sc_step, at(sc_step, 0, 3))
                v.tensor_scalar(ewpow[:, :, :], ewpow[:, :, :], 2.0 ** -60, None, ALU.max).then_inc(sc_step, 1)
                dve.wait_ge(sc_step, at(sc_step, 0, 4))
                bits = ewpow[:, :, :].bitcast(U32)
                v.tensor_scalar(bits, bits, EXP_MASK, None, ALU.bitwise_and).then_inc(sc_step, 1)
                dve.wait_ge(sc_step, at(sc_step, 0, 5))
                v.reciprocal(ewrec[:, :, :].rearrange("p a e -> p (a e)"), ewpow[:, :, :].rearrange("p a e -> p (a e)")).then_inc(sc_step, 1)
                dve.wait_ge(sc_step, at(sc_step, 0, 6))
                v.tensor_scalar(scales[:, :, 0], ewpow[:, 0, :], 2.0 ** -14 / XSCALE, None, ALU.mult)
                v.tensor_scalar(scales[:, :, 1], ewrec[:, 0, :], 2.0 ** 6, None, ALU.mult)
                v.tensor_scalar(scales[:, :, 2], ewrec[:, 0, :], 2.0 ** 14, None, ALU.mult)
                v.tensor_scalar(scales[:, :, 3], ewrec[:, 1, :], 2.0 ** 14, None, ALU.mult)
                v.scalar_tensor_tensor(out=scales[:, :, 4], in0=ewpow[:, 0, :], scalar=2.0 ** -20,
                                                  in1=ewpow[:, 1, :], op0=ALU.mult, op1=ALU.mult).then_inc(sc_step, 1)
                for i, dst in enumerate((gains, picks)):
                    for s in range(CAP // P):
                        dve.wait_ge(pick_turned, at(pick_turned, 0, 2 * i + s))
                        src = (pP[i] if s == 0 else (pQ, pD)[i])[:, 0:NE].rearrange("p (g b e) -> p g e b", g=NG, e=E)
                        v.tensor_copy(
                            dst[:, :].rearrange("p (g e b s) -> p g e b s", g=NG, e=E, s=2)[:, :, :, :, s], src).then_inc(picks_done, 1)

            @block.tensor
            def _(pe):
                t = nc.tensor
                pe.wait_ge(consts, at(consts, 0, 12))
                pe.wait_ge(w_in, at(w_in, 0, 11))
                for i, dst in enumerate((pP[0], pP[1], pQ, pD)):
                    for c in range(DC):
                        for r in range(DC):
                            last = t.transpose(dst[:, c * D + r * P:c * D + (r + 1) * P], wraw[:, i, r, c * P:(c + 1) * P], ident[:, :])
                    last.then_inc(wturn, 1)

                def turn(n, j):
                    h, jj = divmod(j, HALF)
                    pe.wait_ge(lo_done, at(lo_done, n, j))
                    pe.wait_ge(xT_done, at(xT_done, n, j - 1))
                    for a in range(2):
                        for c in range(DC):
                            last = t.transpose(pT[:, a, c, :], xhl[h][:, jj, a, c, :], ident16[:, :])
                    last.then_inc(turned, 1)

                def project(n, j):
                    h, jj = divmod(j, HALF)
                    pe.wait_ge(xT_done, at(xT_done, n, j))
                    pe.wait_ge(v_done, at(v_done, n, j - 2))
                    cols = slice(jj * P, (jj + 1) * P)
                    t.matmul(pP[j % 2][:, :], bias_lhs[:, :], bias_rows[:, :], start=True, stop=False)
                    terms = [(0, 0), (0, 1), (1, 0)]
                    for k, (a, b) in enumerate(terms):
                        for c in range(DC):
                            last = t.matmul(pP[j % 2][:, :], xT[h][:, a, c, cols], wkv[:, b, c, :], start=False,
                                            stop=k == 2 and c == DC - 1)
                    last.then_inc(proj, 1)
                    if jj == 0:
                        pe.wait_ge(gsub_done, at(gsub_done, n, h - 1))
                    for k, (a, b) in enumerate(terms):
                        for c in range(DC):
                            last = t.matmul(pG[:, h, jj, 0:E], xT[h][:, a, c, cols], wg[:, b, c, :],
                                            start=k == 0 and c == 0, stop=k == 2 and c == DC - 1)
                    if jj == HALF - 1:
                        last.then_inc(gated, 1)

                def sum_kv(n, j):
                    pe.wait_ge(k_done, at(k_done, n, j))
                    pe.wait_ge(v_done, at(v_done, n, j))
                    if j == 0:
                        pe.wait_ge(kv_out, at(kv_out, n, -1))
                    for c in range(DC):
                        last = t.matmul(pKV[:, c * (P + 1):(c + 1) * (P + 1)], phik[:, j % 2, c * P:(c + 1) * P],
                                        vone[:, j % 2, c, :], start=j == 0 and c == 0, stop=j == NT - 1,
                                        skip_group_check=True)
                    last.then_inc(kv_used, 1)

                def q_part(n, u, mixed=False):
                    h, c = divmod(u, DC)
                    bank = banks_q[u]
                    if u < 3:
                        pe.wait_ge(qraw_done, at(qraw_done, n, u - 1))
                    if u == 0 and mixed:
                        pe.wait_ge(shifted, at(shifted, n - LAG))
                    if u == 3:
                        pe.wait_ge(qraw_done, at(qraw_done, n, -1))
                        if mixed:
                            pe.wait_ge(qz_done, at(qz_done, n - LAG, 3))
                    terms = [(0, 0), (0, 1), (1, 0)]
                    for k, (a, b) in enumerate(terms):
                        for cc in range(DC):
                            last = t.matmul(bank[:, :], wq[:, b, cc, c * P:(c + 1) * P], xT[h][:, a, cc, :],
                                            start=k == 0 and cc == 0, stop=k == 2 and cc == DC - 1)
                    last.then_inc(q_proj, 1)

                def denominators(m, c):
                    if c == 0:
                        pe.wait_ge(kvm_done, at(kvm_done, m, 3))
                    for jj in range(NT):
                        window = slice(CENTRE - HEADS * jj, CENTRE - HEADS * jj + P)
                        last = t.matmul(pQ[:, 0:P], ksz[:, c, window],
                                        qring[:, ds(m % QR, 1), c, jj * P:(jj + 1) * P].rearrange("p o t -> p (o t)"),
                                        start=c == 0 and jj == 0, stop=c == DC - 1 and jj == NT - 1)
                    if c == DC - 1:
                        last.then_inc(den, 1)

                def reciprocals(m, u, s1=True):
                    h, c = divmod(u, DC)
                    if u == 0:
                        pe.wait_ge(mo_done, at(mo_done, m))
                        pe.wait_ge(zsplit, at(zsplit, m, 3))
                    elif free_of(banks_z[s1], u) is not None:
                        pe.wait_ge(qz_done, at(qz_done, m, free_of(banks_z[s1], u)))
                    bank = banks_z[s1][u % len(banks_z[s1])]
                    for i in range(HALF):
                        for part in range(3):
                            last = t.matmul(bank[:, i * P:(i + 1) * P], spread[:, h * HALF + i, c, :], zpart[:, part, :],
                                            start=part == 0, stop=part == 2)
                    last.then_inc(bcast, 1)

                def output(m, u, s1=True):
                    h = u // 2
                    if u % 2 == 0:
                        pe.wait_ge(qz_done, at(qz_done, m, 2 * h + 1))
                    if free_of(banks_o[s1], u) is not None:
                        pe.wait_ge(mix_done, at(mix_done, m, free_of(banks_o[s1], u)))
                    bank = pair(banks_o[s1][u % len(banks_o[s1])])
                    for i in range(2):
                        tokens = slice(((u % 2) * 2 + i) * P, ((u % 2) * 2 + i + 1) * P)
                        for c in range(DC):
                            last = t.matmul(bank[:, i, :], qz[h][:, c, tokens], mo[:, c, :], start=c == 0, stop=c == DC - 1)
                    last.then_inc(out_mm, 1)

                def body2(n):
                    m = n - LAG
                    denominators(m, 0)
                    denominators(m, 1)
                    pe.wait_ge(qz_done, at(qz_done, m, -1))
                    for c in range(DC):
                        last = t.transpose(pD[:, c * P:(c + 1) * P], kvm[:, c, :], ident[:, :])
                    last.then_inc(kv_turned, 1)
                    pe.wait_ge(kvT_done, at(kvT_done, m))
                    for c in range(DC):
                        last = t.matmul(banks_mo[False][:, c * D:(c + 1) * D], kvT[:, c, :], woT[:, c, :], start=True, stop=True)
                    last.then_inc(mo_mm, 1)
                    for u in range(4):
                        reciprocals(m, u, False)
                    for u in range(4):
                        output(m, u, False)

                pe.wait_ge(wprep, at(wprep, 0, 18))
                pe.wait_ge(whi, at(whi, 0, 4))
                turn(0, 0)

                def body(n, s1, s2, nxt):
                    m = n - LAG
                    for j in range(NT):
                        if s1:
                            if j < NT - 1:
                                turn(n, j + 1)
                            elif nxt:
                                turn(n + 1, 0)
                        if s2 and j == 3:
                            reciprocals(m, 0)
                        if s2 and j >= 4:
                            output(m, j - 4)
                        if s1:
                            project(n, j)
                        if s2:
                            if j == 0:
                                pe.wait_ge(qraw_done, at(qraw_done, n, -2))
                                denominators(m, 0)
                            if j == 1:
                                denominators(m, 1)
                                pe.wait_ge(qraw_done, at(qraw_done, n, -1))
                                for c in range(DC):
                                    last = t.transpose(pD[:, c * P:(c + 1) * P], kvm[:, c, :], ident[:, :])
                                last.then_inc(kv_turned, 1)
                            if j == 2:
                                pe.wait_ge(kvT_done, at(kvT_done, m))
                                for c in range(DC):
                                    last = t.matmul(pD[:, c * D:(c + 1) * D], kvT[:, c, :], woT[:, c, :], start=True, stop=True)
                                last.then_inc(mo_mm, 1)
                            if j in (3, 4, 5):
                                reciprocals(m, j - 2)
                        if s1:
                            if j > 0:
                                sum_kv(n, j - 1)
                            if j in (4, 5):
                                q_part(n, j - 4, s2)
                            if j == 7:
                                q_part(n, 2)
                    if s1:
                        q_part(n, 3, s2)
                        sum_kv(n, NT - 1)

                for lo, hi, s1, s2, nxt in segments:
                    if not s1:
                        pe.wait_ge(prob_done, at(prob_done, NB - 1, 1))
                        pe.wait_ge(v_done, at(v_done, NB - 1, NT - 1))
                        for half in range(2):
                            for jj in range(HALF):
                                last = t.transpose(pP[half][0:NE, jj * P:(jj + 1) * P], probs[:, half * HALF + jj, :], ident[:, :])
                            last.then_inc(p_turned, 1)
                        pe.wait_ge(kv_out, at(kv_out, NB - 1))
                        pe.wait_ge(gsub_done, at(gsub_done, NB - 1, 1))
                        pe.wait_ge(qraw_done, at(qraw_done, NB - 1, 3))
                        pe.wait_ge(rows_done, at(rows_done, 0))
                        with pe.Fori(lo, hi) as n:
                            body2(n)
                        continue
                    if hi - lo == 1:
                        body(lo, s1, s2, nxt)
                    else:
                        with pe.Fori(lo, hi) as n:
                            body(n, s1, s2, nxt)
                pe.wait_ge(kept, at(kept, ROUNDS - 1))
                pe.wait_ge(mo_done, at(mo_done, NB - 1))
                pe.wait_ge(qz_done, at(qz_done, NB - 1, 3))
                for i, src in enumerate((topv, topi)):
                    for s in range(CAP // P):
                        dst = pP[i] if s == 0 else (pQ, pD)[i]
                        t.transpose(dst[:, 0:NE], src[:, s * P:(s + 1) * P], ident[0:NE, 0:NE]).then_inc(pick_turned, 1)

        with ExitStack() as ctx:
            sb, ps = sb_in(ctx), ps_in(ctx)
            w1s = [sb(f"w1s{i}", [P, 2, DC, HID], F16) for i in range(2)]
            w2s = [sb(f"w2s{i}", [P, 2, HC, D], F16) for i in range(2)]
            stage = sb("stage", [P, 4, 1024], F32)
            cur = [sb(f"cur{i}", [P, 5], F32) for i in range(2)]
            idx = [sb(f"idx{i}", [P, 4], U32) for i in range(4)]
            xg = [sb(f"xg{i}", [P, 4, 2, DC, P], F16) for i in range(2)]
            xgT = [sb(f"xgT{i}", [P, 2, DC, 512], F16) for i in range(2)]
            gel = sb("gel", [P, 2, 512], F32)
            hid = sb("hid", [P, 4, 2, 512], F16)
            yo = [sb(f"yo{i}", [P, 4, D], F32) for i in range(2)]
            fmix = sb("fmix", [P, 2, 2, D], F32)
            facc = sb("facc", [P, 2, 2, D], F32)
            fffn = sb("fffn", [P, 2, 2, D], BF16)

            pX = [ps(f"pX{i}", [P, 2, DC, P], F16) for i in range(2)]
            pH = [ps(f"pH{i}", [P, 512]) for i in range(4)]
            pY = [ps(f"pY{i}", [P, 2, D]) for i in range(2)]

            idx_done = event("idx_done", per=4)
            rows_in = [event(f"rows_in{i}", step=64) for i in range(2)]
            x_turned = event("x_turned", per=4)
            xgT_done = event("xgT_done", per=4, credit=2)
            h_mm = event("h_mm", per=HC)
            gel_done = event("gel_done", per=HC, credit=4)
            hhi_done = event("hhi_done", per=HC)
            hlo_done = event("hlo_done", per=HC, credit=2)
            y_mm = event("y_mm", per=HC, credit=4)
            y_half = event("y_half")
            y_done = event("y_done", per=2, credit=2)
            added = [event(f"added{i}", step=64) for i in range(2)]
            part_in = [event(f"part_in{r}", step=16) for r in range(4)]
            cur_done = event("cur_done")
            whi_done = event("whi_done", per=4)
            wlo_done = event("wlo_done", per=4, credit=4)
            fin_in = [event(f"fin_in{i}", step=32) for i in range(2)]
            fin_cast = event("fin_cast")
            fin_done = event("fin_done")
            fin_out = [event(f"fin_out{i}", step=16, credit=1) for i in range(2)]

            LAST = 4 * NBODY - 1
            FIN0 = 16
            bodies = [(0, 1, False, False), (1, 4 if NG > 1 else 3, False, False)]
            if NG > 1:
                bodies.append((4, NBODY - 1, True, False))
            bodies.append((NBODY - 1, NBODY, NG > 1, True))

            def run_b(eng, body, tail=None):
                for lo, hi, fin, last in bodies:
                    if hi - lo == 1:
                        body(lo, fin, last)
                    else:
                        with eng.Fori(lo, hi) as b:
                            body(b, fin, last)
                if tail is not None:
                    with eng.Fori(NBODY, NBODY + 4) as b:
                        tail(b)

            def fin_rows(dram, b, q):
                f = b * 4 + (q - FIN0)
                return dram[ds(f * (2 * P), 2 * P), :].rearrange("(s p) d -> p s d", p=P)

            out_rows = out.rearrange("n t d -> (n t) d")

            def part_src(e, r):
                if r < 2:
                    return w1_rows[ds(e * D + r * P, P), :]
                return w2_rows[ds(e * HID + (r - 2) * 4 * P, 4 * P), :].rearrange("(q p) d -> p q d", p=P)

            def part_dst(i, b, r):
                if r < 2:
                    return w1s[i][:, b, r, :]
                return w2s[i][:, b, (r - 2) * 4:(r - 1) * 4, :]

            def staged(r):
                return stage[:, r, :] if r < 2 else stage[:, r, :].rearrange("p (q d) -> p q d", q=4)

            def first(b, q):
                return isinstance(b, int) and b == 0 and q < 2

            def parts_of(q, last):
                if last and q >= 2:
                    return None, ()
                return 1 + q // 2, ((0, 1), (2, 3))[q % 2]

            block = ctx.enter_context(nc.Block())

            @block.sync
            def _(sp):
                def load_part(load, r):
                    value = held(sp, at(wlo_done, load, r - 4))
                    sp.wait_ge(consts, 1)
                    sp.wait_ge(wlo_done, value)
                    sp.dma_start(staged(r), part_src(load % E, r)).then_inc(part_in[r], 16)

                def load_sums(b, q, tail):
                    i = q % 2
                    if tail:
                        for par in range(2):
                            value = held(sp, at(added[par], LAST // 2))
                            sp.wait_ge(consts, 1)
                            sp.wait_ge(added[par], value)
                    else:
                        value = held(sp, at(added[1 - i], 2 * b, (q - 1) // 2))
                        sp.wait_ge(consts, 1)
                        sp.wait_ge(added[1 - i], value)
                        value = held(sp, at(added[i], 2 * b, q // 2 - 1))
                        sp.wait_ge(consts, 1)
                        sp.wait_ge(added[i], value)
                    value = held(sp, at(fin_out[i], 2 * b, q // 2 - FIN0 // 2 - 1))
                    sp.wait_ge(consts, 1)
                    sp.wait_ge(fin_out[i], value)
                    sp.dma_start(fmix[:, i, :, :], fin_rows(mix, b, q)).then_inc(fin_in[i], 16)
                    sp.dma_start(facc[:, i, :, :], fin_rows(acc, b, q)).then_inc(fin_in[i], 16)

                for r in range(4):
                    load_part(0, r)

                def body(b, fin, last):
                    for q in range(4):
                        ahead, parts = parts_of(q, last)
                        for r in parts:
                            load_part(2 * b + ahead, r)
                        if fin:
                            load_sums(b, q, False)

                def tail(b):
                    for q in range(4):
                        load_sums(b, q, True)

                run_b(sp, body, tail)
                for i in range(2):
                    value = held(sp, at(fin_out[i], 8 * NG - 1))
                    sp.wait_ge(consts, 1)
                    sp.wait_ge(fin_out[i], value)

            @block.gpsimd
            def _(pool):
                g = nc.gpsimd
                for ev in (xgT_done, gel_done, hlo_done, y_mm, y_done, wlo_done, *fin_out):
                    pool.sem_inc(ev, credit(ev))

                def gather(b, q):
                    i = q % 2
                    k = b * 4 + q
                    g.tensor_copy(idx[q % 4][:, :], picks[:, ds(k * 4, 4)]).then_inc(idx_done, 1)
                    value = held(pool, at(idx_done, b, q))
                    pool.wait_ge(consts, 1)
                    pool.wait_ge(idx_done, value)
                    for s in range(4):
                        g.indirect_dma_start(
                            xg[i][:, s, :, :, :].rearrange("p a c t -> p (a c t)"), None, table,
                            bass.IndirectOffsetOnAxis(ap=idx[q % 4][:, s:s + 1], axis=0)).then_inc(rows_in[i], 16)

                gather(0, 0)
                gather(0, 1)

                def body(b, fin, last):
                    for q in range(4):
                        i = q % 2
                        if not first(b, q):
                            pool.wait_ge(added[i], at(added[i], 2 * b, q // 2 - 1))
                        if not (last and q >= 2):
                            pool.wait_ge(x_turned, at(x_turned, 4 * b, 4 * q + 3))
                            gather(b, q + 2)
                        value = held(pool, at(y_done, 4 * b, 2 * q + 1))
                        pool.wait_ge(consts, 1)
                        pool.wait_ge(y_done, value)
                        for s in range(4):
                            g.indirect_dma_start(
                                acc, bass.IndirectOffsetOnAxis(ap=idx[q][:, s:s + 1], axis=0), yo[i][:, s, :], None,
                                compute_op=ALU.add).then_inc(added[i], 16)

                run_b(pool, body)
                for par in range(2):
                    pool.wait_ge(added[par], at(added[par], LAST // 2))

            @block.scalar
            def _(act):
                a = nc.scalar

                def weight_high(b, ahead, r, i):
                    load = 2 * b + ahead
                    act.wait_ge(part_in[r], at(part_in[r], load))
                    act.wait_ge(cur_done, at(cur_done, load))
                    a.activation(part_dst(i, 0, r), staged(r), ACT.Copy,
                                             scale=cur[i][:, 2 + r // 2:3 + r // 2]).then_inc(whi_done, 1)

                def rows_T(b, q, s):
                    act.wait_ge(x_turned, at(x_turned, 4 * b, 4 * q + s))
                    a.activation(xgT[q % 2][:, :, :, s * P:(s + 1) * P], pX[s % 2][:, :, :, :], ACT.Copy).then_inc(xgT_done, 1)

                def hidden(b, q, hc):
                    c = cur[(q // 2) % 2]
                    k = HC * q + hc
                    act.wait_ge(h_mm, at(h_mm, 4 * b, k))
                    act.wait_ge(hlo_done, at(hlo_done, 4 * b, k - 2))
                    a.activation(gel[:, hc % 2, :], pH[hc % 4][:, :], ACT.Gelu_apprx_tanh, scale=c[:, 0:1]).then_inc(gel_done, 1)
                    act.wait_ge(gel_done, at(gel_done, 4 * b, k))
                    act.wait_ge(y_mm, at(y_mm, 4 * b, k - 4))
                    a.activation(hid[:, hc % 4, 0, :], gel[:, hc % 2, :], ACT.Copy, scale=c[:, 1:2]).then_inc(hhi_done, 1)

                def store(b, q):
                    i = q % 2
                    act.wait_ge(fin_done, at(fin_done, 4 * b, q - FIN0))
                    act.dma_start(fin_rows(out_rows, b, q), fmix[:, i, :, :]).then_inc(fin_out[i], 16)

                for r in range(4):
                    weight_high(0, 0, r, 0)
                for s in range(4):
                    rows_T(0, 0, s)
                hidden(0, 0, 0)
                hidden(0, 0, 1)

                def body(b, fin, last):
                    for q in range(4):
                        more = not (last and q == 3)
                        ahead, parts = parts_of(q, last)
                        for hc in range(2, HC):
                            hidden(b, q, hc)
                            if more and hc < 6:
                                rows_T(b, q + 1, hc - 2)
                            if parts and hc in (3, 6):
                                r = parts[hc // 6]
                                if hc == 3 and r == 0:
                                    act.wait_ge(y_mm, at(y_mm, 4 * b, HC * q - 1))
                                weight_high(b, ahead, r, ahead % 2)
                        if fin:
                            store(b, q)
                        if more:
                            hidden(b, q + 1, 0)
                            hidden(b, q + 1, 1)

                def tail(b):
                    for q in range(4):
                        store(b, q)

                run_b(act, body, tail)

            @block.vector
            def _(dve):
                v = nc.vector

                def fetch_scales(b, ahead, i):
                    load = 2 * b + ahead
                    v.tensor_copy(cur[i][:, :], scales[:, ds(load % E, 1), :].rearrange("p o s -> p (o s)")).then_inc(cur_done, 1)

                def weight_low(b, ahead, r, i):
                    load = 2 * b + ahead
                    dve.wait_ge(whi_done, at(whi_done, load, r))
                    v.scalar_tensor_tensor(out=part_dst(i, 1, r), in0=staged(r), scalar=cur[i][:, 2 + r // 2:3 + r // 2],
                                                       in1=part_dst(i, 0, r), op0=ALU.mult, op1=ALU.subtract).then_inc(wlo_done, 1)

                def hidden_low(b, q, hc):
                    k = HC * q + hc
                    dve.wait_ge(hhi_done, at(hhi_done, 4 * b, k))
                    v.scalar_tensor_tensor(out=hid[:, hc % 4, 1, :], in0=gel[:, hc % 2, :],
                                                       scalar=cur[(q // 2) % 2][:, 1:2], in1=hid[:, hc % 4, 0, :],
                                                       op0=ALU.mult, op1=ALU.subtract).then_inc(hlo_done, 1)

                def weigh(b, q):
                    i = q % 2
                    if not first(b, q):
                        dve.wait_ge(added[i], at(added[i], 2 * b, q // 2 - 1))
                    for s in range(4):
                        if s == 0:
                            dve.wait_ge(y_half, at(y_half, 4 * b, q))
                        if s == 2:
                            dve.wait_ge(y_mm, at(y_mm, 4 * b, HC * q + HC - 1))
                        last = v.tensor_scalar(yo[i][:, s, :], pY[s // 2][:, s % 2, :], gains[:, ds((b * 4 + q) * 4 + s, 1)],
                                               cur[(q // 2) % 2][:, 4:5], ALU.mult, ALU.mult)
                        if s % 2 == 1:
                            last.then_inc(y_done, 1)

                def finish(b, q):
                    i = q % 2
                    dve.wait_ge(fin_in[i], at(fin_in[i], 2 * b, q // 2 - FIN0 // 2))
                    v.tensor_copy(fffn[:, i, :, :], facc[:, i, :, :]).then_inc(fin_cast, 1)
                    dve.wait_ge(fin_cast, at(fin_cast, 4 * b, q - FIN0))
                    v.tensor_tensor(fmix[:, i, :, :], fmix[:, i, :, :], fffn[:, i, :, :], ALU.add).then_inc(fin_done, 1)

                fetch_scales(0, 0, 0)
                for r in range(4):
                    weight_low(0, 0, r, 0)
                hidden_low(0, 0, 0)
                hidden_low(0, 0, 1)

                def body(b, fin, last):
                    for q in range(4):
                        ahead, parts = parts_of(q, last)
                        if parts and parts[0] == 0:
                            dve.wait_ge(y_done, at(y_done, 4 * b, 2 * q - 1))
                            fetch_scales(b, ahead, ahead % 2)
                        for hc in range(2, HC):
                            hidden_low(b, q, hc)
                            if parts and hc in (3, 6):
                                weight_low(b, ahead, parts[hc // 6], ahead % 2)
                            if fin and hc == 5:
                                finish(b, q)
                        if not (last and q == 3):
                            hidden_low(b, q + 1, 0)
                        weigh(b, q)
                        if not (last and q == 3):
                            hidden_low(b, q + 1, 1)

                def tail(b):
                    for q in range(4):
                        finish(b, q)

                run_b(dve, body, tail)

            @block.tensor
            def _(pe):
                t = nc.tensor
                terms = [(0, 0), (0, 1), (1, 0)]

                def turn_rows(b, q, s):
                    i = q % 2
                    if s == 0:
                        pe.wait_ge(rows_in[i], at(rows_in[i], 2 * b, q // 2))
                    pe.wait_ge(xgT_done, at(xgT_done, 4 * b, 4 * q + s - 2))
                    for a in range(2):
                        for c in range(DC):
                            last = t.transpose(pX[s % 2][:, a, c, :], xg[i][:, s, a, c, :], ident16[:, :])
                    last.then_inc(x_turned, 1)

                def product1(b, q, hc):
                    i, w = q % 2, w1s[(q // 2) % 2]
                    if hc == 0:
                        pe.wait_ge(xgT_done, at(xgT_done, 4 * b, 4 * q + 3))
                        if q % 2 == 0:
                            pe.wait_ge(wlo_done, at(wlo_done, 2 * b, 4 * (q // 2) + 3))
                    pe.wait_ge(gel_done, at(gel_done, 4 * b, HC * q + hc - 4))
                    for k, (ad, aw) in enumerate(terms):
                        for c in range(DC):
                            last = t.matmul(pH[hc % 4][:, :], w[:, aw, c, hc * P:(hc + 1) * P], xgT[i][:, ad, c, :],
                                            start=k == 0 and c == 0, stop=k == 2 and c == DC - 1)
                    last.then_inc(h_mm, 1)

                def product2(b, q, hc):
                    w = w2s[(q // 2) % 2]
                    pe.wait_ge(hlo_done, at(hlo_done, 4 * b, HC * q + hc))
                    for s in range(4):
                        if hc == 0 and s % 2 == 0:
                            pe.wait_ge(y_done, at(y_done, 4 * b, 2 * (q - 1) + s // 2))
                        for k, (ad, aw) in enumerate(terms):
                            last = t.matmul(pY[s // 2][:, s % 2, :], hid[:, hc % 4, ad, s * P:(s + 1) * P], w[:, aw, hc, :],
                                            start=hc == 0 and k == 0 and s % 2 == 0, stop=hc == HC - 1 and k == 2,
                                            skip_group_check=True)
                        if hc == HC - 1 and s == 1:
                            last.then_inc(y_half, 1)
                    last.then_inc(y_mm, 1)

                for s in range(4):
                    turn_rows(0, 0, s)
                product1(0, 0, 0)
                product1(0, 0, 1)

                def body(b, fin, last):
                    for q in range(4):
                        more = not (last and q == 3)
                        for hc in range(2, HC):
                            product1(b, q, hc)
                            product2(b, q, hc - 2)
                            if more and hc < 6:
                                turn_rows(b, q + 1, hc - 2)
                        if more:
                            product1(b, q + 1, 0)
                        product2(b, q, 6)
                        if more:
                            product1(b, q + 1, 1)
                        product2(b, q, 7)

                run_b(pe, body)


def kernel(L0_attn_x, L0_attn_Wq, L0_attn_bq, L0_attn_Wk, L0_attn_bk, L0_attn_Wv, L0_attn_bv, L0_attn_Wo, L0_attn_bo,
           L0_ffn_gate_w, L0_ffn_w1, L0_ffn_w2):
    import numpy as _np
    import concourse.bacc as _bacc
    from concourse.bass_utils import run_bass_kernel_spmd as _run

    nc = _bacc.Bacc("TRN2", target_bir_lowering=False, num_devices=1)
    arrays, args = {}, []
    for name, a in [("x", L0_attn_x), ("Wq", L0_attn_Wq), ("bq", L0_attn_bq), ("Wk", L0_attn_Wk), ("bk", L0_attn_bk),
                    ("Wv", L0_attn_Wv), ("bv", L0_attn_bv), ("Wo", L0_attn_Wo), ("bo", L0_attn_bo),
                    ("gate_w", L0_ffn_gate_w), ("w1", L0_ffn_w1), ("w2", L0_ffn_w2)]:
        a = _np.ascontiguousarray(a)
        arrays[f"in_{name}"] = a
        args.append(nc.dram_tensor(f"in_{name}", a.shape, F32, kind="ExternalInput").ap())
    shape = tuple(arrays["in_x"].shape)
    tokens = shape[0] * shape[1]
    out = nc.dram_tensor("out_0", shape, F32, kind="ExternalOutput").ap()
    table = nc.dram_tensor("table", (tokens, 2 * D), F16).ap()
    mix = nc.dram_tensor("mix", (tokens, D), F32).ap()
    acc = nc.dram_tensor("acc", (tokens, D), F32).ap()
    block_program(nc, *args, out, table, mix, acc)
    r = _run(nc, [arrays], core_ids=[0])
    return r.results[0]["out_0"]
```

```python
from contextlib import ExitStack

import concourse.bass as bass
from concourse import mybir

ALU = mybir.AluOpType
ACT = mybir.ActivationFunctionType
F32 = mybir.dt.float32
F16 = mybir.dt.float16
BF16 = mybir.dt.bfloat16
U32 = mybir.dt.uint32
I32 = mybir.dt.int32
AX = mybir.AxisListType
ds = bass.ds

P = 128
S = 1024
D = 256
E = 8
HID = 1024
CAP = 2 * S // E
HD = 16
NT = S // P
DC = D // P
HC = HID // P
HALF = NT // 2
XSCALE = 2.0 ** 11
EXP_MASK = 0x7F800000
TOP = 8


class Counts:

    def __init__(self):
        self.of = {}

    def add(self, sem, per, step, credit):
        self.of[sem.name] = (per, step, credit)
        return sem

    def at(self, sem, n, k=0):
        per, step, credit = self.of[sem.name]
        return n * (per * step) + (k + 1 + credit) * step

    def credit(self, sem):
        per, step, credit = self.of[sem.name]
        return credit * step


def held(eng, value):
    return value if isinstance(value, int) else eng.to_reg(value)


def block_program(nc, x, Wq, bq, Wk, bk, Wv, bv, Wo, bo, gate_w, w1, w2, out, table, mix, acc):
    NB = x.shape[0]
    NE = NB * E
    LAG = min(8, NB - 3)
    XR = 3
    QR = LAG + 1
    GB = 4
    NG = NB // GB
    NBODY = 4 * NG
    PIECES = 32 // NB
    ROUNDS = CAP // TOP
    RPL = ROUNDS // LAG
    HEADS = D // HD
    CENTRE = HEADS * (NT - 1)

    x_rows = x.rearrange("n (j p) d -> n p j d", p=P)
    mix_rows = mix.rearrange("(n j p) d -> n p j d", p=P, j=NT)
    acc_rows = acc.rearrange("(n j p) d -> n p j d", p=P, j=NT)
    table_rows = table.rearrange("(n j p) d -> n p j d", p=P, j=NT)
    w1_rows = w1.rearrange("e d f -> (e d) f")
    w2_rows = w2.rearrange("e f d -> (e f) d")

    with ExitStack() as whole:
        def sem(name):
            return whole.enter_context(nc.semaphore(name))

        counts = Counts()
        at, credit = counts.at, counts.credit

        def event(name, per=1, step=1, credit=0):
            return counts.add(sem(name), per, step, credit)

        def sb_in(ctx):
            return lambda name, shape, dt: ctx.enter_context(nc.sbuf_tensor(name, shape, dt))

        def ps_in(ctx):
            return lambda name, shape, dt=F32: ctx.enter_context(nc.psum_tensor(name, shape, dt))

        sb = sb_in(whole)
        ident16 = sb("ident16", [P, P], F16)
        ident = sb("ident", [P, P], F32)
        picks = sb("picks", [P, NG * E * 2 * 4], U32)
        gains = sb("gains", [P, NG * E * 2 * 4], F32)
        scales = sb("scales", [P, E, 5], F32)

        with ExitStack() as ctx:
            sb, ps = sb_in(ctx), ps_in(ctx)
            xring = sb("xring", [P, XR, NT, D], F32)
            x2ring = sb("x2ring", [P, 2, NT, D], F32)
            qring = sb("qring", [P, QR, DC, S], F32)
            kvring = sb("kvring", [P, QR, DC, P + 1], F32)
            xhl = [sb(f"xhl{h}", [P, HALF, 2, DC, P], F16) for h in range(2)]
            xT = [sb(f"xT{h}", [P, 2, DC, HALF * P], F16) for h in range(2)]
            stats = sb("stats", [P, NT, 6], F32)
            moments = sb("moments", [P, NT, 2], F32)
            veps = sb("veps", [P, NT], F32)
            rpow = sb("rpow", [P, NT], F32)
            rstd = sb("rstd", [P, NT], F32)
            minus_half = sb("minus_half", [P, NT], F32)
            xm = sb("xm", [P, 2, D], F32)
            wraw = xring[:, XR - 1, :, :].rearrange("p (w c) d -> p w c d", c=DC)
            graw = sb("graw", [P, DC, E], F32)
            bias_raw = x2ring[:, 1, 0:2, :].rearrange("p j d -> p (j d)")
            bias_tmp = x2ring[:, 1, 2:4, :].rearrange("p j d -> p (j d)")
            bias_rows = sb("bias_rows", [P, 2 * D], F16)
            bias_hi = sb("bias_hi", [P, 2 * D], F16)
            bias_lhs = sb("bias_lhs", [P, P], F16)
            row01 = sb("row01", [P, 1], F32)
            wq = sb("wq", [P, 2, DC, D], F16)
            wkv = sb("wkv", [P, 2, DC, 2 * D], F16)
            wg = sb("wg", [P, 2, DC, E], F16)
            woT = sb("woT", [P, DC, D], F32)
            bqT = sb("bqT", [P, DC], F32)
            bo_row = sb("bo_row", [1, D], F32)
            bo_all = sb("bo_all", [P, D], F32)
            wmax = sb("wmax", [P, 5], F32)
            wmax_all = sb("wmax_all", [P, 5], F32)
            wpow = sb("wpow", [P, 3], F32)
            wsc = sb("wsc", [P, 3], F32)
            wrec = sb("wrec", [P, 3], F32)
            winv = sb("winv", [P, 3], F32)
            winv_neg = sb("winv_neg", [P, 3], F32)
            head_mask = sb("head_mask", [P, P], F32)
            ek = sb("ek", [P, 2, D], F32)
            phik = sb("phik", [P, 2, D], F32)
            kv1 = sb("kv1", [P, 2, 2 * DC, P + 1], F32)
            eq = sb("eq", [P, 2, HALF * P], F32)
            qraw = sb("qraw", [P, 2, HALF * P], F32)
            gsub = sb("gsub", [P, 2, HALF, E], F32)
            gexp = sb("gexp", [P, 2, HALF, E], F32)
            gmax = sb("gmax", [P, 2, HALF], F32)
            gsum = sb("gsum", [P, 2, HALF], F32)
            grec = sb("grec", [P, 2, HALF], F32)
            probs = sb("probs", [P, NT, NE], F32)
            kvs = sb("kvs", [P, DC, P + 1], F32)
            kvm = sb("kvm", [P, DC, P], F32)
            ksz = sb("ksz", [P, DC, CENTRE + P], F32)
            spread = sb("spread", [P, NT, DC, P], BF16)
            kvT = sb("kvT", [P, DC, P], F32)
            mo = sb("mo", [P, DC, D], F32)
            qz = [sb(f"qz{h}", [P, DC, HALF * P], F32) for h in range(2)]
            dd = sb("dd", [P, P], F32)
            zz = sb("zz", [P, P], F32)
            zrest = sb("zrest", [P, P], F32)
            zpart = sb("zpart", [P, 3, P], BF16)
            zeros = sb("zeros", [P, D], F32)
            wpiece = sb("wpiece", [P, 2, 1024], F32)
            piece_max = sb("piece_max", [P, 2, 16], F32)
            ewmax = sb("ewmax", [P, 2, E], F32)
            ewall = sb("ewall", [P, 2, E], F32)
            ewpow = sb("ewpow", [P, 2, E], F32)
            ewrec = sb("ewrec", [P, 2, E], F32)
            rows = wpiece[0:NE, 0, :]
            topv = wpiece[0:NE, 1, 0:CAP]
            topi = wpiece[0:NE, 1, CAP:2 * CAP]
            top8 = sb("top8", [NE, TOP], F32)
            at8 = sb("at8", [NE, TOP], U32)
            rowno = sb("rowno", [NE, 1], I32)
            rowbase = sb("rowbase", [NE, 1], I32)
            rowoff = sb("rowoff", [NE, 1], F32)

            pT = ps("pT", [P, 2, DC, P], F16)
            pP = [ps(f"pP{i}", [P, 512]) for i in range(2)]
            pG = ps("pG", [P, 2, HALF, 64])
            pKV = ps("pKV", [P, 512])
            pQ = ps("pQ", [P, 512])
            pD = ps("pD", [P, 512])
            pO = ps("pO", [P, 2, D])
            banks_z, banks_o, banks_mo = {True: [pD], False: [pD, pKV]}, {True: [pO], False: [pO, pG]}, {True: pD, False: pP[0]}

            banks_q = {True: [pQ, pQ, pQ, pD], False: [pQ, pD, pQ, pD]}

            def pair(bank):
                return (bank[:, :, :, :].rearrange("p a b c -> p (a b c)") if bank is pG else
                        bank[:, :, :].rearrange("p a d -> p (a d)")).rearrange("p (i d) -> p i d", i=2)

            consts = event("consts")
            w_in = event("w_in", step=16)
            wprep = event("wprep")
            wfold = event("wfold")
            wturn = event("wturn")
            whi = event("whi")
            x_in = event("x_in", step=16)
            x2_in = event("x2_in", step=16)
            zero_out = event("zero_out", step=16)
            stat_done = event("stat_done")
            aggr_done = event("aggr_done")
            veps_done = event("veps_done", credit=1)
            rpow_done = event("rpow_done")
            rstd_done = event("rstd_done", credit=1)
            xm_done = event("xm_done", per=NT, credit=1)
            hi_done = event("hi_done", per=NT)
            lo_done = event("lo_done", per=NT)
            row_out = [event(f"row_out{h}", step=16, credit=1) for h in range(2)]
            turned = event("turned", per=NT, credit=HALF + 1)
            xT_done = event("xT_done", per=NT, credit=1)
            proj = event("proj", per=NT)
            gated = event("gated", per=2)
            kv_done = event("kv_done", per=NT, credit=2)
            kneg_done = event("kneg_done", per=NT)
            ek_done = event("ek_done", per=NT)
            k_done = event("k_done", per=NT, credit=2)
            kv_used = event("kv_used", per=NT, credit=2)
            kv_out = event("kv_out", credit=1)
            gmax_done = event("gmax_done", per=2)
            gsub_done = event("gsub_done", per=2, credit=1)
            gexp_done = event("gexp_done", per=2)
            gsum_done = event("gsum_done", per=2)
            grec_done = event("grec_done", per=2)
            prob_done = event("prob_done", per=2)
            q_proj = event("q_proj", per=4, credit=3)
            qneg_done = event("qneg_done", per=4)
            qraw_done = event("qraw_done", per=4, credit=2)
            eq_done = event("eq_done", per=4)
            q_done = event("q_done", per=4, credit=2)
            bo_done = event("bo_done", per=4)
            kvs_done = event("kvs_done")
            kvm_done = event("kvm_done", per=4)
            kv_turned = event("kv_turned", credit=1)
            kvT_done = event("kvT_done")
            mo_mm = event("mo_mm")
            mo_done = event("mo_done")
            den = event("den", credit=1)
            shifted = event("shifted", credit=1)
            inverted = event("inverted")
            zsplit = event("zsplit", per=4)
            bcast = event("bcast", per=4)
            qz_done = event("qz_done", per=4, credit=1)
            z_out = event("z_out", per=4, credit=2)
            o_out = event("o_out", per=4, credit=2)
            out_mm = event("out_mm", per=4)
            mix_done = event("mix_done", per=4, credit=1)
            mix_out = [event(f"mix_out{h}", step=16, credit=1) for h in range(2)]
            piece_in = [event(f"piece_in{i}", per=PIECES // 2, step=16) for i in range(2)]
            piece_done = [event(f"piece_done{i}", per=PIECES // 2, credit=1) for i in range(2)]
            p_turned = event("p_turned")
            rows_done = event("rows_done")
            found = event("found", per=1)
            taken = event("taken", per=1)
            kept = event("kept", per=1)
            sc_step = event("sc_step")
            sc_fold = event("sc_fold")
            pick_turned = event("pick_turned")
            picks_done = event("picks_done")

            segments = [(0, LAG, True, False, True), (LAG, NB - 1, True, True, True),
                        (NB - 1, NB, True, True, False), (NB, NB + LAG, False, True, False)]

            block = ctx.enter_context(nc.Block())

            @block.sync
            def _(sp):
                for i, w in enumerate((Wq, Wk, Wv, Wo)):
                    sp.dma_start(wraw[:, i, :, :], w.rearrange("(c p) d -> p c d", p=P)).then_inc(w_in, 16)
                sp.dma_start(graw[:, :, :], gate_w.rearrange("(c p) e -> p c e", p=P)).then_inc(w_in, 16)
                value = held(sp, at(consts, 0, 0))
                sp.wait_ge(consts, 1)
                sp.wait_ge(consts, value)
                for r in range(2):
                    sp.dma_start(bias_raw[r:r + 1, 0:D], bk.rearrange("(a n) -> a n", a=1)).then_inc(w_in, 16)
                    sp.dma_start(bias_raw[r:r + 1, D:2 * D], bv.rearrange("(a n) -> a n", a=1)).then_inc(w_in, 16)
                sp.dma_start(bo_row[:, :], bo.rearrange("(a n) -> a n", a=1)).then_inc(w_in, 16)
                for c in range(DC):
                    sp.dma_start(bqT[:, c:c + 1], bq[c * P:(c + 1) * P].rearrange("(p a) -> p a", a=1)).then_inc(w_in, 16)
                sp.dma_start(xring[:, 0, :, :], x_rows[0]).then_inc(x_in, 16)
                value = held(sp, at(x_in, 0))
                sp.wait_ge(consts, 1)
                sp.wait_ge(x_in, value)
                sp.dma_start(xring[:, 1, :, :], x_rows[1]).then_inc(x_in, 16)
                sp.dma_start(x2ring[:, 0, :, :], x_rows[0]).then_inc(x2_in, 16)
                value = held(sp, at(consts, 0, 1))
                sp.wait_ge(consts, 1)
                sp.wait_ge(consts, value)
                sp.wait_ge(wprep, at(wprep, 0, 18))
                sp.wait_ge(wturn, at(wturn, 0, 3))

                def pieces(n, which):
                    for q in which:
                        i = q % 2
                        piece = n * (PIECES // 2) + q // 2
                        value = held(sp, at(piece_done[i], n, q // 2 - 1))
                        sp.wait_ge(consts, 1)
                        sp.wait_ge(piece_done[i], value)
                        if i == 0:
                            dst, src = wpiece[:, 0, :], w1_rows[ds(piece * P, P), :]
                        else:
                            dst = wpiece[:, 1, :].rearrange("p (r d) -> p r d", r=4)
                            src = w2_rows[ds(piece * (4 * P), 4 * P), :].rearrange("(r p) d -> p r d", p=P)
                        sp.dma_start(dst, src).then_inc(piece_in[i], 16)

                def body(n, s1, s2, load, load2):
                    if s1:
                        pieces(n, range(min(2, PIECES)))
                    if load:
                        value = held(sp, at(x_in, n, 1))
                        sp.wait_ge(consts, 1)
                        sp.wait_ge(x_in, value)
                        value = held(sp, at(xm_done, n, -1))
                        sp.wait_ge(consts, 1)
                        sp.wait_ge(xm_done, value)
                        sp.dma_start(xring[:, (n + 2) % XR, :, :], x_rows[ds(n + 2, 1)].rearrange("o p j d -> p (o j) d")).then_inc(x_in, 16)
                    if s1:
                        for h in range(2):
                            value = held(sp, at(lo_done, n, (h + 1) * HALF - 1))
                            sp.wait_ge(consts, 1)
                            sp.wait_ge(lo_done, value)
                            value = held(sp, at(row_out[h], n, -1))
                            sp.wait_ge(consts, 1)
                            sp.wait_ge(row_out[h], value)
                            sp.dma_start(
                                table_rows[ds(n, 1), :, h * HALF:(h + 1) * HALF, :].rearrange("o p j d -> p (o j) d"),
                                xhl[h][:, :, :, :, :].rearrange("p j a c t -> p j (a c t)")).then_inc(row_out[h], 16)
                        pieces(n, range(2, PIECES))
                        sp.dma_start(
                            acc_rows[ds(n, 1)].rearrange("o p j d -> p (o j) d"),
                            zeros[:, :].unsqueeze(1).to_broadcast([P, NT, D])).then_inc(zero_out, 16)
                    if load2:
                        value = held(sp, at(x2_in, n - LAG))
                        sp.wait_ge(consts, 1)
                        sp.wait_ge(x2_in, value)
                        for h in range(2):
                            value = held(sp, at(mix_out[h], n - LAG, -1))
                            sp.wait_ge(consts, 1)
                            sp.wait_ge(mix_out[h], value)
                        sp.dma_start(x2ring[:, ds((n - LAG + 1) % 2, 1), :, :].rearrange("p o j d -> p (o j) d"),
                                     x_rows[ds(n - LAG + 1, 1)].rearrange("o p j d -> p (o j) d")).then_inc(x2_in, 16)
                    if s2:
                        for h in range(2):
                            value = held(sp, at(mix_done, n - LAG, 2 * h + 1))
                            sp.wait_ge(consts, 1)
                            sp.wait_ge(mix_done, value)
                            value = held(sp, at(mix_out[h], n - LAG, -1))
                            sp.wait_ge(consts, 1)
                            sp.wait_ge(mix_out[h], value)
                            sp.dma_start(
                                mix_rows[ds(n - LAG, 1), :, h * HALF:(h + 1) * HALF, :].rearrange("o p j d -> p (o j) d"),
                                x2ring[:, ds((n - LAG) % 2, 1), h * HALF:(h + 1) * HALF, :].rearrange("p o j d -> p (o j) d")).then_inc(mix_out[h], 16)

                for lo, hi, s1, s2, load, load2 in [
                        (0, LAG, True, False, True, False), (LAG, NB - 2, True, True, True, True),
                        (NB - 2, NB, True, True, False, True), (NB, NB + LAG - 1, False, True, False, True),
                        (NB + LAG - 1, NB + LAG, False, True, False, False)]:
                    if hi - lo == 1:
                        body(lo, s1, s2, load, load2)
                    elif hi > lo:
                        with sp.Fori(lo, hi) as n:
                            body(n, s1, s2, load, load2)
                value = held(sp, at(zero_out, NB - 1))
                sp.wait_ge(consts, 1)
                sp.wait_ge(zero_out, value)
                for h in range(2):
                    value = held(sp, at(row_out[h], NB - 1))
                    sp.wait_ge(consts, 1)
                    sp.wait_ge(row_out[h], value)
                    value = held(sp, at(mix_out[h], NB - 1))
                    sp.wait_ge(consts, 1)
                    sp.wait_ge(mix_out[h], value)

            @block.gpsimd
            def _(pool):
                g = nc.gpsimd
                for ev in (*row_out, *mix_out, *piece_done, xm_done, veps_done, rstd_done, turned, xT_done, kv_done, k_done, kv_used,
                           kv_out, gsub_done, q_proj, qraw_done, q_done, shifted, den, kv_turned, qz_done, z_out, o_out, mix_done):
                    pool.sem_inc(ev, credit(ev))
                g.memset(bias_raw[:, :], 0.0).then_inc(consts, 1)
                g.memset(zeros[:, :], 0.0).then_inc(consts, 1)
                g.memset(ident[:, :], 0.0).then_inc(consts, 1)
                g.memset(ident16[:, :], 0.0).then_inc(consts, 1)
                g.memset(head_mask[:, :], 1.0).then_inc(consts, 1)
                g.memset(minus_half[:, :], -0.5).then_inc(consts, 1)
                g.iota(rowno[:, :], pattern=[[0, 1]], base=0, channel_multiplier=1).then_inc(consts, 1)
                g.memset(kv1[:, :, :, :], 1.0).then_inc(consts, 1)
                g.memset(ksz[:, :, :], 0.0)
                g.memset(wmax[:, :], 0.0).then_inc(consts, 1)
                pool.wait_ge(consts, at(consts, 0, 8))
                for m in (ident, ident16):
                    g.affine_select(out=m[:, :], in_=m[:, :], compare_op=ALU.not_equal, fill=1.0,
                                              base=0, pattern=[[-1, P]], channel_multiplier=1).then_inc(consts, 1)
                blocks = head_mask[:, :].rearrange("p (b i) -> p b i", i=HD)
                g.affine_select(out=blocks, in_=blocks, compare_op=ALU.is_ge, fill=0.0,
                                          base=0, pattern=[[-HD, P // HD], [0, HD]], channel_multiplier=1).then_inc(consts, 1)
                pool.wait_ge(consts, at(consts, 0, 11))
                g.affine_select(out=blocks, in_=blocks, compare_op=ALU.is_ge, fill=0.0,
                                          base=HD - 1, pattern=[[HD, P // HD], [0, HD]], channel_multiplier=-1).then_inc(consts, 1)
                pool.wait_ge(consts, at(consts, 0, 12))
                pool.wait_ge(w_in, at(w_in, 0, 11))
                g.partition_broadcast(bo_all[:, :], bo_row[:, :], P).then_inc(consts, 1)
                pool.wait_ge(wprep, at(wprep, 0, 2))
                g.partition_all_reduce(wmax_all[:, :], wmax[:, :], P, bass.bass_isa.ReduceOp.max).then_inc(wfold, 1)

                def norm(n):
                    value = held(pool, at(aggr_done, n))
                    pool.wait_ge(consts, 1)
                    pool.wait_ge(aggr_done, value)
                    g.tensor_scalar(veps[:, :], moments[:, :, 1], 1e-5, None, ALU.add).then_inc(veps_done, 1)
                    pool.wait_ge(veps_done, at(veps_done, n))
                    pool.wait_ge(rstd_done, at(rstd_done, n, -1))
                    g.tensor_tensor(rpow[:, :], veps[:, :], minus_half[:, :], ALU.pow).then_inc(rpow_done, 1)

                norm(0)
                g.tensor_copy(spread[:, :, :, :].rearrange("p j c (b i) -> p (j c b) i", i=HD),
                              ident[:, :].unsqueeze(2).to_broadcast([P, P, HD])).then_inc(consts, 1)

                def blocks_of(m):
                    pool.wait_ge(kv_out, at(kv_out, m))
                    pool.wait_ge(den, at(den, m, -1))
                    pool.wait_ge(kv_turned, at(kv_turned, m, -1))
                    g.tensor_copy(kvs[:, :, :], kvring[:, ds(m % QR, 1), :, :].rearrange("p o c t -> p (o c) t")).then_inc(kvs_done, 1)
                    value = held(pool, at(kvs_done, m))
                    pool.wait_ge(consts, 1)
                    pool.wait_ge(kvs_done, value)
                    for c in range(DC):
                        g.tensor_tensor(kvm[:, c, :], kvs[:, c, 0:P], head_mask[:, :], ALU.mult).then_inc(kvm_done, 1)
                        first = CENTRE + c * (P // HD)
                        g.tensor_scalar(ksz[:, c, first:first + P // HD], head_mask[:, :].rearrange("p (b i) -> p b i", i=HD)[:, :, 0],
                                        kvs[:, c, P:P + 1], None, ALU.mult).then_inc(kvm_done, 1)

                def add_bo(m, u):
                    pool.wait_ge(x2_in, at(x2_in, m))
                    tiles = x2ring[:, ds(m % 2, 1), 2 * u:2 * u + 2, :].rearrange("p o j d -> p (o j) d")
                    g.tensor_tensor(tiles, tiles, bo_all[:, :].unsqueeze(1).to_broadcast([P, 2, D]), ALU.add).then_inc(bo_done, 1)

                def divide(m, u):
                    h, c = divmod(u, DC)
                    value = held(pool, at(z_out, m - (NB - LAG), u))
                    q = qring[:, ds(m % QR, 1), c, h * HALF * P:(h + 1) * HALF * P].rearrange("p o t -> p (o t)")
                    pool.wait_ge(consts, 1)
                    pool.wait_ge(z_out, value)
                    g.tensor_tensor(qz[h][:, c, :], q, eq[:, u % 2, :], ALU.mult).then_inc(qz_done, 1)

                def add_x(m, u):
                    values = [(ev, held(pool, v)) for ev, v in ((bo_done, at(bo_done, m, u)), (o_out, at(o_out, m - (NB - LAG), u)))]
                    tiles = x2ring[:, ds(m % 2, 1), 2 * u:2 * u + 2, :].rearrange("p o j d -> p (o j) d")
                    pool.wait_ge(consts, 1)
                    for ev, value in values:
                        pool.wait_ge(ev, value)
                    g.tensor_tensor(tiles, tiles, qraw[:, u % 2, :].rearrange("p (i d) -> p i d", i=2), ALU.add).then_inc(mix_done, 1)

                def body(n, s1, s2, nxt):
                    m = n - LAG
                    if s2 and s1:
                        blocks_of(m)
                    if s2:
                        for u in range(4):
                            add_bo(m, u)
                    if nxt:
                        norm(n + 1)
                    if s2 and not s1:
                        for u in range(4):
                            divide(m, u)

                for lo, hi, s1, s2, nxt, more in [(0, LAG, True, False, True, False), (LAG, NB - 1, True, True, True, False),
                                                  (NB - 1, NB, True, True, False, True), (NB, NB + LAG - 1, False, True, False, True),
                                                  (NB + LAG - 1, NB + LAG, False, True, False, False)]:
                    def step(n):
                        body(n, s1, s2, nxt)
                        if more:
                            blocks_of(n - LAG + 1)
                        if s2 and not s1:
                            for u in range(4):
                                add_x(n - LAG, u)

                    if hi - lo == 1:
                        step(lo)
                    elif hi > lo:
                        with pool.Fori(lo, hi) as n:
                            step(n)
                pool.wait_ge(sc_step, at(sc_step, 0, 0))
                g.partition_all_reduce(ewall[:, :, :].rearrange("p a e -> p (a e)"),
                                                  ewmax[:, :, :].rearrange("p a e -> p (a e)"), P,
                                                  bass.bass_isa.ReduceOp.max).then_inc(sc_fold, 1)

            @block.scalar
            def _(act):
                a = nc.scalar
                act.wait_ge(wprep, at(wprep, 0, 8))
                for i, (src, dst) in enumerate(((pP[0], wq[:, 0, :, :]), (pP[1], wkv[:, 0, :, 0:D]), (pQ, wkv[:, 0, :, D:2 * D]))):
                    act.wait_ge(wturn, at(wturn, 0, i))
                    a.activation(dst, src[:, :].rearrange("p (c e) -> p c e", c=DC), ACT.Copy,
                                        scale=wsc[:, (0, 2, 2)[i]:(0, 2, 2)[i] + 1]).then_inc(whi, 1)
                a.activation(wg[:, 0, :, :], graw[:, :, :], ACT.Copy, scale=wsc[:, 1:2]).then_inc(whi, 1)
                act.wait_ge(wturn, at(wturn, 0, 3))
                a.activation(woT[:, :, :], pD[:, :].rearrange("p (c e) -> p c e", c=DC), ACT.Copy).then_inc(whi, 1)

                def high(n, j):
                    h, jj = divmod(j, HALF)
                    act.wait_ge(xm_done, at(xm_done, n, j))
                    if jj == 0:
                        act.wait_ge(row_out[h], at(row_out[h], n, -1))
                        act.wait_ge(turned, at(turned, n, j + HALF - 1 - NT))
                    a.activation(xhl[h][:, jj, 0, :, :].rearrange("p c t -> p (c t)"), xm[:, j % 2, :], ACT.Copy,
                                            scale=rstd[:, j:j + 1]).then_inc(hi_done, 1)

                def turn_out(n, j):
                    h, jj = divmod(j, HALF)
                    act.wait_ge(turned, at(turned, n, j))
                    if jj == 0:
                        act.wait_ge(q_proj, at(q_proj, n, 2 * h + 1 - 4))
                    a.activation(xT[h][:, :, :, jj * P:(jj + 1) * P], pT[:, :, :, :], ACT.Copy).then_inc(xT_done, 1)

                def q_out(n, u, mixed):
                    c = u % DC
                    act.wait_ge(q_proj, at(q_proj, n, u))
                    act.wait_ge(q_done, at(q_done, n, u - 2))
                    a.activation(qraw[:, u % 2, :], banks_q[mixed][u][:, :], ACT.Identity, scale=winv[:, 0:1], bias=bqT[:, c:c + 1]).then_inc(qraw_done, 1)

                def q_exp(n, u):
                    act.wait_ge(qneg_done, at(qneg_done, n, u))
                    a.activation(eq[:, u % 2, :], eq[:, u % 2, :], ACT.Exp, scale=-1.0).then_inc(eq_done, 1)

                def gate_exp(n, h):
                    act.wait_ge(gsub_done, at(gsub_done, n, h))
                    a.activation(gexp[:, h, :, :], gsub[:, h, :, :], ACT.Exp, scale=winv[:, 1:2]).then_inc(gexp_done, 1)

                act.wait_ge(consts, at(consts, 0, 9))
                act.wait_ge(rstd_done, at(rstd_done, 0))
                for j in range(HALF):
                    high(0, j)
                turn_out(0, 0)

                def body(n, s1, s2, nxt):
                    m = n - LAG
                    for j in range(NT):
                        if s1:
                            if j < NT - 1:
                                turn_out(n, j + 1)
                            elif nxt:
                                turn_out(n + 1, 0)
                            if j < HALF:
                                high(n, j + HALF)
                            elif nxt and j > HALF:
                                high(n + 1, j - HALF)
                            if j in (5, 6):
                                q_out(n, j - 5, s2)
                            act.wait_ge(proj, at(proj, n, j))
                            act.wait_ge(k_done, at(k_done, n, j - 2))
                            a.activation(ek[:, j % 2, :], pP[j % 2][:, 0:D], ACT.Relu, scale=winv_neg[:, 2:3]).then_inc(kneg_done, 1)
                            act.wait_ge(kv_used, at(kv_used, n, j - 2))
                            a.activation(kv1[:, j % 2, :, 0:P], pP[j % 2][:, :].rearrange("p (c t) -> p c t", c=2 * DC),
                                                   ACT.Copy, scale=winv[:, 2:3]).then_inc(kv_done, 1)
                            if j in (5, 6):
                                if j == 5:
                                    gate_exp(n, 0)
                                q_exp(n, j - 5)
                            act.wait_ge(kneg_done, at(kneg_done, n, j))
                            a.activation(ek[:, j % 2, :], ek[:, j % 2, :], ACT.Exp, scale=-1.0).then_inc(ek_done, 1)
                        if nxt and j == HALF:
                            act.wait_ge(rstd_done, at(rstd_done, n, 1))
                            high(n + 1, 0)
                        if s2 and j == 2:
                            act.wait_ge(mo_mm, at(mo_mm, m))
                            a.activation(mo[:, :, :].rearrange("p c d -> p (c d)"), banks_mo[s1][:, :], ACT.Copy).then_inc(mo_done, 1)
                    if s1:
                        q_out(n, 2, s2)
                        q_out(n, 3, s2)
                        gate_exp(n, 1)
                        q_exp(n, 2)
                        q_exp(n, 3)

                def copy_z(m, w, u):
                    act.wait_ge(bcast, at(bcast, m, u))
                    act.wait_ge(qz_done, at(qz_done, m, u - 2))
                    a.activation(eq[:, u % 2, :], banks_z[False][u % 2][:, :], ACT.Copy).then_inc(z_out, 1)

                def copy_o(m, w, u):
                    act.wait_ge(out_mm, at(out_mm, m, u))
                    act.wait_ge(mix_done, at(mix_done, m, u - 2))
                    a.activation(qraw[:, u % 2, :].rearrange("p (i d) -> p i d", i=2), pair(banks_o[False][u % 2]), ACT.Copy).then_inc(o_out, 1)

                def body2(n):
                    m = n - LAG
                    act.wait_ge(mo_mm, at(mo_mm, m))
                    a.activation(mo[:, :, :].rearrange("p c d -> p (c d)"), banks_mo[False][:, :], ACT.Copy).then_inc(mo_done, 1)
                    for u in range(4):
                        copy_z(m, n - NB, u)
                    for u in range(4):
                        copy_o(m, n - NB, u)

                for lo, hi, s1, s2, nxt in segments:
                    if not s1:
                        act.wait_ge(q_done, at(q_done, NB - 1, 3))
                        with act.Fori(lo, hi) as n:
                            body2(n)
                    elif hi - lo == 1:
                        body(lo, s1, s2, nxt)
                    else:
                        with act.Fori(lo, hi) as n:
                            body(n, s1, s2, nxt)

            @block.vector
            def _(dve):
                v = nc.vector
                def tile_of(n, j):
                    return xring[:, ds(n % XR, 1), j, :].rearrange("p o d -> p (o d)")

                def stats_of(n, j):
                    if j == 0:
                        dve.wait_ge(x_in, at(x_in, n))
                    last = v.bn_stats(stats[:, j, :], tile_of(n, j))
                    if j == NT - 1:
                        last.then_inc(stat_done, 1)

                def moments_of(n):
                    value = held(dve, at(veps_done, n, -1))
                    dve.wait_ge(consts, 1)
                    dve.wait_ge(veps_done, value)
                    if not (isinstance(n, int) and n == 0):
                        value = held(dve, at(xm_done, n, -1))
                        dve.wait_ge(consts, 1)
                        dve.wait_ge(xm_done, value)
                    value = held(dve, at(stat_done, n))
                    dve.wait_ge(consts, 1)
                    dve.wait_ge(stat_done, value)
                    for j in range(NT):
                        last = v.bn_aggr(moments[:, j, :], stats[:, j, :])
                    last.then_inc(aggr_done, 1)

                dve.wait_ge(w_in, at(w_in, 0, 11))
                dve.wait_ge(consts, at(consts, 0, 12))
                for col, src in ((0, wraw[:, 0, :, :]), (2, wraw[:, 1, :, :]), (3, wraw[:, 2, :, :])):
                    v.tensor_reduce(wmax[:, col:col + 1], src, AX.XY, ALU.max, apply_absolute_value=True)
                v.tensor_reduce(wmax[:, 1:2], graw[:, :, :], AX.XY, ALU.max, apply_absolute_value=True).then_inc(wprep, 1)
                v.tensor_reduce(wmax[:, 4:5], bias_raw[:, :], AX.X, ALU.max, apply_absolute_value=True).then_inc(wprep, 1)
                v.tensor_tensor(row01[:, :], ident[:, 0:1], ident[:, 1:2], ALU.add).then_inc(wprep, 1)
                v.memset(bias_lhs[:, :], XSCALE).then_inc(wprep, 1)
                dve.wait_ge(wfold, at(wfold, 0))
                v.tensor_copy(wpow[:, 0:2], wmax_all[:, 0:2])
                v.tensor_reduce(wpow[:, 2:3], wmax_all[:, 2:5], AX.X, ALU.max).then_inc(wprep, 1)
                dve.wait_ge(wprep, at(wprep, 0, 4))
                v.tensor_scalar(wpow[:, :], wpow[:, :], 2.0 ** -60, None, ALU.max).then_inc(wprep, 1)
                dve.wait_ge(wprep, at(wprep, 0, 5))
                bits = wpow[:, :].bitcast(U32)
                v.tensor_scalar(bits, bits, EXP_MASK, None, ALU.bitwise_and).then_inc(wprep, 1)
                dve.wait_ge(wprep, at(wprep, 0, 6))
                v.reciprocal(wrec[:, :], wpow[:, :]).then_inc(wprep, 1)
                dve.wait_ge(wprep, at(wprep, 0, 7))
                v.tensor_scalar(wsc[:, :], wrec[:, :], 2.0 ** 14, None, ALU.mult).then_inc(wprep, 1)
                v.tensor_scalar(winv_neg[:, :], wpow[:, :], -2.0 ** -14 / XSCALE, None, ALU.mult)
                v.tensor_scalar(winv[:, :], wpow[:, :], 2.0 ** -14 / XSCALE, None, ALU.mult).then_inc(wprep, 1)
                dve.wait_ge(wprep, at(wprep, 0, 9))
                for i, (src, s, hi, lo) in enumerate((
                        (pP[0], 0, wq[:, 0, :, :], wq[:, 1, :, :]),
                        (pP[1], 2, wkv[:, 0, :, 0:D], wkv[:, 1, :, 0:D]),
                        (pQ, 2, wkv[:, 0, :, D:2 * D], wkv[:, 1, :, D:2 * D]),
                        (None, 1, wg[:, 0, :, :], wg[:, 1, :, :]))):
                    full = graw[:, :, :] if src is None else src[:, :].rearrange("p (c e) -> p c e", c=DC)
                    dve.wait_ge(whi, at(whi, 0, i))
                    v.scalar_tensor_tensor(out=lo, in0=full, scalar=wsc[:, s:s + 1], in1=hi,
                                                    op0=ALU.mult, op1=ALU.subtract).then_inc(wprep, 1)
                for j in range(NT):
                    stats_of(0, j)
                moments_of(0)
                v.tensor_scalar(bias_hi[:, :], bias_raw[:, :], wsc[:, 2:3], None, ALU.mult).then_inc(wprep, 1)
                dve.wait_ge(wprep, at(wprep, 0, 14))
                v.scalar_tensor_tensor(out=bias_tmp[:, :], in0=bias_raw[:, :], scalar=wsc[:, 2:3],
                                                in1=bias_hi[:, :], op0=ALU.mult, op1=ALU.subtract).then_inc(wprep, 1)
                dve.wait_ge(wprep, at(wprep, 0, 15))
                v.tensor_scalar(bias_tmp[:, :], bias_tmp[:, :], ident[:, 1:2], None, ALU.mult).then_inc(wprep, 1)
                dve.wait_ge(wprep, at(wprep, 0, 16))
                v.scalar_tensor_tensor(out=bias_rows[:, :], in0=bias_hi[:, :], scalar=ident[:, 0:1],
                                                in1=bias_tmp[:, :], op0=ALU.mult, op1=ALU.add).then_inc(wprep, 1)
                v.tensor_scalar(bias_lhs[:, :], bias_lhs[:, :], row01[:, 0:1], None, ALU.mult).then_inc(wprep, 1)

                def root_of(n):
                    if not (isinstance(n, int) and n == 0):
                        dve.wait_ge(lo_done, at(lo_done, n, -1))
                    dve.wait_ge(rpow_done, at(rpow_done, n))
                    v.tensor_scalar(rstd[:, :], rpow[:, :], XSCALE, None, ALU.mult).then_inc(rstd_done, 1)

                def centre(n, j):
                    if j == 0:
                        dve.wait_ge(aggr_done, at(aggr_done, n))
                    if j >= 2:
                        dve.wait_ge(lo_done, at(lo_done, n, j - 2))
                    v.tensor_scalar(xm[:, j % 2, :], tile_of(n, j), moments[:, j, 0:1], None, ALU.subtract).then_inc(xm_done, 1)

                def low(n, j):
                    h, jj = divmod(j, HALF)
                    if j == 0:
                        dve.wait_ge(rstd_done, at(rstd_done, n))
                    dve.wait_ge(hi_done, at(hi_done, n, j))
                    v.scalar_tensor_tensor(
                        out=xhl[h][:, jj, 1, :, :].rearrange("p c t -> p (c t)"), in0=xm[:, j % 2, :],
                        scalar=rstd[:, j:j + 1], in1=xhl[h][:, jj, 0, :, :].rearrange("p c t -> p (c t)"),
                        op0=ALU.mult, op1=ALU.subtract).then_inc(lo_done, 1)

                def gate_max(n, h):
                    dve.wait_ge(gated, at(gated, n, h))
                    v.tensor_reduce(gmax[:, h, :], pG[:, h, :, 0:E], AX.X, ALU.max).then_inc(gmax_done, 1)
                    dve.wait_ge(gmax_done, at(gmax_done, n, h))
                    v.tensor_tensor(gsub[:, h, :, :], pG[:, h, :, 0:E],
                                                 gmax[:, h, :].unsqueeze(2).to_broadcast([P, HALF, E]), ALU.subtract).then_inc(gsub_done, 1)

                def gate_probs(n, h):
                    dve.wait_ge(gexp_done, at(gexp_done, n, h))
                    v.tensor_reduce(gsum[:, h, :], gexp[:, h, :, :], AX.X, ALU.add).then_inc(gsum_done, 1)
                    dve.wait_ge(gsum_done, at(gsum_done, n, h))
                    v.reciprocal(grec[:, h, :], gsum[:, h, :]).then_inc(grec_done, 1)
                    dve.wait_ge(grec_done, at(grec_done, n, h))
                    v.tensor_tensor(probs[:, h * HALF:(h + 1) * HALF, ds(n * E, E)], gexp[:, h, :, :],
                                                 grec[:, h, :].unsqueeze(2).to_broadcast([P, HALF, E]), ALU.mult).then_inc(prob_done, 1)

                def q_negative(n, u):
                    dve.wait_ge(qraw_done, at(qraw_done, n, u))
                    v.tensor_scalar(eq[:, u % 2, :], qraw[:, u % 2, :], -1.0, 0.0, ALU.mult, ALU.max).then_inc(qneg_done, 1)

                def q_feature(n, u):
                    h, c = divmod(u, DC)
                    dve.wait_ge(qraw_done, at(qraw_done, n, u))
                    dve.wait_ge(eq_done, at(eq_done, n, u))
                    v.scalar_tensor_tensor(
                        out=qring[:, ds(n % QR, 1), c, h * HALF * P:(h + 1) * HALF * P].rearrange("p o t -> p (o t)"),
                        in0=qraw[:, u % 2, :], scalar=0.0, in1=eq[:, u % 2, :], op0=ALU.max, op1=ALU.add).then_inc(q_done, 1)

                def shift(m):
                    dve.wait_ge(den, at(den, m))
                    v.tensor_scalar(dd[:, :], pQ[:, 0:P], 1e-6, None, ALU.add).then_inc(shifted, 1)

                def invert(m):
                    dve.wait_ge(shifted, at(shifted, m))
                    v.reciprocal(zz[:, :], dd[:, :]).then_inc(inverted, 1)
                    dve.wait_ge(inverted, at(inverted, m))
                    v.tensor_copy(zpart[:, 0, :], zz[:, :]).then_inc(zsplit, 1)

                def split_rest(m):
                    dve.wait_ge(zsplit, at(zsplit, m, 0))
                    v.tensor_tensor(zrest[:, :], zz[:, :], zpart[:, 0, :], ALU.subtract).then_inc(zsplit, 1)
                    dve.wait_ge(zsplit, at(zsplit, m, 1))
                    v.tensor_copy(zpart[:, 1, :], zrest[:, :]).then_inc(zsplit, 1)
                    dve.wait_ge(zsplit, at(zsplit, m, 2))
                    v.tensor_tensor(zpart[:, 2, :], zrest[:, :], zpart[:, 1, :], ALU.subtract).then_inc(zsplit, 1)

                def divide(m, u):
                    h, c = divmod(u, DC)
                    q = qring[:, ds(m % QR, 1), c, h * HALF * P:(h + 1) * HALF * P].rearrange("p o t -> p (o t)")
                    dve.wait_ge(bcast, at(bcast, m, u))
                    v.tensor_tensor(qz[h][:, c, :], q, pD[:, :], ALU.mult).then_inc(qz_done, 1)

                def add_x(m, u):
                    dve.wait_ge(bo_done, at(bo_done, m, u))
                    dve.wait_ge(out_mm, at(out_mm, m, u))
                    tiles = x2ring[:, ds(m % 2, 1), 2 * u:2 * u + 2, :].rearrange("p o j d -> p (o j) d")
                    v.tensor_tensor(tiles, tiles, pO[:, :, :], ALU.add).then_inc(mix_done, 1)

                def piece(n, q):
                    i = q % 2
                    dve.wait_ge(piece_in[i], at(piece_in[i], n, q // 2))
                    v.tensor_reduce(piece_max[:, i, ds(n * (PIECES // 2) + q // 2, 1)], wpiece[:, i, :],
                                                     AX.X, ALU.max, apply_absolute_value=True).then_inc(piece_done[i], 1)

                def top_round(r):
                    v.max(top8[:, :], rows[:, :]).then_inc(found, 1)
                    dve.wait_ge(found, at(found, r))
                    v.tensor_copy(topv[:, ds(r * TOP, TOP)], top8[:, :])
                    v.max_index(at8[:, :], top8[:, :], rows[:, :])
                    v.match_replace(rows[:, :], top8[:, :], rows[:, :], -1.0).then_inc(taken, 1)
                    dve.wait_ge(taken, at(taken, r))
                    v.tensor_scalar(topi[:, ds(r * TOP, TOP)], at8[:, :], rowoff[:, 0:1], None, ALU.add).then_inc(kept, 1)

                root_of(0)
                for j in range(HALF):
                    centre(0, j)
                    low(0, j)
                centre(0, HALF)

                def body2(n):
                    m = n - LAG

                    dve.wait_ge(kv_turned, at(kv_turned, m))
                    v.tensor_copy(kvT[:, :, :].rearrange("p c t -> p (c t)"), pD[:, 0:DC * P]).then_inc(kvT_done, 1)
                    shift(m)
                    invert(m)
                    split_rest(m)
                    for r in range(RPL):
                        top_round((n - NB) * RPL + r)

                def body(n, s1, s2, nxt):
                    m = n - LAG
                    for j in range(NT):
                        if s1:
                            if nxt:
                                for i in ((0, 1, 2), (3, 4, 5), (6, 7))[j] if j < 3 else ():
                                    stats_of(n + 1, i)
                            if j == HALF:
                                gate_max(n, 0)
                            if j < HALF:
                                low(n, j + HALF)
                            elif nxt and j > HALF:
                                low(n + 1, j - HALF)
                        if s2 and j == 2:
                            shift(m)
                        if s1:
                            if j < HALF - 1:
                                centre(n, j + 1 + HALF)
                            elif nxt and j < NT - 1:
                                centre(n + 1, j + 1 - HALF)
                            elif nxt:
                                centre(n + 1, HALF)
                            if nxt and j == 2:
                                moments_of(n + 1)
                        if s2:
                            if j == 2:
                                invert(m)
                            if j >= 5:
                                add_x(m, j - 5)
                            if j in (3, 4, 5, 6):
                                divide(m, j - 3)
                        if s1:
                            if j in (5, 6):
                                q_negative(n, j - 5)
                            dve.wait_ge(kv_done, at(kv_done, n, j))
                            dve.wait_ge(kv_used, at(kv_used, n, j - 2))
                            dve.wait_ge(ek_done, at(ek_done, n, j))
                            v.scalar_tensor_tensor(
                                out=phik[:, j % 2, :].rearrange("p (c t) -> p c t", c=DC), in0=kv1[:, j % 2, 0:DC, 0:P], scalar=0.0,
                                in1=ek[:, j % 2, :].rearrange("p (c t) -> p c t", c=DC), op0=ALU.max, op1=ALU.add).then_inc(k_done, 1)
                        if s2:
                            if j == 1:
                                dve.wait_ge(kv_turned, at(kv_turned, m))
                                v.tensor_copy(kvT[:, :, :].rearrange("p c t -> p (c t)"), pD[:, 0:DC * P]).then_inc(kvT_done, 1)
                            if j == 2:
                                split_rest(m)
                        if nxt and j == HALF:
                            root_of(n + 1)
                            low(n + 1, 0)
                        if s1:
                            if j in (6, 7):
                                q_feature(n, j - 6)
                            if j == 6:
                                gate_probs(n, 0)
                            for q in range(PIECES):
                                if min(2 * q + 5, NT - 1) == j:
                                    piece(n, q)
                    if s1:
                        gate_max(n, 1)
                        q_negative(n, 2)
                    if s2:
                        add_x(m, 3)
                    if s1:
                        q_negative(n, 3)
                        gate_probs(n, 1)
                        q_feature(n, 2)
                        q_feature(n, 3)
                        dve.wait_ge(kv_used, at(kv_used, n, NT - 1))
                        v.tensor_copy(kvring[:, ds(n % QR, 1), :, :].rearrange("p o c t -> p (o c t)"),
                                                pKV[:, 0:DC * (P + 1)]).then_inc(kv_out, 1)

                for lo, hi, s1, s2, nxt in segments:
                    if not s1:
                        v.tensor_reduce(ewmax[:, :, :], piece_max[:, :, :].rearrange("p a (e h) -> p a e h", h=2),
                                                   AX.X, ALU.max).then_inc(sc_step, 1)
                        v.tensor_scalar(rowbase[:, :], rowno[:, :], ~(E - 1) & 0xFFFF, None, ALU.bitwise_and).then_inc(sc_step, 1)
                        dve.wait_ge(sc_step, at(sc_step, 0, 1))
                        v.tensor_scalar(rowoff[:, :], rowbase[:, :], float(S // E), None, ALU.mult).then_inc(sc_step, 1)
                        dve.wait_ge(sc_step, at(sc_step, 0, 2))
                        for i in range(2):
                            dve.wait_ge(piece_done[i], at(piece_done[i], NB - 1, PIECES // 2 - 1))
                        for half in range(2):
                            dve.wait_ge(p_turned, at(p_turned, 0, half))
                            last = v.tensor_copy(rows[:, half * 512:(half + 1) * 512], pP[half][0:NE, :])
                        last.then_inc(rows_done, 1)
                        dve.wait_ge(rows_done, at(rows_done, 0))
                    if not s1:
                        with dve.Fori(lo, hi) as n:
                            body2(n)
                    elif hi - lo == 1:
                        body(lo, s1, s2, nxt)
                    else:
                        with dve.Fori(lo, hi) as n:
                            body(n, s1, s2, nxt)
                for r in range(RPL * LAG, ROUNDS):
                    top_round(r)
                dve.wait_ge(sc_fold, at(sc_fold, 0))
                v.tensor_copy(ewpow[:, :, :], ewall[:, :, :]).then_inc(sc_step, 1)
                dve.wait_ge(sc_step, at(sc_step, 0, 3))
                v.tensor_scalar(ewpow[:, :, :], ewpow[:, :, :], 2.0 ** -60, None, ALU.max).then_inc(sc_step, 1)
                dve.wait_ge(sc_step, at(sc_step, 0, 4))
                bits = ewpow[:, :, :].bitcast(U32)
                v.tensor_scalar(bits, bits, EXP_MASK, None, ALU.bitwise_and).then_inc(sc_step, 1)
                dve.wait_ge(sc_step, at(sc_step, 0, 5))
                v.reciprocal(ewrec[:, :, :].rearrange("p a e -> p (a e)"), ewpow[:, :, :].rearrange("p a e -> p (a e)")).then_inc(sc_step, 1)
                dve.wait_ge(sc_step, at(sc_step, 0, 6))
                v.tensor_scalar(scales[:, :, 0], ewpow[:, 0, :], 2.0 ** -14 / XSCALE, None, ALU.mult)
                v.tensor_scalar(scales[:, :, 1], ewrec[:, 0, :], 2.0 ** 6, None, ALU.mult)
                v.tensor_scalar(scales[:, :, 2], ewrec[:, 0, :], 2.0 ** 14, None, ALU.mult)
                v.tensor_scalar(scales[:, :, 3], ewrec[:, 1, :], 2.0 ** 14, None, ALU.mult)
                v.scalar_tensor_tensor(out=scales[:, :, 4], in0=ewpow[:, 0, :], scalar=2.0 ** -20,
                                                  in1=ewpow[:, 1, :], op0=ALU.mult, op1=ALU.mult).then_inc(sc_step, 1)
                for i, dst in enumerate((gains, picks)):
                    for s in range(CAP // P):
                        dve.wait_ge(pick_turned, at(pick_turned, 0, 2 * i + s))
                        src = (pP[i] if s == 0 else (pQ, pD)[i])[:, 0:NE].rearrange("p (g b e) -> p g e b", g=NG, e=E)
                        v.tensor_copy(
                            dst[:, :].rearrange("p (g e b s) -> p g e b s", g=NG, e=E, s=2)[:, :, :, :, s], src).then_inc(picks_done, 1)

            @block.tensor
            def _(pe):
                t = nc.tensor
                pe.wait_ge(consts, at(consts, 0, 12))
                pe.wait_ge(w_in, at(w_in, 0, 11))
                for i, dst in enumerate((pP[0], pP[1], pQ, pD)):
                    for c in range(DC):
                        for r in range(DC):
                            last = t.transpose(dst[:, c * D + r * P:c * D + (r + 1) * P], wraw[:, i, r, c * P:(c + 1) * P], ident[:, :])
                    last.then_inc(wturn, 1)

                def turn(n, j):
                    h, jj = divmod(j, HALF)
                    pe.wait_ge(lo_done, at(lo_done, n, j))
                    pe.wait_ge(xT_done, at(xT_done, n, j - 1))
                    for a in range(2):
                        for c in range(DC):
                            last = t.transpose(pT[:, a, c, :], xhl[h][:, jj, a, c, :], ident16[:, :])
                    last.then_inc(turned, 1)

                def project(n, j):
                    h, jj = divmod(j, HALF)
                    pe.wait_ge(xT_done, at(xT_done, n, j))
                    pe.wait_ge(kv_done, at(kv_done, n, j - 2))
                    cols = slice(jj * P, (jj + 1) * P)
                    t.matmul(pP[j % 2][:, :], bias_lhs[:, :], bias_rows[:, :], start=True, stop=False)
                    terms = [(0, 0), (0, 1), (1, 0)]
                    for k, (a, b) in enumerate(terms):
                        for c in range(DC):
                            last = t.matmul(pP[j % 2][:, :], xT[h][:, a, c, cols], wkv[:, b, c, :], start=False,
                                            stop=k == 2 and c == DC - 1)
                    last.then_inc(proj, 1)
                    if jj == 0:
                        pe.wait_ge(gsub_done, at(gsub_done, n, h - 1))
                    for k, (a, b) in enumerate(terms):
                        for c in range(DC):
                            last = t.matmul(pG[:, h, jj, 0:E], xT[h][:, a, c, cols], wg[:, b, c, :],
                                            start=k == 0 and c == 0, stop=k == 2 and c == DC - 1)
                    if jj == HALF - 1:
                        last.then_inc(gated, 1)

                def sum_kv(n, j):
                    pe.wait_ge(k_done, at(k_done, n, j))
                    pe.wait_ge(kv_done, at(kv_done, n, j))
                    if j == 0:
                        pe.wait_ge(kv_out, at(kv_out, n, -1))
                    for c in range(DC):
                        last = t.matmul(pKV[:, c * (P + 1):(c + 1) * (P + 1)], phik[:, j % 2, c * P:(c + 1) * P],
                                        kv1[:, j % 2, DC + c, :], start=j == 0 and c == 0, stop=j == NT - 1,
                                        skip_group_check=True)
                    last.then_inc(kv_used, 1)

                def q_part(n, u, mixed=False):
                    h, c = divmod(u, DC)
                    bank = banks_q[mixed][u]
                    if not mixed:
                        pe.wait_ge(qraw_done, at(qraw_done, n, u - 2))
                    elif u < 3:
                        pe.wait_ge(qraw_done, at(qraw_done, n, u - 1))
                    if u == 0 and mixed:
                        pe.wait_ge(shifted, at(shifted, n - LAG))
                    if u == 3 and mixed:
                        pe.wait_ge(qraw_done, at(qraw_done, n, -1))
                        pe.wait_ge(qz_done, at(qz_done, n - LAG, 3))
                    terms = [(0, 0), (0, 1), (1, 0)]
                    for k, (a, b) in enumerate(terms):
                        for cc in range(DC):
                            last = t.matmul(bank[:, :], wq[:, b, cc, c * P:(c + 1) * P], xT[h][:, a, cc, :],
                                            start=k == 0 and cc == 0, stop=k == 2 and cc == DC - 1)
                    last.then_inc(q_proj, 1)

                def denominators(m, c):
                    if c == 0:
                        pe.wait_ge(kvm_done, at(kvm_done, m, 3))
                    for jj in range(NT):
                        window = slice(CENTRE - HEADS * jj, CENTRE - HEADS * jj + P)
                        last = t.matmul(pQ[:, 0:P], ksz[:, c, window],
                                        qring[:, ds(m % QR, 1), c, jj * P:(jj + 1) * P].rearrange("p o t -> p (o t)"),
                                        start=c == 0 and jj == 0, stop=c == DC - 1 and jj == NT - 1)
                    if c == DC - 1:
                        last.then_inc(den, 1)

                def reciprocals(m, u, w=None):
                    h, c = divmod(u, DC)
                    bank = banks_z[w is None][u % len(banks_z[w is None])]
                    if u == 0:
                        pe.wait_ge(mo_done, at(mo_done, m))
                        pe.wait_ge(zsplit, at(zsplit, m, 3))
                    if w is not None:
                        pe.wait_ge(z_out, at(z_out, w, u - 2))
                    elif u > 0:
                        pe.wait_ge(qz_done, at(qz_done, m, u - 1))
                    for i in range(HALF):
                        for part in range(3):
                            last = t.matmul(bank[:, i * P:(i + 1) * P], spread[:, h * HALF + i, c, :], zpart[:, part, :],
                                            start=part == 0, stop=part == 2)
                    last.then_inc(bcast, 1)

                def output(m, u, w=None):
                    h = u // 2
                    bank = pair(banks_o[w is None][u % len(banks_o[w is None])])
                    if u % 2 == 0:
                        pe.wait_ge(qz_done, at(qz_done, m, 2 * h + 1))
                    if w is not None:
                        pe.wait_ge(o_out, at(o_out, w, u - 2))
                    else:
                        pe.wait_ge(mix_done, at(mix_done, m, u - 1))
                    for i in range(2):
                        tokens = slice(((u % 2) * 2 + i) * P, ((u % 2) * 2 + i + 1) * P)
                        for c in range(DC):
                            last = t.matmul(bank[:, i, :], qz[h][:, c, tokens], mo[:, c, :], start=c == 0, stop=c == DC - 1)
                    last.then_inc(out_mm, 1)

                def body2(n):
                    m = n - LAG
                    denominators(m, 0)
                    denominators(m, 1)
                    pe.wait_ge(z_out, at(z_out, n - NB, -1))
                    for c in range(DC):
                        last = t.transpose(pD[:, c * P:(c + 1) * P], kvm[:, c, :], ident[:, :])
                    last.then_inc(kv_turned, 1)
                    pe.wait_ge(kvT_done, at(kvT_done, m))
                    for c in range(DC):
                        last = t.matmul(banks_mo[False][:, c * D:(c + 1) * D], kvT[:, c, :], woT[:, c, :], start=True, stop=True)
                    last.then_inc(mo_mm, 1)
                    for u in range(4):
                        reciprocals(m, u, n - NB)
                    for u in range(4):
                        output(m, u, n - NB)

                pe.wait_ge(wprep, at(wprep, 0, 18))
                pe.wait_ge(whi, at(whi, 0, 4))
                turn(0, 0)

                def body(n, s1, s2, nxt):
                    m = n - LAG
                    for j in range(NT):
                        if s1:
                            if j < NT - 1:
                                turn(n, j + 1)
                            elif nxt:
                                turn(n + 1, 0)
                        if s2 and j >= 5:
                            output(m, j - 5)
                        if s1:
                            project(n, j)
                        if s2:
                            if j == 0:
                                pe.wait_ge(qraw_done, at(qraw_done, n, -2))
                                denominators(m, 0)
                            if j == 1:
                                denominators(m, 1)
                                pe.wait_ge(qraw_done, at(qraw_done, n, -1))
                                for c in range(DC):
                                    last = t.transpose(pD[:, c * P:(c + 1) * P], kvm[:, c, :], ident[:, :])
                                last.then_inc(kv_turned, 1)
                            if j == 2:
                                pe.wait_ge(kvT_done, at(kvT_done, m))
                                for c in range(DC):
                                    last = t.matmul(pD[:, c * D:(c + 1) * D], kvT[:, c, :], woT[:, c, :], start=True, stop=True)
                                last.then_inc(mo_mm, 1)
                            if j == 3:
                                reciprocals(m, 0)
                            if j == 4:
                                reciprocals(m, 1)
                            if j == 5:
                                reciprocals(m, 2)
                            if j == 6:
                                reciprocals(m, 3)
                        if s1:
                            if j > 0:
                                sum_kv(n, j - 1)
                            if j in (4, 5):
                                q_part(n, j - 4, s2)
                            if j == 7:
                                q_part(n, 2)
                    if s2:
                        output(m, 3)
                    if s1:
                        q_part(n, 3, s2)
                        sum_kv(n, NT - 1)

                for lo, hi, s1, s2, nxt in segments:
                    if not s1:
                        pe.wait_ge(prob_done, at(prob_done, NB - 1, 1))
                        pe.wait_ge(kv_done, at(kv_done, NB - 1, NT - 1))
                        for half in range(2):
                            for jj in range(HALF):
                                last = t.transpose(pP[half][0:NE, jj * P:(jj + 1) * P], probs[:, half * HALF + jj, :], ident[:, :])
                            last.then_inc(p_turned, 1)
                        pe.wait_ge(kv_out, at(kv_out, NB - 1))
                        pe.wait_ge(gsub_done, at(gsub_done, NB - 1, 1))
                        pe.wait_ge(qraw_done, at(qraw_done, NB - 1, 3))
                        pe.wait_ge(rows_done, at(rows_done, 0))
                        pe.wait_ge(mix_done, at(mix_done, NB - LAG - 1, 3))
                        with pe.Fori(lo, hi) as n:
                            body2(n)
                        continue
                    if hi - lo == 1:
                        body(lo, s1, s2, nxt)
                    else:
                        with pe.Fori(lo, hi) as n:
                            body(n, s1, s2, nxt)
                pe.wait_ge(kept, at(kept, ROUNDS - 1))
                pe.wait_ge(mo_done, at(mo_done, NB - 1))
                pe.wait_ge(qz_done, at(qz_done, NB - 1, 3))
                for i, src in enumerate((topv, topi)):
                    for s in range(CAP // P):
                        dst = pP[i] if s == 0 else (pQ, pD)[i]
                        t.transpose(dst[:, 0:NE], src[:, s * P:(s + 1) * P], ident[0:NE, 0:NE]).then_inc(pick_turned, 1)

        with ExitStack() as ctx:
            sb, ps = sb_in(ctx), ps_in(ctx)
            w1s = [sb(f"w1s{i}", [P, 2, DC, HID], F16) for i in range(2)]
            w2s = [sb(f"w2s{i}", [P, 2, HC, D], F16) for i in range(2)]
            stage = sb("stage", [P, 4, 1024], F32)
            cur = [sb(f"cur{i}", [P, 5], F32) for i in range(2)]
            idx = [sb(f"idx{i}", [P, 4], U32) for i in range(4)]
            xg = [sb(f"xg{i}", [P, 4, 2, DC, P], F16) for i in range(2)]
            xgT = [sb(f"xgT{i}", [P, 2, DC, 512], F16) for i in range(2)]
            gel = sb("gel", [P, 2, 512], F32)
            hid = sb("hid", [P, 4, 2, 512], F16)
            yo = [sb(f"yo{i}", [P, 4, D], F32) for i in range(2)]
            fmix = sb("fmix", [P, 2, 2, D], F32)
            facc = sb("facc", [P, 2, 2, D], F32)
            fffn = sb("fffn", [P, 2, 2, D], BF16)
            lmix = sb("lmix", [P, GB * NT, D], F32)
            lacc = sb("lacc", [P, GB * NT, D], F32)
            lffn = sb("lffn", [P, 2, HALF, D], BF16)
            LP = 2 * GB

            pX = [ps(f"pX{i}", [P, 2, DC, P], F16) for i in range(2)]
            pH = [ps(f"pH{i}", [P, 512]) for i in range(4)]
            pY = [ps(f"pY{i}", [P, 2, D]) for i in range(2)]

            idx_done = event("idx_done", per=4)
            rows_in = [event(f"rows_in{i}", step=64) for i in range(2)]
            x_turned = event("x_turned", per=4)
            xgT_done = event("xgT_done", per=4, credit=2)
            h_mm = event("h_mm", per=HC)
            gel_done = event("gel_done", per=HC, credit=4)
            hhi_done = event("hhi_done", per=HC)
            hlo_done = event("hlo_done", per=HC, credit=2)
            y_mm = event("y_mm", per=HC, credit=4)
            y_half = event("y_half")
            y_done = event("y_done", per=2, credit=2)
            added = [event(f"added{i}", step=64) for i in range(2)]
            part_in = [event(f"part_in{r}", step=16) for r in range(4)]
            cur_done = event("cur_done")
            whi_done = event("whi_done", per=4)
            wlo_done = event("wlo_done", per=4, credit=4)
            fin_in = [event(f"fin_in{i}", step=32) for i in range(2)]
            fin_cast = event("fin_cast")
            fin_done = event("fin_done")
            fin_out = [event(f"fin_out{i}", step=16, credit=1) for i in range(2)]

            lmix_in = event("lmix_in", step=16)
            lacc_in = [event(f"lacc_in{i}", step=16) for i in range(LP)]
            lcast = event("lcast")
            ldone = event("ldone")
            lout = [event(f"lout{i}", step=16) for i in range(LP)]

            LAST = 4 * NBODY - 1
            FIN0 = 16
            bodies = [(0, 1, False, False), (1, 4 if NG > 1 else 3, False, False)]
            if NG > 1:
                bodies.append((4, NBODY - 1, True, False))
            bodies.append((NBODY - 1, NBODY, NG > 1, True))

            last_rows = [dram[(NG - 1) * GB * S:NG * GB * S, :].rearrange("(s p) d -> p s d", p=P)
                         for dram in (mix, acc, out.rearrange("n t d -> (n t) d"))]

            def piece_of(i):
                return slice(i * HALF, (i + 1) * HALF)

            def run_b(eng, body):
                for lo, hi, fin, last in bodies:
                    if hi - lo == 1:
                        body(lo, fin, last)
                    else:
                        with eng.Fori(lo, hi) as b:
                            body(b, fin, last)

            def fin_rows(dram, b, q):
                f = b * 4 + (q - FIN0)
                return dram[ds(f * (2 * P), 2 * P), :].rearrange("(s p) d -> p s d", p=P)

            out_rows = out.rearrange("n t d -> (n t) d")

            def part_src(e, r):
                if r < 2:
                    return w1_rows[ds(e * D + r * P, P), :]
                return w2_rows[ds(e * HID + (r - 2) * 4 * P, 4 * P), :].rearrange("(q p) d -> p q d", p=P)

            def part_dst(i, b, r):
                if r < 2:
                    return w1s[i][:, b, r, :]
                return w2s[i][:, b, (r - 2) * 4:(r - 1) * 4, :]

            def staged(r):
                return stage[:, r, :] if r < 2 else stage[:, r, :].rearrange("p (q d) -> p q d", q=4)

            def first(b, q):
                return isinstance(b, int) and b == 0 and q < 2

            def parts_of(q, last):
                if last and q >= 2:
                    return None, ()
                return 1 + q // 2, ((0, 1), (2, 3))[q % 2]

            block = ctx.enter_context(nc.Block())

            @block.sync
            def _(sp):
                def load_part(load, r):
                    value = held(sp, at(wlo_done, load, r - 4))
                    sp.wait_ge(consts, 1)
                    sp.wait_ge(wlo_done, value)
                    sp.dma_start(staged(r), part_src(load % E, r)).then_inc(part_in[r], 16)

                def load_sums(b, q):
                    i = q % 2
                    value = held(sp, at(added[1 - i], 2 * b, (q - 1) // 2))
                    sp.wait_ge(consts, 1)
                    sp.wait_ge(added[1 - i], value)
                    value = held(sp, at(added[i], 2 * b, q // 2 - 1))
                    sp.wait_ge(consts, 1)
                    sp.wait_ge(added[i], value)
                    value = held(sp, at(fin_out[i], 2 * b, q // 2 - FIN0 // 2 - 1))
                    sp.wait_ge(consts, 1)
                    sp.wait_ge(fin_out[i], value)
                    sp.dma_start(fmix[:, i, :, :], fin_rows(mix, b, q)).then_inc(fin_in[i], 16)
                    sp.dma_start(facc[:, i, :, :], fin_rows(acc, b, q)).then_inc(fin_in[i], 16)

                for r in range(4):
                    load_part(0, r)

                def body(b, fin, last):
                    for q in range(4):
                        ahead, parts = parts_of(q, last)
                        for r in parts:
                            load_part(2 * b + ahead, r)
                        if fin:
                            load_sums(b, q)
                        if last and q == 0:
                            sp.dma_start(lmix[:, :, :], last_rows[0]).then_inc(lmix_in, 16)

                run_b(sp, body)
                for i in range(LP):
                    if i % (LP // 2) == 0:
                        sp.wait_ge(added[2 * i // LP], at(added[2 * i // LP], LAST // 2))
                    sp.dma_start(lacc[:, piece_of(i), :], last_rows[1][:, piece_of(i), :]).then_inc(lacc_in[i], 16)
                for i in range(2):
                    if NG > 1:
                        sp.wait_ge(fin_out[i], at(fin_out[i], 8 * (NG - 1) - 1))
                for i in range(LP):
                    sp.wait_ge(lout[i], at(lout[i], 0))

            @block.gpsimd
            def _(pool):
                g = nc.gpsimd
                for ev in (xgT_done, gel_done, hlo_done, y_mm, y_done, wlo_done, *fin_out):
                    pool.sem_inc(ev, credit(ev))

                def gather(b, q):
                    i = q % 2
                    k = b * 4 + q
                    g.tensor_copy(idx[q % 4][:, :], picks[:, ds(k * 4, 4)]).then_inc(idx_done, 1)
                    value = held(pool, at(idx_done, b, q))
                    pool.wait_ge(consts, 1)
                    pool.wait_ge(idx_done, value)
                    for s in range(4):
                        g.indirect_dma_start(
                            xg[i][:, s, :, :, :].rearrange("p a c t -> p (a c t)"), None, table,
                            bass.IndirectOffsetOnAxis(ap=idx[q % 4][:, s:s + 1], axis=0)).then_inc(rows_in[i], 16)

                gather(0, 0)
                gather(0, 1)

                def body(b, fin, last):
                    for q in range(4):
                        i = q % 2
                        if not first(b, q):
                            pool.wait_ge(added[i], at(added[i], 2 * b, q // 2 - 1))
                        if not (last and q >= 2):
                            pool.wait_ge(x_turned, at(x_turned, 4 * b, 4 * q + 3))
                            gather(b, q + 2)
                        value = held(pool, at(y_done, 4 * b, 2 * q + 1))
                        pool.wait_ge(consts, 1)
                        pool.wait_ge(y_done, value)
                        for s in range(4):
                            g.indirect_dma_start(
                                acc, bass.IndirectOffsetOnAxis(ap=idx[q][:, s:s + 1], axis=0), yo[i][:, s, :], None,
                                compute_op=ALU.add).then_inc(added[i], 16)

                run_b(pool, body)
                for par in range(2):
                    pool.wait_ge(added[par], at(added[par], LAST // 2))

            @block.scalar
            def _(act):
                a = nc.scalar

                def weight_high(b, ahead, r, i):
                    load = 2 * b + ahead
                    act.wait_ge(part_in[r], at(part_in[r], load))
                    act.wait_ge(cur_done, at(cur_done, load))
                    a.activation(part_dst(i, 0, r), staged(r), ACT.Copy,
                                             scale=cur[i][:, 2 + r // 2:3 + r // 2]).then_inc(whi_done, 1)

                def rows_T(b, q, s):
                    act.wait_ge(x_turned, at(x_turned, 4 * b, 4 * q + s))
                    a.activation(xgT[q % 2][:, :, :, s * P:(s + 1) * P], pX[s % 2][:, :, :, :], ACT.Copy).then_inc(xgT_done, 1)

                def hidden(b, q, hc):
                    c = cur[(q // 2) % 2]
                    k = HC * q + hc
                    act.wait_ge(h_mm, at(h_mm, 4 * b, k))
                    act.wait_ge(hlo_done, at(hlo_done, 4 * b, k - 2))
                    a.activation(gel[:, hc % 2, :], pH[hc % 4][:, :], ACT.Gelu_apprx_tanh, scale=c[:, 0:1]).then_inc(gel_done, 1)
                    act.wait_ge(gel_done, at(gel_done, 4 * b, k))
                    act.wait_ge(y_mm, at(y_mm, 4 * b, k - 4))
                    a.activation(hid[:, hc % 4, 0, :], gel[:, hc % 2, :], ACT.Copy, scale=c[:, 1:2]).then_inc(hhi_done, 1)

                def store(b, q):
                    i = q % 2
                    act.wait_ge(fin_done, at(fin_done, 4 * b, q - FIN0))
                    act.dma_start(fin_rows(out_rows, b, q), fmix[:, i, :, :]).then_inc(fin_out[i], 16)

                def store_last(i):
                    act.wait_ge(ldone, at(ldone, i))
                    act.dma_start(last_rows[2][:, piece_of(i), :], lmix[:, piece_of(i), :]).then_inc(lout[i], 16)

                for r in range(4):
                    weight_high(0, 0, r, 0)
                for s in range(4):
                    rows_T(0, 0, s)
                hidden(0, 0, 0)
                hidden(0, 0, 1)

                def body(b, fin, last):
                    for q in range(4):
                        more = not (last and q == 3)
                        ahead, parts = parts_of(q, last)
                        for hc in range(2, HC):
                            hidden(b, q, hc)
                            if more and hc < 6:
                                rows_T(b, q + 1, hc - 2)
                            if parts and hc in (3, 6):
                                r = parts[hc // 6]
                                if hc == 3 and r == 0:
                                    act.wait_ge(y_mm, at(y_mm, 4 * b, HC * q - 1))
                                weight_high(b, ahead, r, ahead % 2)
                        if fin:
                            store(b, q)
                        if more:
                            hidden(b, q + 1, 0)
                            hidden(b, q + 1, 1)

                run_b(act, body)
                for i in range(LP):
                    store_last(i)

            @block.vector
            def _(dve):
                v = nc.vector

                def fetch_scales(b, ahead, i):
                    load = 2 * b + ahead
                    v.tensor_copy(cur[i][:, :], scales[:, ds(load % E, 1), :].rearrange("p o s -> p (o s)")).then_inc(cur_done, 1)

                def weight_low(b, ahead, r, i):
                    load = 2 * b + ahead
                    dve.wait_ge(whi_done, at(whi_done, load, r))
                    v.scalar_tensor_tensor(out=part_dst(i, 1, r), in0=staged(r), scalar=cur[i][:, 2 + r // 2:3 + r // 2],
                                                       in1=part_dst(i, 0, r), op0=ALU.mult, op1=ALU.subtract).then_inc(wlo_done, 1)

                def hidden_low(b, q, hc):
                    k = HC * q + hc
                    dve.wait_ge(hhi_done, at(hhi_done, 4 * b, k))
                    v.scalar_tensor_tensor(out=hid[:, hc % 4, 1, :], in0=gel[:, hc % 2, :],
                                                       scalar=cur[(q // 2) % 2][:, 1:2], in1=hid[:, hc % 4, 0, :],
                                                       op0=ALU.mult, op1=ALU.subtract).then_inc(hlo_done, 1)

                def weigh(b, q):
                    i = q % 2
                    if not first(b, q):
                        dve.wait_ge(added[i], at(added[i], 2 * b, q // 2 - 1))
                    for s in range(4):
                        if s == 0:
                            dve.wait_ge(y_half, at(y_half, 4 * b, q))
                        if s == 2:
                            dve.wait_ge(y_mm, at(y_mm, 4 * b, HC * q + HC - 1))
                        last = v.tensor_scalar(yo[i][:, s, :], pY[s // 2][:, s % 2, :], gains[:, ds((b * 4 + q) * 4 + s, 1)],
                                               cur[(q // 2) % 2][:, 4:5], ALU.mult, ALU.mult)
                        if s % 2 == 1:
                            last.then_inc(y_done, 1)

                def finish(b, q):
                    i = q % 2
                    dve.wait_ge(fin_in[i], at(fin_in[i], 2 * b, q // 2 - FIN0 // 2))
                    v.tensor_copy(fffn[:, i, :, :], facc[:, i, :, :]).then_inc(fin_cast, 1)
                    dve.wait_ge(fin_cast, at(fin_cast, 4 * b, q - FIN0))
                    v.tensor_tensor(fmix[:, i, :, :], fmix[:, i, :, :], fffn[:, i, :, :], ALU.add).then_inc(fin_done, 1)

                def finish_last(i):
                    if i == 0:
                        dve.wait_ge(lmix_in, at(lmix_in, 0))
                    dve.wait_ge(lacc_in[i], at(lacc_in[i], 0))
                    v.tensor_copy(lffn[:, i % 2, :, :], lacc[:, piece_of(i), :]).then_inc(lcast, 1)
                    dve.wait_ge(lcast, at(lcast, i))
                    v.tensor_tensor(lmix[:, piece_of(i), :], lmix[:, piece_of(i), :], lffn[:, i % 2, :, :], ALU.add).then_inc(ldone, 1)

                fetch_scales(0, 0, 0)
                for r in range(4):
                    weight_low(0, 0, r, 0)
                hidden_low(0, 0, 0)
                hidden_low(0, 0, 1)

                def body(b, fin, last):
                    for q in range(4):
                        ahead, parts = parts_of(q, last)
                        if parts and parts[0] == 0:
                            dve.wait_ge(y_done, at(y_done, 4 * b, 2 * q - 1))
                            fetch_scales(b, ahead, ahead % 2)
                        for hc in range(2, HC):
                            hidden_low(b, q, hc)
                            if parts and hc in (3, 6):
                                weight_low(b, ahead, parts[hc // 6], ahead % 2)
                            if fin and hc == 5:
                                finish(b, q)
                        if not (last and q == 3):
                            hidden_low(b, q + 1, 0)
                        else:
                            for i in range(LP // 2 - 1):
                                finish_last(i)
                        weigh(b, q)
                        if not (last and q == 3):
                            hidden_low(b, q + 1, 1)

                run_b(dve, body)
                for i in range(LP // 2 - 1, LP):
                    finish_last(i)

            @block.tensor
            def _(pe):
                t = nc.tensor
                terms = [(0, 0), (0, 1), (1, 0)]

                def turn_rows(b, q, s):
                    i = q % 2
                    if s == 0:
                        pe.wait_ge(rows_in[i], at(rows_in[i], 2 * b, q // 2))
                    pe.wait_ge(xgT_done, at(xgT_done, 4 * b, 4 * q + s - 2))
                    for a in range(2):
                        for c in range(DC):
                            last = t.transpose(pX[s % 2][:, a, c, :], xg[i][:, s, a, c, :], ident16[:, :])
                    last.then_inc(x_turned, 1)

                def product1(b, q, hc):
                    i, w = q % 2, w1s[(q // 2) % 2]
                    if hc == 0:
                        pe.wait_ge(xgT_done, at(xgT_done, 4 * b, 4 * q + 3))
                        if q % 2 == 0:
                            pe.wait_ge(wlo_done, at(wlo_done, 2 * b, 4 * (q // 2) + 3))
                    pe.wait_ge(gel_done, at(gel_done, 4 * b, HC * q + hc - 4))
                    for k, (ad, aw) in enumerate(terms):
                        for c in range(DC):
                            last = t.matmul(pH[hc % 4][:, :], w[:, aw, c, hc * P:(hc + 1) * P], xgT[i][:, ad, c, :],
                                            start=k == 0 and c == 0, stop=k == 2 and c == DC - 1)
                    last.then_inc(h_mm, 1)

                def product2(b, q, hc):
                    w = w2s[(q // 2) % 2]
                    pe.wait_ge(hlo_done, at(hlo_done, 4 * b, HC * q + hc))
                    for s in range(4):
                        if hc == 0 and s % 2 == 0:
                            pe.wait_ge(y_done, at(y_done, 4 * b, 2 * (q - 1) + s // 2))
                        for k, (ad, aw) in enumerate(terms):
                            last = t.matmul(pY[s // 2][:, s % 2, :], hid[:, hc % 4, ad, s * P:(s + 1) * P], w[:, aw, hc, :],
                                            start=hc == 0 and k == 0 and s % 2 == 0, stop=hc == HC - 1 and k == 2,
                                            skip_group_check=True)
                        if hc == HC - 1 and s == 1:
                            last.then_inc(y_half, 1)
                    last.then_inc(y_mm, 1)

                for s in range(4):
                    turn_rows(0, 0, s)
                product1(0, 0, 0)
                product1(0, 0, 1)

                def body(b, fin, last):
                    for q in range(4):
                        more = not (last and q == 3)
                        for hc in range(2, HC):
                            product1(b, q, hc)
                            product2(b, q, hc - 2)
                            if more and hc < 6:
                                turn_rows(b, q + 1, hc - 2)
                        if more:
                            product1(b, q + 1, 0)
                        product2(b, q, 6)
                        if more:
                            product1(b, q + 1, 1)
                        product2(b, q, 7)

                run_b(pe, body)


def kernel(L0_attn_x, L0_attn_Wq, L0_attn_bq, L0_attn_Wk, L0_attn_bk, L0_attn_Wv, L0_attn_bv, L0_attn_Wo, L0_attn_bo,
           L0_ffn_gate_w, L0_ffn_w1, L0_ffn_w2):
    import numpy as _np
    import concourse.bacc as _bacc
    from concourse.bass_utils import run_bass_kernel_spmd as _run

    nc = _bacc.Bacc("TRN2", target_bir_lowering=False, num_devices=1)
    arrays, args = {}, []
    for name, a in [("x", L0_attn_x), ("Wq", L0_attn_Wq), ("bq", L0_attn_bq), ("Wk", L0_attn_Wk), ("bk", L0_attn_bk),
                    ("Wv", L0_attn_Wv), ("bv", L0_attn_bv), ("Wo", L0_attn_Wo), ("bo", L0_attn_bo),
                    ("gate_w", L0_ffn_gate_w), ("w1", L0_ffn_w1), ("w2", L0_ffn_w2)]:
        a = _np.ascontiguousarray(a)
        arrays[f"in_{name}"] = a
        args.append(nc.dram_tensor(f"in_{name}", a.shape, F32, kind="ExternalInput").ap())
    shape = tuple(arrays["in_x"].shape)
    tokens = shape[0] * shape[1]
    out = nc.dram_tensor("out_0", shape, F32, kind="ExternalOutput").ap()
    table = nc.dram_tensor("table", (tokens, 2 * D), F16).ap()
    mix = nc.dram_tensor("mix", (tokens, D), F32).ap()
    acc = nc.dram_tensor("acc", (tokens, D), F32).ap()
    block_program(nc, *args, out, table, mix, acc)
    r = _run(nc, [arrays], core_ids=[0])
    return r.results[0]["out_0"]
```
